# Optimizing a Trainium2 kernel written in Bass

```python
import numpy as np
import jax
import jax.numpy as jnp

def _softmax(x, axis=-1):
    return jax.nn.softmax(x, axis=axis)

def _gelu(x):
    return jax.nn.gelu(x, approximate=True)

def _silu(x):
    return jax.nn.silu(x)

def _sigmoid(x):
    return jax.nn.sigmoid(x)

def _layernorm(x, axis=-1, eps=1e-05):
    m = jnp.mean(x, axis=axis, keepdims=True)
    v = jnp.var(x, axis=axis, keepdims=True)
    return (x - m) / jnp.sqrt(v + eps)

def _scatter_add(tgt, idx, src, axis=0):
    return tgt.at[idx].add(src)

def _segment_sum(src, seg, n):
    return jax.ops.segment_sum(src, seg, n)
kernel_name = 'mk_macaron_d2_jaxref_r8_332c07'

def setup_inputs(seed: int=0):
    np.random.seed(seed)
    _w = jnp.asarray

    def _L0_attn_setup():
        import jax, jax.numpy as jnp
        import numpy as np
        from math import log2, ceil
        HEADS, DIM_HEAD, BLOCK, EPS = (16, 64, 16, 1e-08)
        key = jax.random.key(seed)
        k1, k2, k3, k4 = jax.random.split(key, 4)
        b, n, dim = (4, 512, 128)
        inner = HEADS * DIM_HEAD
        return {'x': jax.random.normal(k1, (b, n, dim), jnp.float32), 'w_qkv': jax.random.normal(k2, (inner * 3, dim), jnp.float32) * 0.02, 'w_out': jax.random.normal(k3, (dim, inner), jnp.float32) * 0.02, 'b_out': jax.random.normal(k4, (dim,), jnp.float32) * 0.02}
    _L0_attn_in = _L0_attn_setup()

    def _L0_ffn_setup():
        import jax, jax.numpy as jnp
        import numpy as np
        EPS = 1e-05
        NUM_HEADS = 16
        NUM_KV_HEADS = 4
        NUM_EXPERTS = 8
        TOP_K = 2

        def _layernorm(x, w, b):
            mu = jnp.mean(x, axis=-1, keepdims=True)
            var = jnp.mean((x - mu) ** 2, axis=-1, keepdims=True)
            return (x - mu) * jax.lax.rsqrt(var + EPS) * w + b
        key = jax.random.key(seed)
        ks = jax.random.split(key, 8)
        S, B, H = (128, 4, 128)
        F = 256
        hd = H // NUM_HEADS
        qkv_out = (NUM_HEADS + 2 * NUM_KV_HEADS) * hd
        w_scale = 0.02
        return {'hidden_states': jax.random.normal(ks[0], (S, B, H), jnp.float32), 'ln1_weight': jnp.ones((H,), jnp.float32), 'ln1_bias': jnp.zeros((H,), jnp.float32), 'ln2_weight': jnp.ones((H,), jnp.float32), 'ln2_bias': jnp.zeros((H,), jnp.float32), 'qkv_weight': jax.random.normal(ks[1], (qkv_out, H), jnp.float32) * w_scale, 'proj_weight': jax.random.normal(ks[2], (H, H), jnp.float32) * w_scale, 'router_weight': jax.random.normal(ks[3], (NUM_EXPERTS, H), jnp.float32) * w_scale, 'moe_w1': jax.random.normal(ks[4], (NUM_EXPERTS, H, F), jnp.float32) * w_scale, 'moe_w2': jax.random.normal(ks[5], (NUM_EXPERTS, F, H), jnp.float32) * w_scale}
    _L0_ffn_in = _L0_ffn_setup()

    def _L1_attn_setup():
        import jax, jax.numpy as jnp
        import numpy as np
        HIDDEN = 128
        STATE = 32
        EXP = 4
        LN_EPS = 1e-05

        def _layernorm(y, w, b):
            mu = jnp.mean(y, axis=-1, keepdims=True)
            var = jnp.var(y, axis=-1, keepdims=True)
            return (y - mu) * jax.lax.rsqrt(var + LN_EPS) * w + b

        def _reference_tuple_inner(x, A, Bm, C, D, ln_w, ln_b, W1, b1, W2, b2):
            Bsz, T, H = x.shape
            S = A.shape[0]
            state0 = jnp.zeros((Bsz, S), dtype=x.dtype)
            xB = jnp.einsum('bth,sh->tbs', x, Bm)
            xD = jnp.einsum('bth,oh->tbo', x, D)

            def step(state, inp):
                xb_t, xd_t = inp
                state = jnp.tanh(state @ A.T + xb_t)
                out = state @ C.T + xd_t
                return (state, out)
            final_state, outs = jax.lax.scan(step, state0, (xB, xD))
            out_seq = jnp.transpose(outs, (1, 0, 2))
            y = _layernorm(out_seq + x, ln_w, ln_b)
            h = jax.nn.gelu(jnp.einsum('bth,fh->btf', y, W1) + b1, approximate=False)
            y = y + jnp.einsum('btf,hf->bth', h, W2) + b2
            return (y, final_state)
        key = jax.random.key(seed)
        ks = jax.random.split(key, 10)
        B, T, H, S = (8, 256, HIDDEN, STATE)
        x = jax.random.normal(ks[0], (B, T, H), dtype=jnp.float32)
        A = jax.random.normal(ks[1], (S, S), dtype=jnp.float32) * 0.1
        Bm = jax.random.normal(ks[2], (S, H), dtype=jnp.float32) * 0.1
        C = jax.random.normal(ks[3], (H, S), dtype=jnp.float32) * 0.1
        D = jax.random.normal(ks[4], (H, H), dtype=jnp.float32) * 0.1
        ln_w = jnp.ones((H,), dtype=jnp.float32)
        ln_b = jnp.zeros((H,), dtype=jnp.float32)
        lim1 = 1.0 / np.sqrt(H)
        lim2 = 1.0 / np.sqrt(H * EXP)
        W1 = jax.random.uniform(ks[5], (H * EXP, H), minval=-lim1, maxval=lim1, dtype=jnp.float32)
        b1 = jax.random.uniform(ks[6], (H * EXP,), minval=-lim1, maxval=lim1, dtype=jnp.float32)
        W2 = jax.random.uniform(ks[7], (H, H * EXP), minval=-lim2, maxval=lim2, dtype=jnp.float32)
        b2 = jax.random.uniform(ks[8], (H,), minval=-lim2, maxval=lim2, dtype=jnp.float32)
        return {'x': x, 'A': A, 'Bm': Bm, 'C': C, 'D': D, 'ln_w': ln_w, 'ln_b': ln_b, 'W1': W1, 'b1': b1, 'W2': W2, 'b2': b2}
    _L1_attn_in = _L1_attn_setup()

    def _L1_ffn_setup():
        import jax, jax.numpy as jnp
        import numpy as np

        def _binarize(w):
            alpha = jax.lax.stop_gradient(jnp.mean(jnp.abs(w), axis=1, keepdims=True))
            bw = alpha * jnp.sign(w)
            return w + jax.lax.stop_gradient(bw - w)
        key = jax.random.key(seed)
        k1, k2, k3, k4, k5 = jax.random.split(key, 5)
        D, H = (128, 512)
        x = jax.random.normal(k1, (64, 196, D), dtype=jnp.float32)
        w1 = jax.random.normal(k2, (H, D), dtype=jnp.float32) * 0.02
        b1 = jax.random.normal(k3, (H,), dtype=jnp.float32) * 0.02
        w2 = jax.random.normal(k4, (D, H), dtype=jnp.float32) * 0.02
        b2 = jax.random.normal(k5, (D,), dtype=jnp.float32) * 0.02
        return {'x': x, 'w1': w1, 'b1': b1, 'w2': w2, 'b2': b2}
    _L1_ffn_in = _L1_ffn_setup()
    _d = {'L0_attn_x': _L0_attn_in['x'], 'L0_attn_w_qkv': _L0_attn_in['w_qkv'], 'L0_attn_w_out': _L0_attn_in['w_out'], 'L0_attn_b_out': _L0_attn_in['b_out'], 'L0_ffn_ln1_weight': _L0_ffn_in['ln1_weight'], 'L0_ffn_ln1_bias': _L0_ffn_in['ln1_bias'], 'L0_ffn_ln2_weight': _L0_ffn_in['ln2_weight'], 'L0_ffn_ln2_bias': _L0_ffn_in['ln2_bias'], 'L0_ffn_qkv_weight': _L0_ffn_in['qkv_weight'], 'L0_ffn_proj_weight': _L0_ffn_in['proj_weight'], 'L0_ffn_router_weight': _L0_ffn_in['router_weight'], 'L0_ffn_moe_w1': _L0_ffn_in['moe_w1'], 'L0_ffn_moe_w2': _L0_ffn_in['moe_w2'], 'L1_attn_A': _L1_attn_in['A'], 'L1_attn_Bm': _L1_attn_in['Bm'], 'L1_attn_C': _L1_attn_in['C'], 'L1_attn_D': _L1_attn_in['D'], 'L1_attn_ln_w': _L1_attn_in['ln_w'], 'L1_attn_ln_b': _L1_attn_in['ln_b'], 'L1_attn_W1': _L1_attn_in['W1'], 'L1_attn_b1': _L1_attn_in['b1'], 'L1_attn_W2': _L1_attn_in['W2'], 'L1_attn_b2': _L1_attn_in['b2'], 'L1_ffn_w1': _L1_ffn_in['w1'], 'L1_ffn_b1': _L1_ffn_in['b1'], 'L1_ffn_w2': _L1_ffn_in['w2'], 'L1_ffn_b2': _L1_ffn_in['b2']}
    _x0 = _d['L0_attn_x']
    _d['L0_attn_x'] = jax.random.normal(jax.random.fold_in(jax.random.key(seed), 1), (4, 1024, 128), dtype=_x0.dtype)
    del _x0
    return _d

def reference(L0_attn_x, L0_attn_w_qkv, L0_attn_w_out, L0_attn_b_out, L0_ffn_ln1_weight, L0_ffn_ln1_bias, L0_ffn_ln2_weight, L0_ffn_ln2_bias, L0_ffn_qkv_weight, L0_ffn_proj_weight, L0_ffn_router_weight, L0_ffn_moe_w1, L0_ffn_moe_w2, L1_attn_A, L1_attn_Bm, L1_attn_C, L1_attn_D, L1_attn_ln_w, L1_attn_ln_b, L1_attn_W1, L1_attn_b1, L1_attn_W2, L1_attn_b2, L1_ffn_w1, L1_ffn_b1, L1_ffn_w2, L1_ffn_b2):

    def _L0_attn_ref(x, w_qkv, w_out, b_out):
        import jax, jax.numpy as jnp
        import numpy as np
        from math import log2, ceil
        HEADS, DIM_HEAD, BLOCK, EPS = (16, 64, 16, 1e-08)
        b, n, dim = x.shape
        pad_to_len = 2 ** ceil(log2(n))
        if pad_to_len != n:
            x = jnp.pad(x, ((0, 0), (0, pad_to_len - n), (0, 0)))
        qkv = x @ w_qkv.T
        q, k, v = jnp.split(qkv, 3, axis=-1)

        def split_heads(t):
            return t.reshape(b, pad_to_len, HEADS, DIM_HEAD).transpose(0, 2, 1, 3).reshape(b * HEADS, pad_to_len, DIM_HEAD)
        q = split_heads(q) * DIM_HEAD ** (-0.5)
        k = split_heads(k)
        v = split_heads(v)
        num_levels = int(log2(pad_to_len // BLOCK)) - 1
        qkvs = [(q, k, v)]
        for _ in range(num_levels):
            q = q.reshape(q.shape[0], -1, 2, DIM_HEAD).mean(2)
            k = k.reshape(k.shape[0], -1, 2, DIM_HEAD).mean(2)
            v = v.reshape(v.shape[0], -1, 2, DIM_HEAD).sum(2)
            qkvs.append((q, k, v))
        neg_max = -jnp.finfo(x.dtype).max
        idx = jnp.arange(pad_to_len)
        Ysum = jnp.zeros((b * HEADS, pad_to_len, DIM_HEAD), x.dtype)
        Asum = jnp.zeros((b * HEADS, pad_to_len), x.dtype)
        for lvl, (ql, kl, vl) in enumerate(qkvs):
            B = ql.shape[0]
            nb = ql.shape[1] // BLOCK
            ql = ql.reshape(B, nb, BLOCK, DIM_HEAD)
            kl = kl.reshape(B, nb, BLOCK, DIM_HEAD)
            vl = vl.reshape(B, nb, BLOCK, DIM_HEAD)
            if lvl == 0:
                S = jnp.einsum('bnid,bnjd->bnij', ql, kl)
                S = jnp.where(jnp.triu(jnp.ones((BLOCK, BLOCK), bool), 1), neg_max, S)
                S = S - S.max(-1, keepdims=True)
                A = jnp.exp(S)
                y = jnp.einsum('bnij,bnjd->bnid', A, vl).reshape(B, pad_to_len, DIM_HEAD)
                Av = A.sum(-1).reshape(B, pad_to_len)
            else:
                q2 = ql.reshape(B, nb // 2, 2, BLOCK, DIM_HEAD)[:, :, 1]
                k1b = kl.reshape(B, nb // 2, 2, BLOCK, DIM_HEAD)[:, :, 0]
                v1b = vl.reshape(B, nb // 2, 2, BLOCK, DIM_HEAD)[:, :, 0]
                S = jnp.einsum('bnid,bnjd->bnij', q2, k1b)
                S = S - S.max(-1, keepdims=True)
                A = jnp.exp(S)
                y = jnp.einsum('bnij,bnjd->bnid', A, v1b)
                Av = A.sum(-1)
                y = jnp.pad(y[:, :, None], ((0, 0), (0, 0), (1, 0), (0, 0), (0, 0))).reshape(B, -1, DIM_HEAD)
                Av = jnp.pad(Av[:, :, None], ((0, 0), (0, 0), (1, 0), (0, 0))).reshape(B, -1)
                y = jnp.repeat(y, 2 ** lvl, axis=1)
                Av = jnp.repeat(Av, 2 ** lvl, axis=1)
            seq_key = (idx >> lvl << lvl) + (2 ** lvl - 1)
            keep = seq_key <= idx
            Ysum = Ysum + jnp.where(keep[None, :, None], y, 0.0)
            Asum = Asum + jnp.where(keep[None, :], Av, 0.0)
        out = Ysum / (Asum + EPS)[..., None]
        out = out.reshape(b, HEADS, pad_to_len, DIM_HEAD).transpose(0, 2, 1, 3).reshape(b, pad_to_len, HEADS * DIM_HEAD)
        out = out @ w_out.T + b_out
        return out[:, :n]

    def _L0_ffn_ref(hidden_states, ln1_weight, ln1_bias, ln2_weight, ln2_bias, qkv_weight, proj_weight, router_weight, moe_w1, moe_w2):
        import jax, jax.numpy as jnp
        import numpy as np
        EPS = 1e-05
        NUM_HEADS = 16
        NUM_KV_HEADS = 4
        NUM_EXPERTS = 8
        TOP_K = 2

        def _layernorm(x, w, b):
            mu = jnp.mean(x, axis=-1, keepdims=True)
            var = jnp.mean((x - mu) ** 2, axis=-1, keepdims=True)
            return (x - mu) * jax.lax.rsqrt(var + EPS) * w + b
        S, B, H = hidden_states.shape
        hd = H // NUM_HEADS
        rep = NUM_HEADS // NUM_KV_HEADS
        scale = 1.0 / hd ** 0.5
        ln1_out = _layernorm(hidden_states, ln1_weight, ln1_bias)
        qkv = jnp.einsum('sbh,oh->sbo', ln1_out, qkv_weight)
        q = qkv[..., :NUM_HEADS * hd].reshape(S, B, NUM_HEADS, hd)
        k = qkv[..., NUM_HEADS * hd:(NUM_HEADS + NUM_KV_HEADS) * hd].reshape(S, B, NUM_KV_HEADS, hd)
        v = qkv[..., (NUM_HEADS + NUM_KV_HEADS) * hd:].reshape(S, B, NUM_KV_HEADS, hd)
        k = jnp.repeat(k, rep, axis=2)
        v = jnp.repeat(v, rep, axis=2)
        scores = jnp.einsum('sbhd,tbhd->bhst', q, k) * scale
        causal = jnp.tril(jnp.ones((S, S), bool))
        scores = jnp.where(causal, scores, jnp.finfo(scores.dtype).min)
        probs = jax.nn.softmax(scores, axis=-1)
        attn = jnp.einsum('bhst,tbhd->sbhd', probs, v).reshape(S, B, H)
        proj_out = jnp.einsum('sbh,oh->sbo', attn, proj_weight)
        hidden_after_attn = hidden_states + proj_out
        ln2_out = _layernorm(hidden_after_attn, ln2_weight, ln2_bias)
        x = ln2_out.reshape(-1, H)
        logits = jnp.einsum('th,eh->te', x, router_weight)
        gate = jax.nn.softmax(logits, axis=-1)
        top_probs, top_idx = jax.lax.top_k(gate, TOP_K)
        h_mid = jax.nn.gelu(jnp.einsum('th,ehf->etf', x, moe_w1))
        expert_out = jnp.einsum('etf,efh->eth', h_mid, moe_w2)
        e_ids = jnp.arange(NUM_EXPERTS)[:, None, None]
        weights = jnp.sum(jnp.where(top_idx[None] == e_ids, top_probs[None], 0.0), axis=-1)
        moe_out = jnp.einsum('eth,et->th', expert_out, weights).reshape(S, B, H)
        return hidden_after_attn + moe_out

    def _L1_attn_ref(x, A, Bm, C, D, ln_w, ln_b, W1, b1, W2, b2):
        import jax, jax.numpy as jnp
        import numpy as np
        HIDDEN = 128
        STATE = 32
        EXP = 4
        LN_EPS = 1e-05

        def _layernorm(y, w, b):
            mu = jnp.mean(y, axis=-1, keepdims=True)
            var = jnp.var(y, axis=-1, keepdims=True)
            return (y - mu) * jax.lax.rsqrt(var + LN_EPS) * w + b

        def _reference_tuple_inner(x, A, Bm, C, D, ln_w, ln_b, W1, b1, W2, b2):
            Bsz, T, H = x.shape
            S = A.shape[0]
            state0 = jnp.zeros((Bsz, S), dtype=x.dtype)
            xB = jnp.einsum('bth,sh->tbs', x, Bm)
            xD = jnp.einsum('bth,oh->tbo', x, D)

            def step(state, inp):
                xb_t, xd_t = inp
                state = jnp.tanh(state @ A.T + xb_t)
                out = state @ C.T + xd_t
                return (state, out)
            final_state, outs = jax.lax.scan(step, state0, (xB, xD))
            out_seq = jnp.transpose(outs, (1, 0, 2))
            y = _layernorm(out_seq + x, ln_w, ln_b)
            h = jax.nn.gelu(jnp.einsum('bth,fh->btf', y, W1) + b1, approximate=False)
            y = y + jnp.einsum('btf,hf->bth', h, W2) + b2
            return (y, final_state)
        return _reference_tuple_inner(x, A, Bm, C, D, ln_w, ln_b, W1, b1, W2, b2)[0]

    def _L1_ffn_ref(x, w1, b1, w2, b2):
        import jax, jax.numpy as jnp
        import numpy as np

        def _binarize(w):
            alpha = jax.lax.stop_gradient(jnp.mean(jnp.abs(w), axis=1, keepdims=True))
            bw = alpha * jnp.sign(w)
            return w + jax.lax.stop_gradient(bw - w)
        bw1 = _binarize(w1)
        h = jnp.einsum('bsd,hd->bsh', x, bw1) + b1
        h = jax.nn.gelu(h, approximate=False)
        bw2 = _binarize(w2)
        out = jnp.einsum('bsh,dh->bsd', h, bw2) + b2
        return out
    x = L0_attn_x
    x = x + 0.5 * _L0_ffn_ref(_layernorm(x, axis=-1), L0_ffn_ln1_weight, L0_ffn_ln1_bias, L0_ffn_ln2_weight, L0_ffn_ln2_bias, L0_ffn_qkv_weight, L0_ffn_proj_weight, L0_ffn_router_weight, L0_ffn_moe_w1, L0_ffn_moe_w2)
    x = x + _L0_attn_ref(_layernorm(x, axis=-1), L0_attn_w_qkv, L0_attn_w_out, L0_attn_b_out)
    x = x + 0.5 * _L0_ffn_ref(_layernorm(x, axis=-1), L0_ffn_ln1_weight, L0_ffn_ln1_bias, L0_ffn_ln2_weight, L0_ffn_ln2_bias, L0_ffn_qkv_weight, L0_ffn_proj_weight, L0_ffn_router_weight, L0_ffn_moe_w1, L0_ffn_moe_w2)
    x = x + 0.5 * _L1_ffn_ref(_layernorm(x, axis=-1), L1_ffn_w1, L1_ffn_b1, L1_ffn_w2, L1_ffn_b2)
    x = x + _L1_attn_ref(_layernorm(x, axis=-1), L1_attn_A, L1_attn_Bm, L1_attn_C, L1_attn_D, L1_attn_ln_w, L1_attn_ln_b, L1_attn_W1, L1_attn_b1, L1_attn_W2, L1_attn_b2)
    x = x + 0.5 * _L1_ffn_ref(_layernorm(x, axis=-1), L1_ffn_w1, L1_ffn_b1, L1_ffn_w2, L1_ffn_b2)
    return x

_drawn_inputs = setup_inputs


def setup_inputs(seed=0):
    import zlib

    import numpy as np

    out = dict(_drawn_inputs(seed))
    spreads = {'L0_ffn_ln1_weight': (1.0, 0.6),
     'L0_ffn_ln1_bias': (0.0, 0.8),
     'L0_ffn_ln2_weight': (1.0, 0.6),
     'L0_ffn_ln2_bias': (0.0, 0.8),
     'L1_attn_ln_w': (1.0, 0.2),
     'L1_attn_ln_b': (0.0, 0.364)}
    factors = {'L0_attn_b_out': 4.273,
     'L0_ffn_router_weight': 8.0,
     'L0_ffn_moe_w1': 8.0,
     'L0_ffn_moe_w2': 8.0,
     'L1_attn_b1': 8.0,
     'L1_attn_b2': 5.869,
     'L1_ffn_w1': 3.981,
     'L1_ffn_b1': 8.0,
     'L1_ffn_w2': 3.873,
     'L1_ffn_b2': 6.535,
     'L1_attn_A': 2.686}
    for name, (base, spread) in spreads.items():
        noise = np.random.default_rng([zlib.crc32(name.encode()), seed]).standard_normal(out[name].shape)
        drawn = base * np.exp(spread * noise) if base else spread * noise
        out[name] = jnp.asarray(drawn.astype(out[name].dtype))
    for name, factor in factors.items():
        out[name] = (out[name] * factor).astype(out[name].dtype)
    return out
```

```python
import concourse.bass as bass
from concourse import mybir
from contextlib import ExitStack

F32 = mybir.dt.float32
F16 = mybir.dt.float16
U32 = mybir.dt.uint32
ALU = mybir.AluOpType
ACT = mybir.ActivationFunctionType
AX = mybir.AxisListType

NB, SEQ, D = 4, 1024, 128
GROUPS = SEQ // 128
EPS = 1e-5
MASKED = -1e30
ONE = 1
HEADS0, KV_HEADS0 = 16, 4
HD0 = D // HEADS0
QKV = 3 * D
PAIRS = NB * (NB + 1) // 2
EXPERTS, EXP_F, TOP_K = 8, 256, 2
CHUNKS = EXPERTS * EXP_F // 128
H_RING, UP_RING = 8, 3
FC = 4
STATE = 32




def causal_moe_ffn(nc, S, tag):
    x = S["x"]
    ident, lnw1, lnb1, lnw2, lnb2 = S["ident"], S["lnw1"], S["lnb1"], S["lnw2"], S["lnb2"]
    wqkv, wproj, wrouter, w1, w2 = S["wqkv"], S["wproj"], S["wrouter"], S["moe1"], S["moe2"]
    minus_half, epsilon, expert_ids = S["minus_half"], S["epsilon"], S["expert_ids"]
    with ExitStack() as ctx:
        def sb(name, shape, dt=F32):
            return ctx.enter_context(nc.sbuf_tensor(f"{tag}_{name}", shape, dt))

        def bank(name):
            return ctx.enter_context(nc.psum_tensor(f"{tag}_{name}", [128, 512], F32))

        sems = []

        def sem(name):
            sems.append(ctx.enter_context(nc.semaphore(f"{tag}_{name}")))
            return sems[-1]

        stats, mv = sb("stats", [128, NB, 6]), sb("mv", [128, NB, 2])
        stats2, mv2 = sb("stats2", [128, NB, 6]), sb("mv2", [128, NB, 2])
        roots, roots2 = sb("roots", [128, 5, NB]), sb("roots2", [128, 2, NB])
        hs, xn1, xn2 = sb("hs", [128, NB, D]), sb("xn1", [128, NB, D]), sb("xn2", [128, NB, D])
        ln1T, headsT = sb("ln1T", [128, NB * 128]), sb("headsT", [128, NB * 128])
        qkv = sb("qkv", [128, NB, QKV])
        pairs = sb("pairs", [128, PAIRS, D])
        pvs = sb("pvs", [128, PAIRS, D])
        scores = sb("scores", [128, NB, HEADS0, NB])
        shifted = sb("shifted", [128, NB, HEADS0, NB])
        probs = sb("probs", [128, NB, HEADS0, NB])
        small = sb("small", [128, 3, NB, HEADS0])
        after = [sb(f"after{i}", [128, NB, D]) for i in range(2)]
        x2T = [sb(f"x2T{i}", [128, NB * 128]) for i in range(2)]
        shifted_g, gate = sb("shifted_g", [128, NB, EXPERTS]), sb("gate", [128, NB, EXPERTS])
        gsmall = sb("gsmall", [128, 3, NB])
        top, topf = sb("top", [128, NB, 8]), sb("topf", [128, NB, 8])
        topi = sb("topi", [128, NB, 8], U32)
        pick = sb("pick", [128, 2, NB, EXPERTS])
        weight = [sb(f"weight{i}", [128, NB, EXPERTS]) for i in range(2)]
        hT = [sb(f"hT{i}", [128, NB * 128]) for i in range(H_RING)]

        up = [bank(f"up{i}") for i in range(UP_RING)]
        down = [bank(f"down{i}") for i in range(2)]
        qb = [bank(f"qkvb{i}") for i in range(2)]
        turn = bank("turn")

        s_stats, s_root = sem("stats_done"), sem("root_done")
        s_stats2, s_root2 = sem("stats2_done"), sem("root2_done")
        s_xn1, s_turn1, s_ln1T = sem("xn1_done"), sem("turned1"), sem("ln1T_done")
        s_q, s_qkv = sem("qkv_product"), sem("qkv_in_sbuf")
        s_shift, s_exp, s_heads = sem("scores_shifted"), sem("scores_exp"), sem("heads_done")
        s_turn2, s_headsT, s_proj = sem("turned2"), sem("headsT_done"), sem("proj_done")
        s_xn2, s_turn3, s_x2T = sem("xn2_done"), sem("turned3"), sem("x2T_done")
        s_logit, s_gshift, s_gexp = sem("logits_done"), sem("logits_shifted"), sem("logits_exp")
        s_up, s_h, s_down, s_add = sem("up_done"), sem("h_done"), sem("down_done"), sem("add_done")

        first = [sum(NB - u for u in range(t)) for t in range(NB)]

        def grp(t, g):
            return t[:, bass.ds(g, 1), :, :].rearrange("p a s d -> p (a s) d")

        with nc.Block() as block:
            @block.sync
            def _(sp):
                for s in sems:
                    sp.sem_inc(s, ONE)

            @block.gpsimd
            def _(pool):
                def power(out, in_):
                    pool.tensor_tensor(out, in_, minus_half[:, 0:NB], ALU.pow)
                    pool.drain()

                def a1(g):
                    pool.wait_ge(s_stats, ONE + g + 1)
                    pool.wait_ge(s_xn1, ONE + g)
                    var = mv[:, :, 1]
                    pool.tensor_tensor(roots[:, 0, :], var, epsilon[:, 0:NB], ALU.add)
                    pool.drain()
                    power(roots[:, 1, :], roots[:, 0, :])
                    pool.tensor_tensor(roots[:, 2, :], roots[:, 1, :], roots[:, 1, :], ALU.mult)
                    pool.drain()
                    pool.tensor_tensor(roots[:, 0, :], roots[:, 2, :], var, ALU.mult)
                    pool.drain()
                    pool.tensor_scalar(roots[:, 2, :], roots[:, 0, :], EPS, None, ALU.add)
                    pool.drain()
                    power(roots[:, 3, :], roots[:, 2, :])
                    pool.tensor_tensor(roots[:, 4, :], roots[:, 3, :], roots[:, 1, :], ALU.mult).then_inc(s_root, 1)

                def a2(g):
                    pool.wait_ge(s_stats2, ONE + g + 1)
                    pool.wait_ge(s_xn2, ONE + g)
                    pool.tensor_tensor(roots2[:, 0, :], mv2[:, :, 1], epsilon[:, 0:NB], ALU.add)
                    pool.drain()
                    pool.tensor_tensor(roots2[:, 1, :], roots2[:, 0, :], minus_half[:, 0:NB],
                                       ALU.pow).then_inc(s_root2, 1)

                with pool.Fori(0, GROUPS) as g:
                    a1(g)
                    pool.drain()
                    a2(g)
                    pool.drain()

            @block.scalar
            def _(act):
                def a_ln1T(g):
                    act.wait_ge(s_turn1, ONE + g + 1)
                    act.wait_ge(s_q, ONE + NB * g)
                    nc.scalar.activation(ln1T[:, :], turn[:, :], ACT.Identity, bias=lnb1[:, :],
                                         scale=lnw1[:, :]).then_inc(s_ln1T, 1)

                def a_qkv(g):
                    act.wait_ge(s_heads, ONE + g)
                    for s in range(NB):
                        act.wait_ge(s_q, ONE + NB * g + s + 1)
                        nc.scalar.activation(qkv[:, s, :], qb[s % 2][:, 0:QKV], ACT.Copy).then_inc(s_qkv, 1)

                def a_exp(g):
                    act.wait_ge(s_shift, ONE + g + 1)
                    nc.scalar.activation(probs[:, :, :, :], shifted[:, :, :, :], ACT.Exp,
                                         scale=HD0 ** -0.5).then_inc(s_exp, 1)

                def a_headsT(g):
                    act.wait_ge(s_turn2, ONE + g + 1)
                    act.wait_ge(s_proj, ONE + g)
                    nc.scalar.activation(headsT[:, :], turn[:, :], ACT.Copy).then_inc(s_headsT, 1)

                def a_x2T(g, b):
                    act.wait_ge(s_turn3, ONE + g + 1)
                    nc.scalar.activation(x2T[b][:, :], turn[:, :], ACT.Identity, bias=lnb2[:, :],
                                         scale=lnw2[:, :]).then_inc(s_x2T, 1)

                def a_gexp(g):
                    act.wait_ge(s_gshift, ONE + g + 1)
                    nc.scalar.activation(gate[:, :, :], shifted_g[:, :, :], ACT.Exp).then_inc(s_gexp, 1)

                def gelu(g, c):
                    act.wait_ge(s_up, ONE + CHUNKS * g + c + 1)
                    act.wait_ge(s_down, ONE + EXPERTS * g + (max(c - H_RING, -2)) // 2 + 1)
                    nc.scalar.activation(hT[c % H_RING][:, :], up[c % UP_RING][:, :],
                                         ACT.Gelu_apprx_tanh).then_inc(s_h, 1)

                def group(g, b, ahead):
                    for c in range(CHUNKS):
                        gelu(g, c)
                        if ahead:
                            if c == 3:
                                a_ln1T(g + 1)
                            if c == 5:
                                a_qkv(g + 1)
                            if c == 7:
                                a_exp(g + 1)
                            if c == 11:
                                a_headsT(g + 1)
                    if ahead:
                        a_x2T(g + 1, 1 - b)
                        a_gexp(g + 1)

                a_ln1T(0)
                a_qkv(0)
                a_exp(0)
                a_headsT(0)
                a_x2T(0, 0)
                a_gexp(0)
                with act.Fori(0, GROUPS - 2, 2) as g:
                    group(g, 0, True)
                    group(g + 1, 1, True)
                group(GROUPS - 2, 0, True)
                group(GROUPS - 1, 1, False)

            @block.tensor
            def _(pe):
                def turn_tiles(src, signal):
                    for s in range(NB):
                        last = nc.tensor.transpose(turn[:, s * 128:(s + 1) * 128], src[:, s, :], ident[:, :])
                    last.then_inc(signal, 1)

                def p_turn1(g):
                    pe.wait_ge(s_xn1, ONE + g + 1)
                    pe.wait_ge(s_gshift, ONE + g)
                    turn_tiles(xn1, s_turn1)

                def p_qkv(g):
                    pe.wait_ge(s_ln1T, ONE + g + 1)
                    for s in range(NB):
                        pe.wait_ge(s_qkv, ONE + NB * g + max(s - 1, 0))
                        nc.tensor.matmul(qb[s % 2][:, 0:QKV], ln1T[:, s * 128:(s + 1) * 128], wqkv[:, :],
                                         start=True, stop=True).then_inc(s_q, 1)

                def p_turn2(g):
                    pe.wait_ge(s_heads, ONE + g + 1)
                    turn_tiles(pvs[:, 0:NB, :], s_turn2)

                def p_proj(g):
                    pe.wait_ge(s_headsT, ONE + g + 1)
                    for s in range(NB):
                        last = nc.tensor.matmul(turn[:, s * 128:(s + 1) * 128], headsT[:, s * 128:(s + 1) * 128],
                                                wproj[:, :], start=True, stop=True)
                    last.then_inc(s_proj, 1)

                def p_turn3(g):
                    pe.wait_ge(s_xn2, ONE + g + 1)
                    turn_tiles(xn2, s_turn3)

                def p_router(g, b):
                    pe.wait_ge(s_x2T, ONE + g + 1)
                    for s in range(NB):
                        last = nc.tensor.matmul(turn[:, s * EXPERTS:(s + 1) * EXPERTS],
                                                x2T[b][:, s * 128:(s + 1) * 128], wrouter[:, :],
                                                start=True, stop=True)
                    last.then_inc(s_logit, 1)

                def up_products(g, b, e):
                    for c in (2 * e, 2 * e + 1):
                        pe.wait_ge(s_h, ONE + CHUNKS * g + max(c - UP_RING + 1, 0))
                        nc.tensor.matmul(up[c % UP_RING][:, :], w1[:, c * 128:(c + 1) * 128], x2T[b][:, :],
                                         start=True, stop=True).then_inc(s_up, 1)

                def down_products(g, e):
                    pe.wait_ge(s_h, ONE + CHUNKS * g + 2 * e + 2)
                    pe.wait_ge(s_add, ONE + EXPERTS * g + max(e - 1, 0))
                    for s in range(NB):
                        for c in (2 * e, 2 * e + 1):
                            last = nc.tensor.matmul(down[e % 2][:, s * 128:(s + 1) * 128],
                                                    hT[c % H_RING][:, s * 128:(s + 1) * 128],
                                                    w2[:, c * 128:(c + 1) * 128],
                                                    start=(c % 2 == 0), stop=(c % 2 == 1))
                    last.then_inc(s_down, 1)

                def group(g, b, ahead):
                    up_products(g, b, 0)
                    for e in range(EXPERTS):
                        if e + 1 < EXPERTS:
                            up_products(g, b, e + 1)
                        down_products(g, e)
                        if ahead:
                            if e == 1:
                                p_turn1(g + 1)
                            if e == 2:
                                p_qkv(g + 1)
                            if e == 5:
                                p_turn2(g + 1)
                            if e == 6:
                                p_proj(g + 1)
                    if ahead:
                        p_turn3(g + 1)
                        p_router(g + 1, 1 - b)

                p_turn1(0)
                p_qkv(0)
                p_turn2(0)
                p_proj(0)
                p_turn3(0)
                p_router(0, 0)
                with pe.Fori(0, GROUPS - 2, 2) as g:
                    group(g, 0, True)
                    group(g + 1, 1, True)
                group(GROUPS - 2, 0, True)
                group(GROUPS - 1, 1, False)

            @block.vector
            def _(dve):
                def v_stats(g):
                    xg = grp(x, g)
                    for s in range(NB):
                        dve.bn_stats(stats[:, s, :], xg[:, s, :])
                    dve.drain()
                    for s in range(NB):
                        last = dve.bn_aggr(mv[:, s, :], stats[:, s, :])
                    last.then_inc(s_stats, 1)

                def v_norm1(g):
                    dve.wait_ge(s_root, ONE + g + 1)
                    dve.wait_ge(s_turn1, ONE + g)
                    xg = grp(x, g)
                    for s in range(NB):
                        dve.tensor_scalar(hs[:, s, :], xg[:, s, :], mv[:, s, 0:1], roots[:, 1, s:s + 1],
                                          ALU.subtract, ALU.mult)
                    for s in range(NB):
                        last = dve.tensor_scalar(xn1[:, s, :], xg[:, s, :], mv[:, s, 0:1], roots[:, 4, s:s + 1],
                                                 ALU.subtract, ALU.mult)
                    last.then_inc(s_xn1, 1)

                def v_scores(g):
                    dve.drain()
                    dve.wait_ge(s_qkv, ONE + NB * (g + 1))
                    for t in range(NB):
                        n = NB - t
                        dve.tensor_tensor(pairs[:, first[t]:first[t] + n, :], qkv[:, t:NB, 0:D],
                                          qkv[:, t, D:2 * D].unsqueeze(1).broadcast_to([128, n, D]), ALU.mult)
                    dve.drain()
                    for t in range(NB):
                        n = NB - t
                        dve.tensor_reduce(scores[:, t:NB, :, t],
                                          pairs[:, first[t]:first[t] + n, :].rearrange("p s (h d) -> p s h d", d=HD0),
                                          AX.X, ALU.add)
                    dve.drain()
                    dve.tensor_reduce(small[:, 0, :, :], scores[:, :, :, :], AX.X, ALU.max)
                    dve.drain()
                    dve.tensor_tensor(shifted[:, :, :, :], scores[:, :, :, :],
                                      small[:, 0, :, :].unsqueeze(3).broadcast_to([128, NB, HEADS0, NB]),
                                      ALU.subtract).then_inc(s_shift, 1)

                def v_values(g):
                    dve.wait_ge(s_exp, ONE + g + 1)
                    dve.wait_ge(s_turn2, ONE + g)
                    dve.tensor_reduce(small[:, 1, :, :], probs[:, :, :, :], AX.X, ALU.add)
                    dve.drain()
                    dve.reciprocal(small[:, 2, :, :], small[:, 1, :, :])
                    for t in range(NB):
                        n = NB - t
                        for s in range(t, NB):
                            dve.tensor_tensor(
                                pvs[:, first[t] + s - t, :].rearrange("p (h d) -> p h d", d=HD0),
                                probs[:, s, :, t].unsqueeze(2).broadcast_to([128, HEADS0, HD0]),
                                qkv[:, t, 2 * D:3 * D].rearrange("p (h d) -> p h d", d=HD0), ALU.mult)
                    dve.drain()
                    for t in range(1, NB):
                        n = NB - t
                        dve.tensor_tensor(pvs[:, t:NB, :], pvs[:, t:NB, :], pvs[:, first[t]:first[t] + n, :], ALU.add)
                        dve.drain()
                    out = pvs[:, 0:NB, :].rearrange("p s (h d) -> p (s h) d", d=HD0)
                    dve.tensor_tensor(out, out,
                                      small[:, 2, :, :].rearrange("p s h -> p (s h)").unsqueeze(2)
                                      .broadcast_to([128, NB * HEADS0, HD0]), ALU.mult).then_inc(s_heads, 1)

                def v_after(g, b):
                    dve.wait_ge(s_proj, ONE + g + 1)
                    dve.tensor_tensor(after[b][:, :, :], turn[:, :].rearrange("p (s d) -> p s d", d=D),
                                      hs[:, :, :], ALU.add)
                    dve.drain()
                    for s in range(NB):
                        dve.bn_stats(stats2[:, s, :], after[b][:, s, :])
                    dve.drain()
                    for s in range(NB):
                        last = dve.bn_aggr(mv2[:, s, :], stats2[:, s, :])
                    last.then_inc(s_stats2, 1)

                def v_norm2(g, b):
                    dve.wait_ge(s_root2, ONE + g + 1)
                    dve.wait_ge(s_turn3, ONE + g)
                    for s in range(NB):
                        last = dve.tensor_scalar(xn2[:, s, :], after[b][:, s, :], mv2[:, s, 0:1],
                                                 roots2[:, 1, s:s + 1], ALU.subtract, ALU.mult)
                    last.then_inc(s_xn2, 1)

                def v_logits(g):
                    dve.wait_ge(s_logit, ONE + g + 1)
                    logits = turn[:, 0:NB * EXPERTS].rearrange("p (s e) -> p s e", e=EXPERTS)
                    dve.tensor_reduce(gsmall[:, 0, :], logits, AX.X, ALU.max)
                    dve.drain()
                    dve.tensor_tensor(shifted_g[:, :, :], logits,
                                      gsmall[:, 0, :].unsqueeze(2).broadcast_to([128, NB, EXPERTS]),
                                      ALU.subtract).then_inc(s_gshift, 1)

                def v_weights(g, b):
                    dve.wait_ge(s_gexp, ONE + g + 1)
                    dve.tensor_reduce(gsmall[:, 1, :], gate[:, :, :], AX.X, ALU.add)
                    dve.drain()
                    dve.reciprocal(gsmall[:, 2, :], gsmall[:, 1, :])
                    dve.drain()
                    dve.tensor_tensor(gate[:, :, :], gate[:, :, :],
                                      gsmall[:, 2, :].unsqueeze(2).broadcast_to([128, NB, EXPERTS]), ALU.mult)
                    dve.drain()
                    for s in range(NB):
                        dve.max(top[:, s, :], gate[:, s, :])
                    dve.drain()
                    for s in range(NB):
                        dve.max_index(topi[:, s, :], top[:, s, :], gate[:, s, :])
                    dve.drain()
                    dve.tensor_copy(topf[:, :, :], topi[:, :, :])
                    dve.drain()
                    for k in range(TOP_K):
                        for s in range(NB):
                            dve.tensor_scalar(pick[:, k, s, :], expert_ids[:, :], topf[:, s, k:k + 1],
                                              top[:, s, k:k + 1], ALU.is_equal, ALU.mult)
                    dve.drain()
                    dve.tensor_tensor(weight[b][:, :, :], pick[:, 0, :, :], pick[:, 1, :, :], ALU.add)
                    dve.drain()

                def add_expert(g, b, e):
                    dve.wait_ge(s_down, ONE + EXPERTS * g + e + 1)
                    dve.wait_ge(s_add, ONE + EXPERTS * g + e)
                    for s in range(NB):
                        last = dve.scalar_tensor_tensor(after[b][:, s, :], down[e % 2][:, s * 128:(s + 1) * 128],
                                                        weight[b][:, s, e:e + 1], after[b][:, s, :],
                                                        ALU.mult, ALU.add)
                    last.then_inc(s_add, 1)

                def finish(g, b):
                    dve.wait_ge(s_add, ONE + EXPERTS * (g + 1))
                    xg = grp(x, g)
                    dve.scalar_tensor_tensor(xg, after[b][:, :, :], 0.5, xg, ALU.mult, ALU.add)
                    dve.drain()

                def group(g, b, ahead):
                    if ahead:
                        v_stats(g + 1)
                    for e in range(EXPERTS):
                        add_expert(g, b, e)
                        if ahead:
                            if e == 0:
                                v_norm1(g + 1)
                            if e == 3:
                                v_scores(g + 1)
                            if e == 4:
                                v_values(g + 1)
                            if e == 6:
                                v_after(g + 1, 1 - b)
                    finish(g, b)
                    if ahead:
                        v_norm2(g + 1, 1 - b)
                        v_logits(g + 1)
                        v_weights(g + 1, 1 - b)

                dve.memset(scores[:, :, :, :], MASKED)
                dve.drain()
                v_stats(0)
                v_norm1(0)
                v_scores(0)
                v_values(0)
                v_after(0, 0)
                v_norm2(0, 0)
                v_logits(0)
                v_weights(0, 0)
                with dve.Fori(0, GROUPS - 2, 2) as g:
                    group(g, 0, True)
                    group(g + 1, 1, True)
                group(GROUPS - 2, 0, True)
                group(GROUPS - 1, 1, False)


def load_second_half(nc, ctx, A, S, load):
    load("bin1", [128, FC * D], A["bin1"])
    load("bin2", [128, FC * 128], A["bin2"])
    load("rnnA", [128, STATE], A["rnnA"])
    load("rnnB", [D, STATE], A["rnnB"])
    load("rnnC", [STATE, D], A["rnnC"])
    load("rnnD", [128, D], A["rnnD"])
    load("mlp1", [128, FC * 128], A["mlp1"])
    load("mlp2", [128, FC * D], A["mlp2"])
    load("chunk_bias", [128, 2 * FC], A["chunk_bias"])
    load("rows", [128, 4, D], A["rows"].partition_broadcast(128))


def layouts_second_half(f):
    import numpy as np
    chunks_first = lambda w: w.reshape(FC, 128, -1).transpose(1, 0, 2).reshape(128, -1)
    return {
        "bin1": chunks_first(f("L1_ffn_w1")), "bin2": f("L1_ffn_w2"),
        "rnnA": np.pad(f("L1_attn_A").T, ((0, 128 - STATE), (0, 0))), "rnnB": f("L1_attn_Bm").T, "rnnC": f("L1_attn_C").T,
        "rnnD": f("L1_attn_D").T,
        "mlp1": f("L1_attn_W1").T, "mlp2": chunks_first(f("L1_attn_W2").T),
        "chunk_bias": np.concatenate([f("L1_ffn_b1").reshape(FC, 128).T, f("L1_attn_b1").reshape(FC, 128).T], 1),
        "rows": np.stack([f("L1_attn_ln_w"), f("L1_attn_ln_b"), f("L1_attn_b2"), f("L1_ffn_b2")]),
    }


def binarize(nc, S):
    with ExitStack() as ctx:
        sgn = ctx.enter_context(nc.sbuf_tensor("sgn", [128, 2, FC, 128], F32))
        alpha = ctx.enter_context(nc.sbuf_tensor("alpha", [128, FC + 1], F32))
        banks = [ctx.enter_context(nc.psum_tensor(f"bin_turn{i}", [128, 512], F32)) for i in range(2)]
        s_sign, s_bin, s_turn = (ctx.enter_context(nc.semaphore(n)) for n in ("signs", "binarised", "bin_turned"))
        w1 = S["bin1"][:, :].rearrange("p (c d) -> p c d", d=D)
        w2 = S["bin2"][:, :].rearrange("p (c h) -> p c h", h=128)
        with nc.Block() as block:
            @block.scalar
            def _(act):
                for i, w in enumerate((w1, w2)):
                    nc.scalar.activation(sgn[:, i, :, :], w, ACT.Sign).then_inc(s_sign, 1)

            @block.vector
            def _(dve):
                dve.tensor_reduce(alpha[:, 0:FC], w1, AX.X, ALU.add, apply_absolute_value=True)
                dve.tensor_reduce(alpha[:, FC:FC + 1], w2, AX.XY, ALU.add, apply_absolute_value=True)
                dve.drain()
                dve.tensor_scalar(alpha[:, 0:FC], alpha[:, 0:FC], 1.0 / D, None, ALU.mult)
                dve.tensor_scalar(alpha[:, FC:FC + 1], alpha[:, FC:FC + 1], 1.0 / (FC * 128), None, ALU.mult)
                dve.drain()
                dve.wait_ge(s_sign, 2)
                for i, w in enumerate((w1, w2)):
                    for c in range(FC):
                        a = alpha[:, c:c + 1] if i == 0 else alpha[:, FC:FC + 1]
                        dve.scalar_tensor_tensor(sgn[:, i, c, :], sgn[:, i, c, :], a, w[:, c, :],
                                                 ALU.mult, ALU.subtract)
                dve.drain()
                for i, w in enumerate((w1, w2)):
                    dve.tensor_tensor(sgn[:, i, :, :], sgn[:, i, :, :], w, ALU.add).then_inc(s_bin, 1)
                rows = S["rows"]
                dve.tensor_tensor(rows[:, 1, :], rows[:, 1, :], rows[:, 2, :], ALU.add)
                dve.tensor_scalar(rows[:, 3, :], rows[:, 3, :], 0.5, None, ALU.mult)
                for i, n in enumerate(("bin1", "bin2")):
                    dve.wait_ge(s_turn, i + 1)
                    dve.tensor_copy(S[n][:, :], banks[i][:, :])

            @block.tensor
            def _(pe):
                for i in range(2):
                    pe.wait_ge(s_bin, i + 1)
                    for c in range(FC):
                        last = nc.tensor.transpose(banks[i][:, c * 128:(c + 1) * 128], sgn[:, i, c, :],
                                                   S["ident"][:, :])
                    last.then_inc(s_turn, 1)


def second_half(nc, S, tag):
    x = S["x"]
    ident, rows, bias = S["ident"], S["rows"], S["chunk_bias"]
    rnnA, rnnB, rnnC, rnnD = S["rnnA"], S["rnnB"], S["rnnC"], S["rnnD"]
    minus_half = S["minus_half"]
    with ExitStack() as ctx:
        def sb(name, shape, dt=F32):
            return ctx.enter_context(nc.sbuf_tensor(f"{tag}_{name}", shape, dt))

        def bank(name):
            return ctx.enter_context(nc.psum_tensor(f"{tag}_{name}", [128, 512], F32))

        sems = []

        def sem(name):
            sems.append(ctx.enter_context(nc.semaphore(f"{tag}_{name}")))
            return sems[-1]

        NORMS = ("a", "p", "r", "z")
        FFNS = ("a", "r", "z")
        stats = {k: sb(f"stats_{k}", [128, NB, 6]) for k in NORMS}
        mv = {k: sb(f"mv_{k}", [128, NB, 2]) for k in NORMS}
        root = {k: sb(f"root_{k}", [128, 2, NB]) for k in NORMS}
        xn = {k: [sb(f"xn_{k}", [128, NB, D])] * 2 for k in ("a", "r", "z")}
        xn["p"] = [sb(f"xn_p{i}", [128, NB, D]) for i in range(2)]
        nT = {k: [sb(f"nT_{k}", [128, 512])] * 2 for k in ("a", "r", "z")}
        nT["p"] = [sb(f"nT_p{i}", [128, 512]) for i in range(2)]
        state = [sb(f"state{i}", [128, 512]) for i in range(2)]
        mixed = sb("mixed", [128, NB, D])
        resid = sb("resid", [128, NB, D])
        h_pre = [sb(f"h_pre{c}", [128, 512]) for c in range(FC)]
        h_post = [sb(f"h_post{c}", [128, 512]) for c in range(FC)]
        H = {"a": h_pre, "r": h_post, "z": h_post}
        scan = [bank(f"scan{i}") for i in range(2)]
        pre_misc, post_misc = bank("pre_misc"), bank("post_misc")
        up_pre, up_post = [bank(f"up_pre{i}") for i in range(2)], [bank(f"up_post{i}") for i in range(2)]
        MISC = {"a": pre_misc, "p": pre_misc, "r": post_misc, "z": post_misc}
        UP = {"a": up_pre, "r": up_post, "z": up_post}
        W1 = {"a": S["bin1"], "r": S["mlp1"], "z": S["bin1"]}
        W2 = {"a": S["bin2"], "r": S["mlp2"], "z": S["bin2"]}
        BIAS = {"a": 0, "r": FC, "z": 0}

        s_stats = {k: sem(f"stats_{k}") for k in NORMS}
        s_root = {k: sem(f"root_{k}") for k in NORMS}
        s_xn = {k: sem(f"xn_{k}") for k in NORMS}
        s_turn = {k: sem(f"turned_{k}") for k in NORMS}
        s_nT = {k: sem(f"nT_{k}") for k in NORMS}
        s_up = {k: sem(f"up_{k}") for k in FFNS}
        s_h = {k: sem(f"h_{k}") for k in FFNS}
        s_down = {k: sem(f"down_{k}") for k in FFNS}
        s_x = {k: sem(f"x_{k}") for k in FFNS}
        s_step, s_tanh, s_out, s_zero = sem("step_product"), sem("tanh_done"), sem("mixed_product"), sem("zero_state")

        def grp(g):
            return x[:, bass.ds(g, 1), :, :].rearrange("p a s d -> p (a s) d")

        with nc.Block() as block:
            @block.sync
            def _(sp):
                for s in sems:
                    sp.sem_inc(s, ONE)

            @block.gpsimd
            def _(pool):
                def rsqrt(k, g):
                    pool.wait_ge(s_stats[k], ONE + g + 1)
                    pool.wait_ge(s_xn[k], ONE + g)
                    pool.tensor_tensor(root[k][:, 0, :], mv[k][:, :, 1], S["epsilon"][:, 0:NB], ALU.add)
                    pool.drain()
                    pool.tensor_tensor(root[k][:, 1, :], root[k][:, 0, :], minus_half[:, 0:NB],
                                       ALU.pow).then_inc(s_root[k], 1)

                def body(g, post, pre):
                    if pre:
                        rsqrt("a", g + 1)
                    if post:
                        rsqrt("r", g - 1)
                        rsqrt("z", g - 1)
                    if pre:
                        rsqrt("p", g + 1)

                rsqrt("a", 0)
                rsqrt("p", 0)
                body(0, False, True)
                with pool.Fori(1, GROUPS - 1) as g:
                    body(g, True, True)
                body(GROUPS - 1, True, False)
                rsqrt("r", GROUPS - 1)
                rsqrt("z", GROUPS - 1)

            @block.vector
            def _(dve):
                def v_stats(k, src):
                    for s in range(NB):
                        dve.bn_stats(stats[k][:, s, :], src[:, s, :])
                    dve.drain()
                    for s in range(NB):
                        last = dve.bn_aggr(mv[k][:, s, :], stats[k][:, s, :])
                    last.then_inc(s_stats[k], 1)

                def v_norm(k, g, b, src):
                    dve.wait_ge(s_root[k], ONE + g + 1)
                    dve.wait_ge(s_turn[k], ONE + g)
                    for s in range(NB):
                        last = dve.tensor_scalar(xn[k][b][:, s, :], src[:, s, :], mv[k][:, s, 0:1],
                                                 root[k][:, 1, s:s + 1], ALU.subtract, ALU.mult)
                    last.then_inc(s_xn[k], 1)

                def v_nT(k, g, b):
                    dve.wait_ge(s_turn[k], ONE + g + 1)
                    if k == "p":
                        dve.tensor_copy(nT[k][b][:, :].rearrange("p (t s) -> p s t", s=NB),
                                        MISC[k][:, :].rearrange("p (s t) -> p s t", s=NB)).then_inc(s_nT[k], 1)
                        return
                    dve.wait_ge(s_up[k], ONE + FC * g)
                    if k == "r":
                        dve.tensor_scalar(nT[k][b][:, :], MISC[k][:, :], S["lnw_rnn"], S["lnb_rnn"],
                                          ALU.mult, ALU.add).then_inc(s_nT[k], 1)
                    else:
                        dve.tensor_copy(nT[k][b][:, :], MISC[k][:, :]).then_inc(s_nT[k], 1)

                def v_update_bin(k, g):
                    dve.wait_ge(s_down[k], ONE + g + 1)
                    dve.scalar_tensor_tensor(resid[:, :, :], MISC[k][:, :].rearrange("p (s d) -> p s d", d=D), 0.5,
                                             rows[:, 3, :].unsqueeze(1).broadcast_to([128, NB, D]), ALU.mult, ALU.add)
                    dve.drain()
                    dve.tensor_tensor(grp(g), grp(g), resid[:, :, :], ALU.add).then_inc(s_x[k], 1)
                    dve.drain()

                def v_mix(g, b):
                    dve.wait_ge(s_out, ONE + g + 1)
                    dve.tensor_tensor(mixed[:, :, :], post_misc[:, :].rearrange("p (s d) -> p s d", d=D),
                                      xn["p"][b][:, :, :], ALU.add)
                    dve.drain()
                    v_stats("r", mixed)

                def v_resid(g):
                    y = xn["r"][0]
                    dve.drain()
                    dve.tensor_tensor(resid[:, :, :], y[:, :, :],
                                      rows[:, 0, :].unsqueeze(1).broadcast_to([128, NB, D]), ALU.mult)
                    dve.drain()
                    dve.tensor_tensor(resid[:, :, :], resid[:, :, :],
                                      rows[:, 1, :].unsqueeze(1).broadcast_to([128, NB, D]), ALU.add)
                    dve.drain()
                    dve.tensor_tensor(grp(g), grp(g), resid[:, :, :], ALU.add)
                    dve.drain()

                def v_update_mlp(g):
                    dve.wait_ge(s_down["r"], ONE + g + 1)
                    dve.tensor_tensor(grp(g), post_misc[:, :].rearrange("p (s d) -> p s d", d=D), grp(g),
                                      ALU.add).then_inc(s_x["r"], 1)
                    dve.drain()

                def pre_first(g, b):
                    v_stats("a", grp(g))
                    v_norm("a", g, b, grp(g))

                def pre_last(g, b):
                    v_update_bin("a", g)
                    v_stats("p", grp(g))
                    v_norm("p", g, b, grp(g))
                    v_nT("p", g, b)

                def body(g, b, post, pre):
                    if pre:
                        pre_first(g + 1, 1 - b)
                    if post:
                        v_mix(g - 1, 1 - b)
                    if pre:
                        v_nT("a", g + 1, 1 - b)
                    if post:
                        v_norm("r", g - 1, 1 - b, mixed)
                        v_nT("r", g - 1, 1 - b)
                        v_resid(g - 1)
                        v_update_mlp(g - 1)
                        v_stats("z", grp(g - 1))
                        v_norm("z", g - 1, 1 - b, grp(g - 1))
                        v_nT("z", g - 1, 1 - b)
                    if pre:
                        pre_last(g + 1, 1 - b)
                    if post:
                        v_update_bin("z", g - 1)

                for half in state:
                    last = dve.memset(half[:, :], 0.0)
                last.then_inc(s_zero, 1)
                pre_first(0, 0)
                v_nT("a", 0, 0)
                pre_last(0, 0)
                body(0, 0, False, True)
                with dve.Fori(0, GROUPS // 2 - 1) as i:
                    body(2 * i + 1, 1, True, True)
                    body(2 * i + 2, 0, True, True)
                body(GROUPS - 1, 1, True, False)
                v_mix(GROUPS - 1, 1)
                v_norm("r", GROUPS - 1, 1, mixed)
                v_nT("r", GROUPS - 1, 1)
                v_resid(GROUPS - 1)
                v_update_mlp(GROUPS - 1)
                v_stats("z", grp(GROUPS - 1))
                v_norm("z", GROUPS - 1, 1, grp(GROUPS - 1))
                v_nT("z", GROUPS - 1, 1)
                v_update_bin("z", GROUPS - 1)

            def up_piece(pe, k, g, b, i):
                c, s = divmod(i, NB)
                if s == 0:
                    pe.wait_ge(s_nT[k], ONE + g + 1)
                    if c >= 2:
                        pe.wait_ge(s_h[k], ONE + FC * g + c - 1)
                    elif k == "r":
                        pe.wait_ge(s_h["z"], ONE + FC * g)
                    elif k == "z":
                        pe.wait_ge(s_h["r"], ONE + FC * (g + 1))
                    else:
                        pe.wait_ge(s_h[k], ONE + FC * g)
                ins = nc.tensor.matmul(UP[k][c % 2][:, s * 128:(s + 1) * 128], W1[k][:, c * 128:(c + 1) * 128],
                                       nT[k][b][:, s * 128:(s + 1) * 128], start=True, stop=True)
                if s == NB - 1:
                    ins.then_inc(s_up[k], 1)

            def down_piece(pe, k, g, i):
                s, c = divmod(i, FC)
                if i == 0:
                    pe.wait_ge(s_h[k], ONE + FC * (g + 1))
                ins = nc.tensor.matmul(MISC[k][:, s * 128:(s + 1) * 128], H[k][c][:, s * 128:(s + 1) * 128],
                                       W2[k][:, c * 128:(c + 1) * 128], start=(c == 0), stop=(c == FC - 1))
                if i == NB * FC - 1:
                    ins.then_inc(s_down[k], 1)

            def turn_piece(pe, k, g, b, s):
                if s == 0:
                    pe.wait_ge(s_xn[k], ONE + g + 1)
                    if k == "a":
                        pe.wait_ge(s_nT["p"], ONE + g)
                ins = nc.tensor.transpose(MISC[k][:, s * 128:(s + 1) * 128], xn[k][b][:, s, :], ident[:, :])
                if s == NB - 1:
                    ins.then_inc(s_turn[k], 1)

            def input_piece(pe, g, b):
                pe.wait_ge(s_nT["p"], ONE + g + 1)
                nc.tensor.matmul(scan[b][0:STATE, :], rnnB[:, :], nT["p"][b][:, :], start=True, stop=False,
                                 skip_group_check=True)

            def mix_piece(pe, g, b, i):
                s, second = divmod(i, 2)
                if i == 0:
                    pe.wait_ge(s_tanh, ONE + 128 * (g + 1))
                    pe.wait_ge(s_x["z"], ONE + g)
                lhs = (nT["p"][b][:, :] if second else state[b][0:STATE, :]).rearrange("p (t s) -> p s t", s=NB)[:, s, :]
                ins = nc.tensor.matmul(post_misc[:, s * 128:(s + 1) * 128], lhs, (rnnD if second else rnnC)[:, :],
                                       start=not second, stop=bool(second))
                if i == 2 * NB - 1:
                    ins.then_inc(s_out, 1)

            def plan_post(pe, g, b):
                p = [(t, mix_piece, (pe, g, b, t)) for t in range(8)]
                p += [(18 + s, turn_piece, (pe, "r", g, b, s)) for s in range(NB)]
                p += [(24 + i, up_piece, (pe, "r", g, b, i)) for i in range(16)]
                p += [(44 + i, down_piece, (pe, "r", g, i)) for i in range(16)]
                p += [(74 + s, turn_piece, (pe, "z", g, b, s)) for s in range(NB)]
                p += [(80 + i, up_piece, (pe, "z", g, b, i)) for i in range(16)]
                p += [(100 + i, down_piece, (pe, "z", g, i)) for i in range(16)]
                return p

            def plan_pre(pe, g, b):
                p = [(12 + s, turn_piece, (pe, "a", g, b, s)) for s in range(NB)]
                p += [(t, up_piece, (pe, "a", g, b, i)) for i, t in enumerate([40, 41, 42, 43] + list(range(60, 72)))]
                p += [(78 + i, down_piece, (pe, "a", g, i)) for i in range(16)]
                p += [(106 + s, turn_piece, (pe, "p", g, b, s)) for s in range(NB)]
                p += [(120, input_piece, (pe, g, b))]
                return p

            @block.tensor
            def _(pe):
                def run(plan, t):
                    for at, f, args in plan:
                        if at == t:
                            f(*args)

                def body(g, b, post, pre):
                    plan = (plan_post(pe, g - 1, 1 - b) if post else []) + (plan_pre(pe, g + 1, 1 - b) if pre else [])
                    for t in range(128):
                        last = state[b][:, NB * (t - 1):NB * t] if t else state[1 - b][:, 512 - NB:512]
                        pe.wait_ge(s_tanh, ONE + 128 * g + t)
                        nc.tensor.matmul(scan[b][0:STATE, NB * t:NB * (t + 1)], rnnA[:, :], last, start=False,
                                         stop=(t == 127), skip_group_check=True).then_inc(s_step, 1)
                        run(plan, t)

                pre = plan_pre(pe, 0, 0)
                for t in range(128):
                    run(pre, t)
                pe.wait_ge(s_zero, ONE + 1)
                body(0, 0, False, True)
                with pe.Fori(0, GROUPS // 2 - 1) as i:
                    body(2 * i + 1, 1, True, True)
                    body(2 * i + 2, 0, True, True)
                body(GROUPS - 1, 1, True, False)
                post = plan_post(pe, GROUPS - 1, 1)
                for t in range(128):
                    run(post, t)

            @block.scalar
            def _(act):
                def gelu_piece(k, g, c, s):
                    if s == 0:
                        act.wait_ge(s_up[k], ONE + FC * g + c + 1)
                        if k == "z":
                            act.wait_ge(s_down["r"], ONE + g + 1)
                        else:
                            act.wait_ge(s_down["z" if k == "r" else "a"], ONE + g)
                    ins = nc.scalar.activation(H[k][c][:, s * 128:(s + 1) * 128],
                                               UP[k][c % 2][:, s * 128:(s + 1) * 128], ACT.Gelu,
                                               bias=bias[:, BIAS[k] + c:BIAS[k] + c + 1])
                    if s == NB - 1:
                        ins.then_inc(s_h[k], 1)

                def plan_gelus(g_post, g_pre):
                    p = []
                    for c in range(FC):
                        for s in range(NB):
                            if g_post is not None:
                                p.append((28 + 4 * c + s, ("r", g_post, c, s)))
                                p.append((84 + 4 * c + s, ("z", g_post, c, s)))
                            if g_pre is not None:
                                p.append(((44 if c == 0 else 60 + 4 * c) + s, ("a", g_pre, c, s)))
                    return p

                def run(plan, t):
                    for at, args in plan:
                        if at == t:
                            gelu_piece(*args)

                def body(g, b, post, pre):
                    plan = plan_gelus(g - 1 if post else None, g + 1 if pre else None)
                    if post:
                        act.wait_ge(s_out, ONE + g - 1)
                    for t in range(128):
                        act.wait_ge(s_step, ONE + 128 * g + t + 1)
                        nc.scalar.activation(state[b][0:STATE, NB * t:NB * (t + 1)], scan[b][0:STATE, NB * t:NB * (t + 1)],
                                             ACT.Tanh).then_inc(s_tanh, 1)
                        run(plan, t)

                plan = plan_gelus(None, 0)
                for t in range(128):
                    run(plan, t)
                body(0, 0, False, True)
                with act.Fori(0, GROUPS // 2 - 1) as i:
                    body(2 * i + 1, 1, True, True)
                    body(2 * i + 2, 0, True, True)
                body(GROUPS - 1, 1, True, False)
                plan = plan_gelus(GROUPS - 1, None)
                for t in range(128):
                    run(plan, t)


HEADS, HD, BLK, LEVELS = 16, 64, 16, 5
HH = HEADS // 2
FINE = SEQ // BLK
NBLK = [FINE // 2 ** (l + 1) for l in range(1, LEVELS + 1)]
BASE = [FINE + sum(NBLK[:l]) for l in range(LEVELS)]
QBLK = 96
assert BASE[-1] + NBLK[-1] == QBLK - 1
COLS = [SEQ // 2 ** l for l in range(LEVELS + 1)]
COL0 = [sum(COLS[:l]) for l in range(LEVELS + 1)]
X_UP, M_UP, A_UP, N_UP, Y_UP = 16.0, 16.0, 256.0, 256.0, 64.0
ATT_EPS = 1e-8
MASK0 = -3e38
LEAST = 1e-20


def attention_layouts(f):
    import numpy as np
    w = f("L0_attn_w_qkv").reshape(3, HEADS, HD, D).transpose(0, 2, 1, 3).reshape(3, HD, HEADS * D)
    p = np.arange(128)
    head, i = p // BLK, p % BLK
    sel = np.zeros((128, 2, BLK, HEADS), np.float16)
    for half in range(2):
        sel[p, half, i, head + HH * half] = 1
    own = np.zeros((128, 2, HEADS), np.float32)
    for half in range(2):
        own[p, half, head + HH * half] = 1
    return {
        "att_wq": w[0], "att_wk": w[1], "att_wv": w[2],
        "att_wo": f("L0_attn_w_out").T.reshape(HEADS, HD, D).transpose(1, 0, 2).reshape(HD, HEADS * D),
        "att_bias": f("L0_attn_b_out").reshape(1, D),
        "att_sel": sel.reshape(128, -1), "att_selT": sel.transpose(3, 1, 2, 0).reshape(HEADS, -1),
        "att_own": own.reshape(128, -1),
        "att_mask": np.where(np.arange(BLK)[None, :] > i[:, None], MASK0, 0.0).astype(np.float32),
    }


def load_attention(nc, ctx, A, S, load):
    load("att_sel", [128, 2 * BLK * HEADS], A["att_sel"], F16)
    load("att_selT", [HEADS, 2 * BLK * 128], A["att_selT"], F16)
    load("att_own", [128, 2 * HEADS], A["att_own"])
    load("att_mask", [128, BLK], A["att_mask"])
    load("att_bias", [128, 1, D], A["att_bias"].partition_broadcast(128))


def combine_weights(nc, A, S, att):
    rmax = bass.bass_isa.ReduceOp.max
    with ExitStack() as ctx:
        sb = lambda n, shape: ctx.enter_context(nc.sbuf_tensor(n, shape, F32))
        w = {k: sb(f"w_{k}", [HD, HEADS * D]) for k in ("att_wq", "att_wk", "att_wv", "att_wo")}
        banks = [ctx.enter_context(nc.psum_tensor(f"cw{i}", [128, 512], F32)) for i in range(8)]
        scaled = [sb(f"scaled{i}", [128, HEADS * D]) for i in range(2)]
        peak, allpeak, up = sb("peak", [128, 32]), sb("allpeak", [128, 32]), sb("up", [128, 32])
        tmp = sb("own_peaks", [128, 2, HEADS])
        s_w, s_mm, s_peak, s_all, s_sc, s_hi = (ctx.enter_context(nc.semaphore(n)) for n in
                                               ("cw_load", "cw_mm", "cw_peak", "cw_all", "cw_scaled", "cw_hi"))
        with nc.Block() as block:
            @block.sync
            def _(sp):
                for k in w:
                    sp.dma_start(w[k][:, :], A[k]).then_inc(s_w, 16)

            @block.tensor
            def _(pe):
                pe.wait_ge(s_w, 64)
                for i, (a, b) in enumerate((("att_wq", "att_wk"), ("att_wv", "att_wo"))):
                    for h in range(HEADS):
                        ins = nc.tensor.matmul(banks[4 * i + h // 4][:, (h % 4) * D:(h % 4 + 1) * D],
                                               w[a][:, h * D:(h + 1) * D], w[b][:, h * D:(h + 1) * D],
                                               start=True, stop=True)
                    ins.then_inc(s_mm, 1)

            @block.gpsimd
            def _(pool):
                pool.wait_ge(s_peak, 1)
                pool.partition_all_reduce(allpeak[:, :], peak[:, :], 128, rmax).then_inc(s_all, 1)

            @block.vector
            def _(dve):
                dve.memset(peak[:, :], 0.0)
                dve.drain()
                dve.wait_ge(s_mm, 2)
                for j in range(4):
                    dve.tensor_reduce(peak[:, 4 * j:4 * j + 4], banks[j][:, :].rearrange("p (h d) -> p h d", d=D),
                                      AX.X, ALU.max, apply_absolute_value=True)
                    dve.tensor_reduce(peak[:, 16 + j:17 + j], banks[4 + j][:, :], AX.X, ALU.max,
                                      apply_absolute_value=True)
                dve.drain()
                dve.tensor_reduce(peak[:, 20:21], peak[:, 16:20], AX.X, ALU.max).then_inc(s_peak, 1)
                dve.wait_ge(s_all, 1)
                dve.tensor_scalar(allpeak[:, :], allpeak[:, :], LEAST, None, ALU.max)
                dve.drain()
                dve.reciprocal(up[:, :], allpeak[:, :])
                dve.drain()
                dve.tensor_scalar(up[:, 0:16], up[:, 0:16], M_UP, None, ALU.mult)
                dve.tensor_scalar(up[:, 20:21], up[:, 20:21], N_UP, None, ALU.mult)
                for half in range(2):
                    dve.tensor_tensor(tmp[:, half, :], S["att_own"][:, half * HEADS:(half + 1) * HEADS],
                                      allpeak[:, 0:HEADS], ALU.mult)
                dve.drain()
                dve.tensor_reduce(att["undo"][:, 0:2], tmp[:, :, :], AX.X, ALU.add)
                dve.tensor_scalar(att["undo"][:, 2:3], allpeak[:, 20:21], 1.0 / (N_UP * Y_UP), None, ALU.mult)
                dve.drain()
                dve.tensor_scalar(att["undo"][:, 0:2], att["undo"][:, 0:2], HD ** -0.5 / (X_UP * X_UP * M_UP), None,
                                  ALU.mult)
                for h in range(HEADS):
                    dve.tensor_scalar(scaled[0][:, h * D:(h + 1) * D], banks[h // 4][:, (h % 4) * D:(h % 4 + 1) * D],
                                      up[:, h:h + 1], None, ALU.mult)
                for j in range(4):
                    dve.tensor_scalar(scaled[1][:, 512 * j:512 * (j + 1)], banks[4 + j][:, :], up[:, 20:21], None,
                                      ALU.mult)
                dve.drain().then_inc(s_sc, 1)
                dve.wait_ge(s_hi, 2)
                for i, n in enumerate("MN"):
                    dve.tensor_tensor(att[n + "lo"][:, :], scaled[i][:, :], att[n + "hi"][:, :], ALU.subtract)

            @block.scalar
            def _(act):
                act.wait_ge(s_sc, 1)
                for i, n in enumerate("MN"):
                    nc.scalar.activation(att[n + "hi"][:, :], scaled[i][:, :], ACT.Copy).then_inc(s_hi, 1)


def hierarchical_attention(nc, A, S, tag):
    x, ident = S["x"], S["ident"]
    outer = ExitStack()
    with outer:
        att = {n: outer.enter_context(nc.sbuf_tensor("att_" + n, [128, HEADS * D], F16))
               for n in ("Mhi", "Mlo", "Nhi", "Nlo")}
        att["undo"] = outer.enter_context(nc.sbuf_tensor("att_undo", [128, 4], F32))
        combine_weights(nc, A, S, att)
        attention_core(nc, S, att, x, ident)


def attention_core(nc, S, att, x, ident):
    sel = S["att_sel"][:, :].rearrange("p (j h) -> p j h", h=HEADS)
    selT = S["att_selT"][:, :].rearrange("h (j p) -> h j p", p=128)
    with ExitStack() as ctx:
        sb = lambda n, shape, dt=F32: ctx.enter_context(nc.sbuf_tensor("at_" + n, shape, dt))
        bank = lambda n: ctx.enter_context(nc.psum_tensor("at_" + n, [128, 512], F32))
        sems = []

        def sem(n):
            sems.append(ctx.enter_context(nc.semaphore("at_" + n)))
            return sems[-1]

        stats, mv, root = sb("stats", [128, GROUPS, 6]), sb("mv", [128, GROUPS, 2]), sb("root", [128, 3, GROUPS])
        xn = sb("xn", [128, GROUPS, D])
        xT = sb("xT", [128, sum(COLS)])
        keys = sb("keys", [128, QBLK, 4, BLK], F16)
        coarse_q = sb("coarse_q", [128, 2, QBLK - FINE, BLK], F16)
        values = sb("values", [128, QBLK // 2, 2, D], F16)
        big = [sb(f"big{i}", [128, 2 * 32 * HEADS * BLK], F16) for i in range(2)]
        half_of = lambda t, i: t[:, i * 8192:(i + 1) * 8192].rearrange("p (q h i) -> p q h i", h=HEADS, i=BLK)
        XH, XL = ([half_of(t, i) for i in range(2)] for t in big)
        W4 = 2 * QBLK * 4 * BLK
        A4 = big[0][:, 0:W4].rearrange("p (q e i) -> p q e i", e=4, i=BLK)
        A4T = big[1][:, 0:W4].rearrange("p (a q c) -> p a q c", a=2, c=128)
        tile_of = lambda t, i: t[:, W4 + i * HEADS * 128:W4 + (i + 1) * HEADS * 128].rearrange("p (h t) -> p h t", h=HEADS)
        YH, YL = ([tile_of(t, i) for i in range(2)] for t in big)
        rden16 = big[0][0:HEADS, W4:W4 + 2 * BLK * QBLK].rearrange("h (e i q) -> h e i q", e=2, q=QBLK)
        logits = [sb(f"logits{i}", [128, 2, 16, BLK]) for i in range(2)]
        peaks = [sb(f"peaks{i}", [128, 2, 16]) for i in range(2)]
        E = sb("E", [128, 2, QBLK, BLK])
        sums, sums16 = sb("sums", [128, 2, QBLK]), sb("sums16", [128, 2, 2 * QBLK], F16)
        den = xn[0:HEADS, :, :].rearrange("h g d -> h (g d)")
        rden = xT[0:HEADS, 0:BLK * QBLK].rearrange("h (i q) -> h i q", q=QBLK)
        cden = sb("cden", [HEADS, BLK, QBLK - FINE])
        scale = sb("scale", [128, 2 * QBLK])
        ident16 = sb("ident16", [128, 128], F16)

        xmb = [bank(f"xm{i}") for i in range(2)]
        sbk = [bank(f"s{i}") for i in range(2)]
        TRN = 4
        tr = [bank(f"tr{i}") for i in range(TRN)]

        s_stats, s_root, s_xn, s_tr, s_trout = sem("stats"), sem("root"), sem("xn"), sem("turned"), sem("turn_out")
        s_pool, s_khi, s_keys = sem("pooled"), sem("keys_hi"), sem("keys")
        s_xm, s_xhi, s_xlo = sem("xm"), sem("xm_hi"), sem("xm_lo")
        s_s, s_sread, s_sub, s_e = sem("logits"), sem("logits_read"), sem("logits_shifted"), sem("exp")
        s_sums, s_den, s_denread, s_rden, s_scaled = (sem("sums"), sem("den"), sem("den_read"), sem("rden"),
                                                      sem("scaled"))
        s_ahi, s_a4, s_y, s_yhi, s_ylo, s_out, s_x = (sem("a_hi"), sem("a4"), sem("y"), sem("y_hi"), sem("y_lo"),
                                                      sem("out"), sem("x"))
        s_const = sem("const")

        U_X, U_V, U_R, U_A = 0, 2, 8, 9
        USES = U_A + 12
        CH = 3

        def level(l, odd):
            v = xT[:, COL0[l]:COL0[l] + COLS[l]].rearrange("p (m o i) -> p m o i", o=2, i=BLK)
            return v[:, :, odd, :]

        def spots(t, l):
            step = 2 ** l
            v = t[:, :].rearrange("h (m o i r) -> h m o i r", o=2, i=BLK, r=step)
            return v[:, :, 1, :, step - 1]

        def xs(s):
            return x[:, :, bass.ds(s, 1), :].rearrange("p g a d -> p g (a d)")

        with nc.Block() as block:
            @block.sync
            def _(sp):
                for s in sems:
                    sp.sem_inc(s, ONE)

            @block.gpsimd
            def _(pool):
                with pool.Fori(0, NB) as s:
                    pool.wait_ge(s_stats, ONE + s + 1)
                    pool.wait_ge(s_xn, ONE + s)
                    pool.tensor_tensor(root[:, 0, :], mv[:, :, 1], S["epsilon"][:, 0:GROUPS], ALU.add)
                    pool.drain()
                    pool.tensor_tensor(root[:, 1, :], root[:, 0, :], S["minus_half"][:, 0:GROUPS], ALU.pow)
                    pool.drain()
                    pool.tensor_scalar(root[:, 2, :], root[:, 1, :], X_UP, None, ALU.mult).then_inc(s_root, 1)
                    pool.drain()

            @block.scalar
            def _(act):
                def hi_keys(s):
                    act.wait_ge(s_pool, ONE + s + 1)
                    act.wait_ge(s_s, ONE + 6 * s)
                    act.wait_ge(s_tr, ONE + USES * s)
                    nc.scalar.activation(keys[:, 0:FINE, 0:2, :],
                                         xT[:, 0:SEQ].rearrange("p (q i) -> p q i", i=BLK).unsqueeze(2)
                                         .broadcast_to([128, FINE, 2, BLK]), ACT.Copy)
                    for l in range(1, LEVELS + 1):
                        n, b = NBLK[l - 1], BASE[l - 1]
                        nc.scalar.activation(keys[:, b:b + n, 0:2, :],
                                             level(l, 0).unsqueeze(2).broadcast_to([128, n, 2, BLK]),
                                             ACT.Copy, scale=2.0 ** -l)
                        last = nc.scalar.activation(coarse_q[:, 0, b - FINE:b - FINE + n, :], level(l, 1),
                                                    ACT.Copy, scale=2.0 ** -l)
                    last.then_inc(s_khi, 1)

                def hi_xm(s, c):
                    act.wait_ge(s_s, ONE + 6 * s + 2 * max(c - 1, 0))
                    if c == 0:
                        act.wait_ge(s_out, ONE + 8 * s)
                    for h in range(HEADS):
                        act.wait_ge(s_xm, ONE + 48 * s + 16 * c + h + 1)
                        nc.scalar.activation(XH[c % 2][:, :, h, :], xmb[h % 2][:, :].rearrange("p (q i) -> p q i", i=BLK),
                                             ACT.Copy).then_inc(s_xhi, 1)

                def exps(s, c):
                    for j in range(2):
                        k = 2 * c + j
                        act.wait_ge(s_sub, ONE + 6 * s + k + 1)
                        act.wait_ge(s_a4, ONE + s)
                        for half in range(2):
                            last = nc.scalar.activation(E[:, half, 16 * k:16 * k + 16, :], logits[j][:, half, :, :],
                                                        ACT.Exp, scale=att["undo"][:, half:half + 1])
                        last.then_inc(s_e, 1)

                def hi_weights(s):
                    act.wait_ge(s_scaled, ONE + s + 1)
                    act.wait_ge(s_tr, ONE + USES * s)
                    nc.scalar.activation(A4[:, :, 0:4:2, :],
                                         E[:, :, :, :].rearrange("p a q i -> p (a q) i").unsqueeze(2)
                                         .broadcast_to([128, 2 * QBLK, 2, BLK]), ACT.Copy).then_inc(s_ahi, 1)

                def hi_y(s, ck, half):
                    n = 2 * ck + half
                    t = ck // 2
                    act.wait_ge(s_y, ONE + 32 * s + n + 1)
                    act.wait_ge(s_out, ONE + 8 * s + max(t - 1, 0))
                    nc.scalar.activation(YH[t % 2][:, HH * half:HH * (half + 1), 64 * (ck % 2):64 * (ck % 2) + 64],
                                         xmb[n % 2][:, :].rearrange("p (h t) -> p h t", h=HH), ACT.Copy,
                                         scale=Y_UP / (X_UP * A_UP)).then_inc(s_yhi, 1)

                act.wait_ge(s_const, ONE + 1)
                with act.Fori(0, NB) as s:
                    hi_keys(s)
                    hi_xm(s, 0)
                    hi_xm(s, 1)
                    exps(s, 0)
                    hi_xm(s, 2)
                    exps(s, 1)
                    exps(s, 2)
                    hi_weights(s)
                    for ck in range(16):
                        for half in range(2):
                            hi_y(s, ck, half)

            @block.tensor
            def _(pe):
                def use(s, u):
                    pe.wait_ge(s_trout, ONE + USES * s + max(u - TRN + 1, 0))
                    return tr[u % TRN]

                def rows(s):
                    pe.wait_ge(s_xn, ONE + s + 1)
                    for u in range(2):
                        b = use(s, U_X + u)
                        for j in range(4):
                            last = nc.tensor.transpose(b[:, 128 * j:128 * (j + 1)], xn[:, 4 * u + j, :], ident[:, :])
                        last.then_inc(s_tr, 1)

                def turn_values(s):
                    pe.wait_ge(s_keys, ONE + s + 1)
                    for u in range(6):
                        b = use(s, U_V + u)[:, :].bitcast(F16)
                        for j in range(8):
                            src = keys[:, 16 * u + 2 * j:16 * u + 2 * j + 2, :, :].rearrange("p q e i -> p (q e i)")
                            last = nc.tensor.transpose(b[:, 128 * j:128 * (j + 1)], src, ident16[:, :])
                        last.then_inc(s_tr, 1)

                def xm(s, c):
                    src = lambda lo: keys[:, 32 * c:32 * c + 32, 2 * lo, :] if c < 2 else coarse_q[:, lo, :, :]
                    for h in range(HEADS):
                        n = 16 * c + h
                        pe.wait_ge(s_xlo, ONE + 48 * s + max(n - 1, 0))
                        if n < 2:
                            pe.wait_ge(s_ylo, ONE + 32 * s)
                        for i, (w, lo) in enumerate((("Mhi", 0), ("Mhi", 1), ("Mlo", 0))):
                            last = nc.tensor.matmul(xmb[h % 2][:, :], att[w][:, h * D:(h + 1) * D], src(lo),
                                                    start=(i == 0), stop=(i == 2))
                        last.then_inc(s_xm, 1)

                def logits_of(s, c):
                    pe.wait_ge(s_xlo, ONE + 48 * s + 16 * (c + 1))
                    for j in range(2):
                        k = 2 * c + j
                        pe.wait_ge(s_sread, ONE + 6 * s + max(k - 1, 0))
                        if k < 2:
                            pe.wait_ge(s_x, ONE + 8 * s)
                        for q in range(16):
                            blk = 16 * k + q
                            for half in range(2):
                                o = sbk[j][:, 256 * half + BLK * q:256 * half + BLK * (q + 1)]
                                hs_ = slice(HH * half, HH * (half + 1))
                                lh = XH[c % 2][:, 16 * j + q, hs_, :].rearrange("p h i -> p (h i)")
                                ll = XL[c % 2][:, 16 * j + q, hs_, :].rearrange("p h i -> p (h i)")
                                nc.tensor.matmul(o, lh, keys[:, blk, 0, :], start=True, stop=False)
                                nc.tensor.matmul(o, lh, keys[:, blk, 2, :], start=False, stop=False)
                                last = nc.tensor.matmul(o, ll, keys[:, blk, 0, :], start=False, stop=True)
                        last.then_inc(s_s, 1)

                def denominators(s):
                    pe.wait_ge(s_sums, ONE + s + 1)
                    for u in range(4):
                        if u >= 2:
                            pe.wait_ge(s_denread, ONE + 4 * s + u - 1)
                        for ii in range(4):
                            i = 4 * u + ii
                            for n, (half, lo) in enumerate(((0, 0), (0, 1), (1, 0), (1, 1))):
                                last = nc.tensor.matmul(sbk[u % 2][0:HEADS, 128 * ii:128 * ii + QBLK],
                                                        sel[:, BLK * half + i, :],
                                                        sums16[:, lo, QBLK * half:QBLK * (half + 1)],
                                                        start=(n == 0), stop=(n == 3))
                        last.then_inc(s_den, 1)

                def spread(s):
                    pe.wait_ge(s_rden, ONE + s + 1)
                    b = use(s, U_R)
                    for half in range(2):
                        for i in range(BLK):
                            for lo in range(2):
                                last = nc.tensor.matmul(b[:, QBLK * half:QBLK * (half + 1)],
                                                        selT[:, BLK * half + i, :], rden16[:, lo, i, :],
                                                        start=(i == 0 and lo == 0), stop=(i == BLK - 1 and lo == 1))
                    last.then_inc(s_tr, 1)

                def turn_weights(s):
                    pe.wait_ge(s_a4, ONE + s + 1)
                    for u in range(12):
                        b = use(s, U_A + u)[:, :].bitcast(F16)
                        for j in range(8):
                            n = 16 * u + 2 * j
                            last = nc.tensor.transpose(b[:, 128 * j:128 * (j + 1)],
                                                       A4[:, n:n + 2, :, :].rearrange("p q e i -> p (q e i)"),
                                                       ident16[:, :])
                        last.then_inc(s_tr, 1)

                def apply_weights(s, ck, half):
                    n = 2 * ck + half
                    if n == 0:
                        pe.wait_ge(s_trout, ONE + USES * (s + 1))
                    pe.wait_ge(s_ylo, ONE + 32 * s + max(n - 1, 0))
                    y = xmb[n % 2][:, :].rearrange("p (h t) -> p h t", h=HH)
                    jobs = [(4 * ck + j, 0, BLK, 16 * j, 1) for j in range(4)]
                    for l in range(1, LEVELS + 1):
                        step = 2 ** l
                        start = 64 * ck + step - 1 if step * BLK >= 64 else 64 * ck + 32 + step - 1
                        blk, i = divmod(start // step, BLK)
                        if blk % 2 == 1:
                            cnt = (64 * (ck + 1) - start + step - 1) // step
                            jobs.append((BASE[l - 1] + blk // 2, i, cnt, start - 64 * ck, step))
                    for a, (q, i, cnt, at, step) in enumerate(jobs):
                        rhs = A4T[:, half, q // 2, :].rearrange("p (h i) -> p h i", i=BLK)[:, :, i:i + cnt]
                        last = nc.tensor.matmul(y[:, :, at:at + (cnt - 1) * step + 1:step], values[:, q // 2, q % 2, :], rhs,
                                                start=(a == 0), stop=(a == len(jobs) - 1), skip_group_check=True)
                    last.then_inc(s_y, 1)

                def project(s, t):
                    pe.wait_ge(s_ylo, ONE + 32 * s + 4 * (t + 1))
                    pe.wait_ge(s_x, ONE + 8 * s + max(t - 1, 0))
                    if t < 2:
                        pe.wait_ge(s_denread, ONE + 4 * (s + 1))
                    for h in range(HEADS):
                        for n, (y, w) in enumerate(((YH, "Nhi"), (YH, "Nlo"), (YL, "Nhi"))):
                            last = nc.tensor.matmul(sbk[t % 2][:, 0:D], y[t % 2][:, h, :], att[w][:, h * D:(h + 1) * D],
                                                    start=(h == 0 and n == 0), stop=(h == HEADS - 1 and n == 2))
                    last.then_inc(s_out, 1)

                pe.wait_ge(s_const, ONE + 1)
                with pe.Fori(0, NB) as s:
                    rows(s)
                    turn_values(s)
                    xm(s, 0)
                    xm(s, 1)
                    logits_of(s, 0)
                    xm(s, 2)
                    logits_of(s, 1)
                    logits_of(s, 2)
                    denominators(s)
                    spread(s)
                    turn_weights(s)
                    for ck in range(16):
                        for half in range(2):
                            apply_weights(s, ck, half)
                        if ck % 2 == 1 and ck >= 3:
                            project(s, ck // 2 - 1)
                    project(s, 7)

            @block.vector
            def _(dve):
                def norm(s):
                    for g in range(GROUPS):
                        dve.bn_stats(stats[:, g, :], xs(s)[:, g, :])
                    dve.drain()
                    for g in range(GROUPS):
                        last = dve.bn_aggr(mv[:, g, :], stats[:, g, :])
                    last.then_inc(s_stats, 1)
                    dve.wait_ge(s_root, ONE + s + 1)
                    dve.wait_ge(s_tr, ONE + USES * s)
                    for g in range(GROUPS):
                        last = dve.tensor_scalar(xn[:, g, :], xs(s)[:, g, :], mv[:, g, 0:1], root[:, 2, g:g + 1],
                                                 ALU.subtract, ALU.mult)
                    last.then_inc(s_xn, 1)
                    dve.wait_ge(s_xn, ONE + s + 1)
                    dve.tensor_tensor(xs(s), xs(s), S["att_bias"][:, :, :].broadcast_to([128, GROUPS, D]), ALU.add)

                def pool_levels(s):
                    for u in range(2):
                        dve.wait_ge(s_tr, ONE + USES * s + U_X + u + 1)
                        dve.tensor_copy(xT[:, 512 * u:512 * (u + 1)], tr[(U_X + u) % TRN][:, :]).then_inc(s_trout, 1)
                    for l in range(1, LEVELS + 1):
                        dve.drain()
                        v = xT[:, COL0[l - 1]:COL0[l - 1] + COLS[l - 1]].rearrange("p (t o) -> p t o", o=2)
                        last = dve.tensor_tensor(xT[:, COL0[l]:COL0[l] + COLS[l]], v[:, :, 0], v[:, :, 1], ALU.add)
                    last.then_inc(s_pool, 1)

                def lo_keys(s):
                    dve.wait_ge(s_khi, ONE + s + 1)
                    dve.wait_ge(s_pool, ONE + s + 1)
                    fine = xT[:, 0:SEQ].rearrange("p (q i) -> p q i", i=BLK)
                    dve.tensor_tensor(keys[:, 0:FINE, 2, :], fine, keys[:, 0:FINE, 0, :], ALU.subtract)
                    for l in range(1, LEVELS + 1):
                        n, b = NBLK[l - 1], BASE[l - 1]
                        dve.scalar_tensor_tensor(keys[:, b:b + n, 2, :], level(l, 0), 2.0 ** -l,
                                                 keys[:, b:b + n, 0, :], ALU.mult, ALU.subtract)
                        c = slice(b - FINE, b - FINE + n)
                        dve.scalar_tensor_tensor(coarse_q[:, 1, c, :], level(l, 1), 2.0 ** -l,
                                                 coarse_q[:, 0, c, :], ALU.mult, ALU.subtract)
                    dve.drain()
                    dve.tensor_copy(keys[:, 0:QBLK - 1, 3, :], keys[:, 0:QBLK - 1, 2, :]).then_inc(s_keys, 1)

                def out_values(s):
                    for u in range(6):
                        dve.wait_ge(s_tr, ONE + USES * s + U_V + u + 1)
                        if u == 0:
                            dve.wait_ge(s_y, ONE + 32 * s)
                        for o in range(2):
                            r = slice(64 * o, 64 * o + 64)
                            last = dve.tensor_copy(values[r, 8 * u:8 * u + 8, o, :],
                                                   tr[(U_V + u) % TRN][r, :].bitcast(F16)
                                                   .rearrange("p (q d) -> p q d", d=D))
                        last.then_inc(s_trout, 1)

                def lo_xm(s, c):
                    dve.wait_ge(s_s, ONE + 6 * s + 2 * max(c - 1, 0))
                    if c == 0:
                        dve.wait_ge(s_out, ONE + 8 * s)
                    for h in range(HEADS):
                        dve.wait_ge(s_xhi, ONE + 48 * s + 16 * c + h + 1)
                        dve.tensor_tensor(XL[c % 2][:, :, h, :], xmb[h % 2][:, :].rearrange("p (q i) -> p q i", i=BLK),
                                          XH[c % 2][:, :, h, :], ALU.subtract).then_inc(s_xlo, 1)

                def shift(s, k):
                    j = k % 2
                    dve.wait_ge(s_s, ONE + 6 * s + k + 1)
                    dve.wait_ge(s_e, ONE + 6 * s + max(k - 1, 0))
                    t = logits[j][:, :, :, :].rearrange("p a q i -> p (a q) i")
                    src = sbk[j][:, :].rearrange("p (q i) -> p q i", i=BLK)
                    if k < 4:
                        dve.tensor_tensor(t, src, S["att_mask"][:, :].unsqueeze(1).broadcast_to([128, 32, BLK]),
                                          ALU.add).then_inc(s_sread, 1)
                    else:
                        dve.tensor_copy(t, src).then_inc(s_sread, 1)
                    dve.drain()
                    pk = peaks[j][:, :, :].rearrange("p a q -> p (a q)")
                    dve.tensor_reduce(pk, t, AX.X, ALU.max)
                    dve.drain()
                    dve.tensor_tensor(t, t, pk.unsqueeze(2).broadcast_to([128, 32, BLK]),
                                      ALU.subtract).then_inc(s_sub, 1)

                def add_up(s, k):
                    dve.wait_ge(s_e, ONE + 6 * s + k + 1)
                    dve.tensor_reduce(sums[:, :, 16 * k:16 * k + 16], E[:, :, 16 * k:16 * k + 16, :], AX.X, ALU.add)

                def split_sums(s):
                    dve.drain()
                    flat = sums[:, :, :].rearrange("p a q -> p (a q)")
                    dve.tensor_copy(sums16[:, 0, :], flat)
                    dve.drain()
                    dve.tensor_tensor(sums16[:, 1, :], flat, sums16[:, 0, :], ALU.subtract).then_inc(s_sums, 1)

                def invert(s):
                    dv = den[:, :].rearrange("h (q i) -> h i q", i=BLK)
                    for u in range(4):
                        dve.wait_ge(s_den, ONE + 4 * s + u + 1)
                        b = sbk[u % 2][0:HEADS, :].rearrange("h (i q) -> h i q", q=128)
                        dve.tensor_copy(dv[:, 4 * u:4 * u + 4, :], b[:, :, 0:FINE])
                        dve.tensor_copy(cden[:, 4 * u:4 * u + 4, :], b[:, :, FINE:QBLK]).then_inc(s_denread, 1)
                    for l in range(1, LEVELS + 1):
                        dve.drain()
                        n, b = NBLK[l - 1], BASE[l - 1] - FINE
                        at = spots(den, l)
                        dve.tensor_tensor(at, at, cden[:, :, b:b + n].rearrange("h i m -> h m i"), ALU.add)
                    dve.drain()
                    dve.tensor_scalar(den[:, :], den[:, :], ATT_EPS, None, ALU.add)
                    dve.drain()
                    dve.reciprocal(den[:, :], den[:, :])
                    dve.drain()
                    dve.memset(rden[:, :, QBLK - 1:QBLK], 0.0)
                    dve.tensor_scalar(rden[:, :, 0:FINE], dv, A_UP, None, ALU.mult)
                    for l in range(1, LEVELS + 1):
                        n, b = NBLK[l - 1], BASE[l - 1]
                        dve.tensor_scalar(rden[:, :, b:b + n].rearrange("h i m -> h m i"), spots(den, l),
                                          A_UP * 2.0 ** l, None, ALU.mult)
                    dve.drain()
                    dve.tensor_copy(rden16[:, 0, :, :], rden[:, :, :])
                    dve.drain()
                    dve.tensor_tensor(rden16[:, 1, :, :], rden[:, :, :], rden16[:, 0, :, :],
                                      ALU.subtract).then_inc(s_rden, 1)

                def weights(s):
                    dve.wait_ge(s_tr, ONE + USES * s + U_R + 1)
                    dve.tensor_copy(scale[:, :], tr[U_R % TRN][:, 0:2 * QBLK]).then_inc(s_trout, 1)
                    dve.drain()
                    e = E[:, :, :, :].rearrange("p a q i -> p (a q) i")
                    dve.tensor_tensor(e, e, scale[:, :].unsqueeze(2).broadcast_to([128, 2 * QBLK, BLK]),
                                      ALU.mult).then_inc(s_scaled, 1)
                    dve.wait_ge(s_ahi, ONE + s + 1)
                    dve.wait_ge(s_scaled, ONE + s + 1)
                    dve.tensor_tensor(A4[:, :, 1, :], e, A4[:, :, 0, :], ALU.subtract)
                    dve.drain()
                    dve.tensor_copy(A4[:, :, 3, :], A4[:, :, 1, :]).then_inc(s_a4, 1)

                def out_weights(s):
                    for u in range(12):
                        dve.wait_ge(s_tr, ONE + USES * s + U_A + u + 1)
                        half, q = divmod(8 * u, QBLK // 2)
                        dve.tensor_copy(A4T[:, half, q:q + 8, :].rearrange("p q d -> p (q d)").bitcast(F32),
                                        tr[(U_A + u) % TRN][:, :]).then_inc(s_trout, 1)

                def lo_y(s, ck, half):
                    n = 2 * ck + half
                    t = ck // 2
                    dve.wait_ge(s_yhi, ONE + 32 * s + n + 1)
                    dve.wait_ge(s_out, ONE + 8 * s + max(t - 1, 0))
                    where = (slice(None), slice(HH * half, HH * (half + 1)), slice(64 * (ck % 2), 64 * (ck % 2) + 64))
                    dve.scalar_tensor_tensor(YL[t % 2][where], xmb[n % 2][:, :].rearrange("p (h t) -> p h t", h=HH),
                                             Y_UP / (X_UP * A_UP), YH[t % 2][where], ALU.mult,
                                             ALU.subtract).then_inc(s_ylo, 1)

                def update(s, t):
                    dve.wait_ge(s_out, ONE + 8 * s + t + 1)
                    xt = xs(s)[:, t, :]
                    dve.scalar_tensor_tensor(xt, sbk[t % 2][:, 0:D], att["undo"][:, 2:3], xt, ALU.mult,
                                             ALU.add).then_inc(s_x, 1)

                dve.memset(values[:, :, :, :], 0.0)
                dve.memset(keys[:, QBLK - 1:QBLK, :, :], 0.0)
                dve.memset(coarse_q[:, :, QBLK - FINE - 1:QBLK - FINE, :], 0.0)
                dve.tensor_copy(ident16[:, :], ident[:, :])
                dve.drain().then_inc(s_const, 1)
                with dve.Fori(0, NB) as s:
                    norm(s)
                    pool_levels(s)
                    lo_keys(s)
                    out_values(s)
                    lo_xm(s, 0)
                    lo_xm(s, 1)
                    shift(s, 0)
                    shift(s, 1)
                    add_up(s, 0)
                    add_up(s, 1)
                    lo_xm(s, 2)
                    shift(s, 2)
                    shift(s, 3)
                    add_up(s, 2)
                    add_up(s, 3)
                    shift(s, 4)
                    shift(s, 5)
                    add_up(s, 4)
                    add_up(s, 5)
                    split_sums(s)
                    invert(s)
                    weights(s)
                    out_weights(s)
                    for ck in range(16):
                        for half in range(2):
                            lo_y(s, ck, half)
                        if ck % 2 == 1 and ck >= 3:
                            update(s, ck // 2 - 1)
                    update(s, 7)
                    dve.drain()


def macaron_kernel(nc, A, out, phases):
    with ExitStack() as ctx:
        def sb(name, shape, dt=F32):
            return ctx.enter_context(nc.sbuf_tensor(name, shape, dt))

        S = {"x": sb("x_all", [128, GROUPS, NB, D])}
        loads = []

        def load(name, shape, src, dt=F32):
            S[name] = sb(name, shape, dt)
            loads.append((S[name], src))

        load("wqkv", [128, QKV], A["wqkvT"])
        load("wproj", [128, D], A["wprojT"])
        load("wrouter", [128, EXPERTS], A["wrouterT"])
        load("moe1", [128, EXPERTS * EXP_F], A["moe1"])
        load("moe2", [128, CHUNKS * D], A["moe2"])
        load("columns", [128, 6], A["columns"])
        load("ident", [128, 128], A["ident"])
        load("expert_ids", [128, EXPERTS], A["expert_ids"])
        for i, n in enumerate(("lnw1", "lnb1", "lnw2", "lnb2")):
            S[n] = S["columns"][:, i:i + 1]
        S["minus_half"], S["epsilon"] = sb("minus_half", [128, GROUPS]), sb("epsilon", [128, GROUPS])
        s_load = ctx.enter_context(nc.semaphore("loaded"))
        s_store = ctx.enter_context(nc.semaphore("stored"))
        s_const = ctx.enter_context(nc.semaphore("constants"))
        load_second_half(nc, ctx, A, S, load)
        load_attention(nc, ctx, A, S, load)
        S["lnw_rnn"], S["lnb_rnn"] = S["columns"][:, 4:5], S["columns"][:, 5:6]
        with nc.Block() as block:
            @block.sync
            def _(sp):
                for s in range(NB):
                    sp.dma_start(S["x"][:, :, s, :], A["x"][s].rearrange("(g p) d -> p g d", p=128)).then_inc(s_load, 16)
                for dst, src in loads:
                    sp.dma_start(dst[tuple(slice(None) for _ in dst.shape)], src).then_inc(s_load, 16)
                sp.wait_ge(s_load, 16 * (NB + len(loads)))

            @block.vector
            def _(dve):
                dve.memset(S["minus_half"][:, :], -0.5)
                dve.memset(S["epsilon"][:, :], EPS).then_inc(s_const, 1)

        for i, ph in enumerate(phases):
            if ph == "ffn":
                causal_moe_ffn(nc, S, f"f{i}")
            if ph == "attn":
                hierarchical_attention(nc, A, S, f"h{i}")
            if ph == "second":
                binarize(nc, S)
                second_half(nc, S, "r")
        with nc.Block() as block:
            @block.sync
            def _(sp):
                for s in range(NB):
                    sp.dma_start(out[s].rearrange("(g p) d -> p g d", p=128), S["x"][:, :, s, :]).then_inc(s_store, 16)
                sp.wait_ge(s_store, 16 * NB)


PHASES = ("ffn", "attn", "ffn", "second")


def layouts(inputs):
    import numpy as np
    f = lambda n: np.asarray(inputs[n])
    kv = slice(0, 0)
    q = f("L0_ffn_qkv_weight")
    nq, nk = HEADS0 * HD0, KV_HEADS0 * HD0
    rep = HEADS0 // KV_HEADS0
    per_head = lambda w: np.repeat(w.reshape(KV_HEADS0, 1, HD0, D), rep, axis=1).reshape(HEADS0 * HD0, D)
    wq = np.concatenate([q[:nq], per_head(q[nq:nq + nk]), per_head(q[nq + nk:])], 0)
    cols = np.zeros((128, 6), np.float32)
    for i, n in enumerate(("L0_ffn_ln1_weight", "L0_ffn_ln1_bias", "L0_ffn_ln2_weight", "L0_ffn_ln2_bias",
                           "L1_attn_ln_w", "L1_attn_ln_b")):
        cols[:, i] = f(n)
    a = {
        "x": f("L0_attn_x"),
        "wqkvT": wq.T, "wprojT": f("L0_ffn_proj_weight").T, "wrouterT": f("L0_ffn_router_weight").T,
        "moe1": f("L0_ffn_moe_w1").transpose(1, 0, 2).reshape(D, EXPERTS * EXP_F),
        "moe2": f("L0_ffn_moe_w2").reshape(CHUNKS, 128, D).transpose(1, 0, 2).reshape(128, CHUNKS * D),
        "columns": cols,
        "ident": np.eye(128, dtype=np.float32),
        "expert_ids": np.tile(np.arange(EXPERTS, dtype=np.float32), (128, 1)),
    }
    a.update(layouts_second_half(f))
    a.update(attention_layouts(f))
    return {k: np.ascontiguousarray(v) for k, v in a.items()}


def kernel(phases=PHASES, **inputs):
    import concourse.bacc as bacc
    from concourse.bass_utils import run_bass_kernel_spmd

    arrays = layouts(inputs)
    nc = bacc.Bacc("TRN2", target_bir_lowering=False, num_devices=1)
    aps = {k: nc.dram_tensor(f"in_{k}", v.shape, mybir.dt.from_np(v.dtype), kind="ExternalInput").ap()
           for k, v in arrays.items()}
    out = nc.dram_tensor("out", (NB, SEQ, D), F32, kind="ExternalOutput").ap()
    macaron_kernel(nc, aps, out, phases)
    r = run_bass_kernel_spmd(nc, [{f"in_{k}": v for k, v in arrays.items()}], core_ids=[0])
    return r.results[0]["out"]
```

```python
import concourse.bass as bass
from concourse import mybir
from contextlib import ExitStack

F32 = mybir.dt.float32
F16 = mybir.dt.float16
U32 = mybir.dt.uint32
ALU = mybir.AluOpType
ACT = mybir.ActivationFunctionType
AX = mybir.AxisListType

NB, SEQ, D = 4, 1024, 128
GROUPS = SEQ // 128
EPS = 1e-5
MASKED = -1e30
ONE = 1
HEADS0, KV_HEADS0 = 16, 4
HD0 = D // HEADS0
QKV = 3 * D
PAIRS = NB * (NB + 1) // 2
EXPERTS, EXP_F, TOP_K = 8, 256, 2
CHUNKS = EXPERTS * EXP_F // 128
H_RING, UP_RING = 8, 3
FC = 4
STATE = 32


def causal_moe_ffn(nc, S, tag, s_weights, weights_loaded):
    x = S["x"]
    ident, lnw1, lnb1, lnw2, lnb2 = S["ident"], S["lnw1"], S["lnb1"], S["lnw2"], S["lnb2"]
    wqkv, wproj, wrouter, w1, w2 = S["wqkv"], S["wproj"], S["wrouter"], S["moe1"], S["moe2"]
    minus_half, epsilon, expert_ids = S["minus_half"], S["epsilon"], S["expert_ids"]
    with ExitStack() as ctx:
        def sb(name, shape, dt=F32):
            return ctx.enter_context(nc.sbuf_tensor(f"{tag}_{name}", shape, dt))

        def bank(name):
            return ctx.enter_context(nc.psum_tensor(f"{tag}_{name}", [128, 512], F32))

        sems = []

        def sem(name):
            sems.append(ctx.enter_context(nc.semaphore(f"{tag}_{name}")))
            return sems[-1]

        stats, mv = sb("stats", [128, NB, 6]), sb("mv", [128, NB, 2])
        stats2, mv2 = sb("stats2", [128, NB, 6]), sb("mv2", [128, NB, 2])
        roots, roots2 = sb("roots", [128, 5, NB]), sb("roots2", [128, 2, NB])
        hs = [sb(f"hs{i}", [128, NB, D]) for i in range(2)]
        xn1, xn2 = sb("xn1", [128, NB, D]), sb("xn2", [128, NB, D])
        ln1T, headsT = sb("ln1T", [128, NB * 128]), sb("headsT", [128, NB * 128])
        qkv = sb("qkv", [128, NB, QKV])
        pairs = sb("pairs", [128, PAIRS, D])
        pvs = sb("pvs", [128, PAIRS, D])
        scores = sb("scores", [128, NB, HEADS0, NB])
        shifted = sb("shifted", [128, NB, HEADS0, NB])
        probs = sb("probs", [128, NB, HEADS0, NB])
        small = sb("small", [128, 3, NB, HEADS0])
        after = sb("after", [128, NB, D])
        x2T = [sb(f"x2T{i}", [128, NB * 128]) for i in range(2)]
        shifted_g, gate = sb("shifted_g", [128, NB, EXPERTS]), sb("gate", [128, NB, EXPERTS])
        gsmall = sb("gsmall", [128, 3, NB])
        top, topf = sb("top", [128, NB, 8]), sb("topf", [128, NB, 8])
        topi = sb("topi", [128, NB, 8], U32)
        pick = sb("pick", [128, NB, TOP_K, EXPERTS])
        weight = [sb(f"weight{i}", [128, NB, EXPERTS]) for i in range(2)]
        hT = [sb(f"hT{i}", [128, NB * 128]) for i in range(H_RING)]

        up = [bank(f"up{i}") for i in range(UP_RING)]
        down = [bank(f"down{i}") for i in range(2)]
        qb = [bank(f"qkvb{i}") for i in range(2)]
        turn = bank("turn")

        s_stats, s_root = sem("stats_done"), sem("root_done")
        s_stats2, s_root2 = sem("stats2_done"), sem("root2_done")
        s_xn1, s_turn1, s_ln1T = sem("xn1_done"), sem("turned1"), sem("ln1T_done")
        s_q, s_qkv = sem("qkv_product"), sem("qkv_in_sbuf")
        s_pairs, s_shift, s_exp, s_heads = sem("pairs"), sem("scores_shifted"), sem("scores_exp"), sem("heads_done")
        s_turn2, s_headsT, s_proj = sem("turned2"), sem("headsT_done"), sem("proj_done")
        s_xn2, s_turn3, s_x2T = sem("xn2_done"), sem("turned3"), sem("x2T_done")
        s_logit, s_gshift, s_gexp = sem("logits_done"), sem("logits_shifted"), sem("logits_exp")
        s_up, s_h, s_down, s_add = sem("up_done"), sem("h_done"), sem("down_done"), sem("add_done")

        first = [sum(NB - u for u in range(t)) for t in range(NB)]

        def grp(t, g):
            return t[:, bass.ds(g, 1), :, :].rearrange("p a s d -> p (a s) d")

        with nc.Block() as block:
            @block.sync
            def _(sp):
                for s in sems:
                    sp.sem_inc(s, ONE)

            @block.gpsimd
            def _(pool):
                def power(out, in_):
                    pool.tensor_tensor(out, in_, minus_half[:, 0:NB], ALU.pow)
                    pool.drain()

                def a1(g):
                    pool.wait_ge(s_stats, ONE + g + 1)
                    pool.wait_ge(s_xn1, ONE + g)
                    var = mv[:, :, 1]
                    pool.tensor_tensor(roots[:, 0, :], var, epsilon[:, 0:NB], ALU.add)
                    pool.drain()
                    power(roots[:, 1, :], roots[:, 0, :])
                    pool.tensor_tensor(roots[:, 2, :], roots[:, 1, :], roots[:, 1, :], ALU.mult)
                    pool.drain()
                    pool.tensor_tensor(roots[:, 0, :], roots[:, 2, :], var, ALU.mult)
                    pool.drain()
                    pool.tensor_scalar(roots[:, 2, :], roots[:, 0, :], EPS, None, ALU.add)
                    pool.drain()
                    power(roots[:, 3, :], roots[:, 2, :])
                    pool.tensor_tensor(roots[:, 4, :], roots[:, 3, :], roots[:, 1, :], ALU.mult).then_inc(s_root, 1)

                def a2(g):
                    pool.wait_ge(s_stats2, ONE + g + 1)
                    pool.wait_ge(s_xn2, ONE + g)
                    pool.tensor_tensor(roots2[:, 0, :], mv2[:, :, 1], epsilon[:, 0:NB], ALU.add)
                    pool.drain()
                    pool.tensor_tensor(roots2[:, 1, :], roots2[:, 0, :], minus_half[:, 0:NB],
                                       ALU.pow).then_inc(s_root2, 1)

                def query_key(g):
                    pool.wait_ge(s_qkv, ONE + NB * (g + 1))
                    pool.wait_ge(s_shift, ONE + g)
                    for t in range(NB):
                        n = NB - t
                        last = pool.tensor_tensor(pairs[:, first[t]:first[t] + n, :], qkv[:, t:NB, 0:D],
                                                  qkv[:, t, D:2 * D].unsqueeze(1).broadcast_to([128, n, D]), ALU.mult)
                    last.then_inc(s_pairs, 1)

                a1(0)
                query_key(0)
                with pool.Fori(0, GROUPS - 1) as g:
                    a1(g + 1)
                    a2(g)
                    query_key(g + 1)
                a2(GROUPS - 1)

            @block.scalar
            def _(act):
                def a_ln1T(g):
                    act.wait_ge(s_turn1, ONE + g + 1)
                    act.wait_ge(s_q, ONE + NB * g)
                    nc.scalar.activation(ln1T[:, :], qb[1][:, :], ACT.Identity, bias=lnb1[:, :],
                                         scale=lnw1[:, :]).then_inc(s_ln1T, 1)

                def a_qkv(g):
                    act.wait_ge(s_heads, ONE + g)
                    for s in range(NB):
                        act.wait_ge(s_q, ONE + NB * g + s + 1)
                        nc.scalar.activation(qkv[:, s, :], qb[s % 2][:, 0:QKV], ACT.Copy).then_inc(s_qkv, 1)

                def a_exp(g):
                    act.wait_ge(s_shift, ONE + g + 1)
                    nc.scalar.activation(probs[:, :, :, :], shifted[:, :, :, :], ACT.Exp,
                                         scale=HD0 ** -0.5).then_inc(s_exp, 1)

                def a_headsT(g):
                    act.wait_ge(s_turn2, ONE + g + 1)
                    act.wait_ge(s_proj, ONE + g)
                    nc.scalar.activation(headsT[:, :], turn[:, :], ACT.Copy).then_inc(s_headsT, 1)

                def a_x2T(g, b):
                    act.wait_ge(s_turn3, ONE + g + 1)
                    nc.scalar.activation(x2T[b][:, :], turn[:, :], ACT.Identity, bias=lnb2[:, :],
                                         scale=lnw2[:, :]).then_inc(s_x2T, 1)

                def a_gexp(g):
                    act.wait_ge(s_gshift, ONE + g + 1)
                    nc.scalar.activation(gate[:, :, :], shifted_g[:, :, :], ACT.Exp).then_inc(s_gexp, 1)

                def gelu(g, c):
                    act.wait_ge(s_up, ONE + CHUNKS * g + c + 1)
                    act.wait_ge(s_down, ONE + EXPERTS * g + (max(c - H_RING, -2)) // 2 + 1)
                    nc.scalar.activation(hT[c % H_RING][:, :], up[c % UP_RING][:, :],
                                         ACT.Gelu_apprx_tanh).then_inc(s_h, 1)

                def between(g, b, c, front, back):
                    if c == 7 and back:
                        a_headsT(g + 1)
                    if c == 9 and front:
                        a_ln1T(g + 2)
                    if c == 11 and front:
                        a_qkv(g + 2)
                    if c == 13 and back:
                        a_x2T(g + 1, 1 - b)
                    if c == 15 and front:
                        a_exp(g + 2)
                    if c == 15 and back:
                        a_gexp(g + 1)

                def group(g, b, front, back):
                    for c in range(CHUNKS):
                        gelu(g, c)
                        between(g, b, c, front, back)

                a_ln1T(0)
                a_qkv(0)
                a_exp(0)
                for c in range(CHUNKS):
                    between(-1, 1, c, True, True)
                with act.Fori(0, GROUPS // 2 - 1) as i:
                    group(2 * i, 0, True, True)
                    group(2 * i + 1, 1, True, True)
                group(GROUPS - 2, 0, False, True)
                group(GROUPS - 1, 1, False, False)

            @block.tensor
            def _(pe):
                def turn_tiles(src, signal, bank=turn):
                    for s in range(NB):
                        last = nc.tensor.transpose(bank[:, s * 128:(s + 1) * 128], src[:, s, :], ident[:, :])
                    last.then_inc(signal, 1)

                def p_turn1(g):
                    pe.wait_ge(s_xn1, ONE + g + 1)
                    pe.wait_ge(s_qkv, ONE + NB * g)
                    turn_tiles(xn1, s_turn1, qb[1])

                def p_qkv(g):
                    pe.wait_ge(s_ln1T, ONE + g + 1)
                    for s in range(NB):
                        pe.wait_ge(s_qkv, ONE + NB * g + max(s - 1, 0))
                        nc.tensor.matmul(qb[s % 2][:, 0:QKV], ln1T[:, s * 128:(s + 1) * 128], wqkv[:, :],
                                         start=True, stop=True).then_inc(s_q, 1)

                def p_turn2(g):
                    pe.wait_ge(s_heads, ONE + g + 1)
                    pe.wait_ge(s_gshift, ONE + g)
                    turn_tiles(pvs[:, 0:NB, :], s_turn2)

                def p_proj(g):
                    pe.wait_ge(s_headsT, ONE + g + 1)
                    for s in range(NB):
                        last = nc.tensor.matmul(turn[:, s * 128:(s + 1) * 128], headsT[:, s * 128:(s + 1) * 128],
                                                wproj[:, :], start=True, stop=True)
                    last.then_inc(s_proj, 1)

                def p_turn3(g):
                    pe.wait_ge(s_xn2, ONE + g + 1)
                    turn_tiles(xn2, s_turn3)

                def p_router(g, b):
                    pe.wait_ge(s_x2T, ONE + g + 1)
                    for s in range(NB):
                        last = nc.tensor.matmul(turn[:, s * EXPERTS:(s + 1) * EXPERTS],
                                                x2T[b][:, s * 128:(s + 1) * 128], wrouter[:, :],
                                                start=True, stop=True)
                    last.then_inc(s_logit, 1)

                def up_products(g, b, e):
                    for c in (2 * e, 2 * e + 1):
                        pe.wait_ge(s_h, ONE + CHUNKS * g + max(c - UP_RING + 1, 0))
                        nc.tensor.matmul(up[c % UP_RING][:, :], w1[:, c * 128:(c + 1) * 128], x2T[b][:, :],
                                         start=True, stop=True).then_inc(s_up, 1)

                def down_products(g, e):
                    pe.wait_ge(s_h, ONE + CHUNKS * g + 2 * e + 2)
                    pe.wait_ge(s_add, ONE + EXPERTS * g + max(e - 1, 0))
                    for s in range(NB):
                        for c in (2 * e, 2 * e + 1):
                            last = nc.tensor.matmul(down[e % 2][:, s * 128:(s + 1) * 128],
                                                    hT[c % H_RING][:, s * 128:(s + 1) * 128],
                                                    w2[:, c * 128:(c + 1) * 128],
                                                    start=(c % 2 == 0), stop=(c % 2 == 1))
                    last.then_inc(s_down, 1)

                def between(g, b, e, front, back):
                    if e == 2 and back:
                        p_turn2(g + 1)
                    if e == 3 and back:
                        p_proj(g + 1)
                    if e == 3 and front:
                        p_turn1(g + 2)
                    if e == 4 and front:
                        p_qkv(g + 2)
                    if e == 5 and back:
                        p_turn3(g + 1)
                    if e == 6 and back:
                        p_router(g + 1, 1 - b)

                def group(g, b, front, back):
                    up_products(g, b, 0)
                    for e in range(EXPERTS):
                        if e + 1 < EXPERTS:
                            up_products(g, b, e + 1)
                        down_products(g, e)
                        between(g, b, e, front, back)

                p_turn1(0)
                p_qkv(0)
                pe.wait_ge(s_weights, weights_loaded)
                for e in range(EXPERTS):
                    between(-1, 1, e, True, True)
                with pe.Fori(0, GROUPS // 2 - 1) as i:
                    group(2 * i, 0, True, True)
                    group(2 * i + 1, 1, True, True)
                group(GROUPS - 2, 0, False, True)
                group(GROUPS - 1, 1, False, False)

            @block.vector
            def _(dve):
                def v_stats(g):
                    xg = grp(x, g)
                    for s in range(NB):
                        dve.bn_stats(stats[:, s, :], xg[:, s, :])
                    dve.drain()
                    for s in range(NB):
                        last = dve.bn_aggr(mv[:, s, :], stats[:, s, :])
                    last.then_inc(s_stats, 1)

                def v_norm1(g, b):
                    dve.wait_ge(s_root, ONE + g + 1)
                    dve.wait_ge(s_turn1, ONE + g)
                    xg = grp(x, g)
                    for s in range(NB):
                        dve.tensor_scalar(hs[b][:, s, :], xg[:, s, :], mv[:, s, 0:1], roots[:, 1, s:s + 1],
                                          ALU.subtract, ALU.mult)
                    for s in range(NB):
                        last = dve.tensor_scalar(xn1[:, s, :], xg[:, s, :], mv[:, s, 0:1], roots[:, 4, s:s + 1],
                                                 ALU.subtract, ALU.mult)
                    last.then_inc(s_xn1, 1)

                def v_scores(g):
                    dve.drain()
                    dve.wait_ge(s_pairs, ONE + g + 1)
                    for t in range(NB):
                        n = NB - t
                        dve.tensor_reduce(scores[:, t:NB, :, t],
                                          pairs[:, first[t]:first[t] + n, :].rearrange("p s (h d) -> p s h d", d=HD0),
                                          AX.X, ALU.add)

                def v_shift(g):
                    dve.drain()
                    dve.tensor_reduce(small[:, 0, :, :], scores[:, :, :, :], AX.X, ALU.max)
                    dve.drain()
                    dve.tensor_tensor(shifted[:, :, :, :], scores[:, :, :, :],
                                      small[:, 0, :, :].unsqueeze(3).broadcast_to([128, NB, HEADS0, NB]),
                                      ALU.subtract).then_inc(s_shift, 1)

                def v_values(g):
                    dve.wait_ge(s_exp, ONE + g + 1)
                    dve.wait_ge(s_turn2, ONE + g)
                    dve.tensor_reduce(small[:, 1, :, :], probs[:, :, :, :], AX.X, ALU.add)
                    dve.drain()
                    dve.reciprocal(small[:, 2, :, :], small[:, 1, :, :])
                    v_products(g, 0)

                def v_products(g, t):
                    for s in range(t, NB):
                        dve.tensor_tensor(
                            pvs[:, first[t] + s - t, :].rearrange("p (h d) -> p h d", d=HD0),
                            probs[:, s, :, t].unsqueeze(2).broadcast_to([128, HEADS0, HD0]),
                            qkv[:, t, 2 * D:3 * D].rearrange("p (h d) -> p h d", d=HD0), ALU.mult)

                def v_heads(g):
                    for t in range(1, NB):
                        v_products(g, t)
                    dve.drain()
                    for t in range(1, NB):
                        n = NB - t
                        dve.tensor_tensor(pvs[:, t:NB, :], pvs[:, t:NB, :], pvs[:, first[t]:first[t] + n, :], ALU.add)
                        dve.drain()
                    out = pvs[:, 0:NB, :].rearrange("p s (h d) -> p (s h) d", d=HD0)
                    dve.tensor_tensor(out, out,
                                      small[:, 2, :, :].rearrange("p s h -> p (s h)").unsqueeze(2)
                                      .broadcast_to([128, NB * HEADS0, HD0]), ALU.mult).then_inc(s_heads, 1)

                def v_after(g, b):
                    dve.wait_ge(s_proj, ONE + g + 1)
                    dve.tensor_tensor(after[:, :, :], turn[:, :].rearrange("p (s d) -> p s d", d=D),
                                      hs[b][:, :, :], ALU.add)
                    dve.drain()
                    for s in range(NB):
                        dve.bn_stats(stats2[:, s, :], after[:, s, :])
                    dve.drain()
                    for s in range(NB):
                        last = dve.bn_aggr(mv2[:, s, :], stats2[:, s, :])
                    last.then_inc(s_stats2, 1)

                def v_norm2(g):
                    dve.wait_ge(s_root2, ONE + g + 1)
                    dve.wait_ge(s_turn3, ONE + g)
                    for s in range(NB):
                        last = dve.tensor_scalar(xn2[:, s, :], after[:, s, :], mv2[:, s, 0:1],
                                                 roots2[:, 1, s:s + 1], ALU.subtract, ALU.mult)
                    last.then_inc(s_xn2, 1)

                def v_logits(g):
                    dve.wait_ge(s_logit, ONE + g + 1)
                    logits = turn[:, 0:NB * EXPERTS].rearrange("p (s e) -> p s e", e=EXPERTS)
                    dve.tensor_reduce(gsmall[:, 0, :], logits, AX.X, ALU.max)
                    dve.drain()
                    dve.tensor_tensor(shifted_g[:, :, :], logits,
                                      gsmall[:, 0, :].unsqueeze(2).broadcast_to([128, NB, EXPERTS]),
                                      ALU.subtract).then_inc(s_gshift, 1)

                def v_weights(g, b):
                    dve.wait_ge(s_gexp, ONE + g + 1)
                    dve.tensor_reduce(gsmall[:, 1, :], gate[:, :, :], AX.X, ALU.add)
                    dve.drain()
                    dve.reciprocal(gsmall[:, 2, :], gsmall[:, 1, :])
                    dve.drain()
                    dve.scalar_tensor_tensor(gate[:, :, :], gate[:, :, :], 0.5,
                                             gsmall[:, 2, :].unsqueeze(2).broadcast_to([128, NB, EXPERTS]),
                                             ALU.mult, ALU.mult)
                    dve.drain()
                    for s in range(NB):
                        dve.max(top[:, s, :], gate[:, s, :])
                    dve.drain()
                    for s in range(NB):
                        dve.max_index(topi[:, s, :], top[:, s, :], gate[:, s, :])
                    dve.drain()
                    dve.tensor_copy(topf[:, :, :], topi[:, :, :])
                    dve.drain()
                    ids = expert_ids[:, :].unsqueeze(1).unsqueeze(1).broadcast_to([128, NB, TOP_K, EXPERTS])
                    best = lambda t: t[:, :, 0:TOP_K].unsqueeze(3).broadcast_to([128, NB, TOP_K, EXPERTS])
                    dve.tensor_tensor(pick[:, :, :, :], ids, best(topf), ALU.is_equal)
                    dve.drain()
                    dve.tensor_tensor(pick[:, :, :, :], pick[:, :, :, :], best(top), ALU.mult)
                    dve.drain()
                    dve.tensor_tensor(weight[b][:, :, :], pick[:, :, 0, :], pick[:, :, 1, :], ALU.add)
                    dve.drain()

                def add_expert(g, b, e):
                    dve.wait_ge(s_down, ONE + EXPERTS * g + e + 1)
                    dve.wait_ge(s_add, ONE + EXPERTS * g + e)
                    xg = grp(x, g)
                    for s in range(NB):
                        last = dve.scalar_tensor_tensor(xg[:, s, :], down[e % 2][:, s * 128:(s + 1) * 128],
                                                        weight[b][:, s, e:e + 1], xg[:, s, :],
                                                        ALU.mult, ALU.add)
                    last.then_inc(s_add, 1)

                def residual(g):
                    xg = grp(x, g)
                    dve.scalar_tensor_tensor(xg, after[:, :, :], 0.5, xg, ALU.mult, ALU.add)
                    dve.drain()

                def between(g, b, e, front, back):
                    if e == 0 and back:
                        v_values(g + 1)
                    if e == 1 and back:
                        v_heads(g + 1)
                    if e == 2 and front:
                        v_norm1(g + 2, b)
                    if e == 3 and back:
                        v_after(g + 1, 1 - b)
                    if e == 4 and back:
                        v_norm2(g + 1)
                        residual(g + 1)
                    if e == 5 and front:
                        v_scores(g + 2)
                    if e == 6 and front:
                        v_shift(g + 2)
                    if e == 6 and back:
                        v_logits(g + 1)
                    if e == 7 and back:
                        v_weights(g + 1, 1 - b)

                def group(g, b, front, back):
                    if front:
                        v_stats(g + 2)
                    for e in range(EXPERTS):
                        add_expert(g, b, e)
                        between(g, b, e, front, back)

                dve.memset(scores[:, :, :, :], MASKED)
                dve.drain()
                v_stats(0)
                v_norm1(0, 0)
                v_scores(0)
                v_shift(0)
                dve.wait_ge(s_weights, weights_loaded)
                v_stats(1)
                for e in range(EXPERTS):
                    between(-1, 1, e, True, True)
                with dve.Fori(0, GROUPS // 2 - 1) as i:
                    group(2 * i, 0, True, True)
                    group(2 * i + 1, 1, True, True)
                group(GROUPS - 2, 0, False, True)
                group(GROUPS - 1, 1, False, False)
def load_second_half(nc, ctx, A, S, load):
    load("bin1", [128, FC * D], A["bin1"])
    load("bin2", [128, FC * 128], A["bin2"])
    load("rnnA", [128, STATE], A["rnnA"])
    load("rnnB", [D, STATE], A["rnnB"])
    load("rnnC", [STATE, D], A["rnnC"])
    load("rnnD", [128, D], A["rnnD"])
    load("mlp1", [128, FC * 128], A["mlp1"])
    load("mlp2", [128, FC * D], A["mlp2"])
    load("chunk_bias", [128, 2 * FC], A["chunk_bias"])
    load("rows", [128, 4, D], A["rows"].partition_broadcast(128))


def layouts_second_half(f):
    import numpy as np
    chunks_first = lambda w: w.reshape(FC, 128, -1).transpose(1, 0, 2).reshape(128, -1)
    return {
        "bin1": chunks_first(f("L1_ffn_w1")), "bin2": f("L1_ffn_w2"),
        "rnnA": np.pad(f("L1_attn_A").T, ((0, 128 - STATE), (0, 0))), "rnnB": f("L1_attn_Bm").T, "rnnC": f("L1_attn_C").T,
        "rnnD": f("L1_attn_D").T,
        "mlp1": f("L1_attn_W1").T, "mlp2": chunks_first(f("L1_attn_W2").T),
        "chunk_bias": np.concatenate([f("L1_ffn_b1").reshape(FC, 128).T, f("L1_attn_b1").reshape(FC, 128).T], 1),
        "rows": np.stack([f("L1_attn_ln_w"), f("L1_attn_ln_b"), f("L1_attn_b2"), f("L1_ffn_b2")]),
    }


def binarize(nc, S):
    with ExitStack() as ctx:
        sgn = ctx.enter_context(nc.sbuf_tensor("sgn", [128, 2, FC, 128], F32))
        alpha = ctx.enter_context(nc.sbuf_tensor("alpha", [128, FC + 1], F32))
        banks = [ctx.enter_context(nc.psum_tensor(f"bin_turn{i}", [128, 512], F32)) for i in range(2)]
        s_sign, s_bin, s_turn = (ctx.enter_context(nc.semaphore(n)) for n in ("signs", "binarised", "bin_turned"))
        w1 = S["bin1"][:, :].rearrange("p (c d) -> p c d", d=D)
        w2 = S["bin2"][:, :].rearrange("p (c h) -> p c h", h=128)
        with nc.Block() as block:
            @block.scalar
            def _(act):
                for i, w in enumerate((w1, w2)):
                    nc.scalar.activation(sgn[:, i, :, :], w, ACT.Sign).then_inc(s_sign, 1)

            @block.vector
            def _(dve):
                dve.tensor_reduce(alpha[:, 0:FC], w1, AX.X, ALU.add, apply_absolute_value=True)
                dve.tensor_reduce(alpha[:, FC:FC + 1], w2, AX.XY, ALU.add, apply_absolute_value=True)
                dve.drain()
                dve.tensor_scalar(alpha[:, 0:FC], alpha[:, 0:FC], 1.0 / D, None, ALU.mult)
                dve.tensor_scalar(alpha[:, FC:FC + 1], alpha[:, FC:FC + 1], 1.0 / (FC * 128), None, ALU.mult)
                dve.drain()
                dve.wait_ge(s_sign, 2)
                for i, w in enumerate((w1, w2)):
                    for c in range(FC):
                        a = alpha[:, c:c + 1] if i == 0 else alpha[:, FC:FC + 1]
                        dve.scalar_tensor_tensor(sgn[:, i, c, :], sgn[:, i, c, :], a, w[:, c, :],
                                                 ALU.mult, ALU.subtract)
                dve.drain()
                for i, w in enumerate((w1, w2)):
                    dve.tensor_tensor(sgn[:, i, :, :], sgn[:, i, :, :], w, ALU.add).then_inc(s_bin, 1)
                rows = S["rows"]
                dve.tensor_tensor(rows[:, 1, :], rows[:, 1, :], rows[:, 2, :], ALU.add)
                dve.tensor_scalar(rows[:, 3, :], rows[:, 3, :], 0.5, None, ALU.mult)
                for i, n in enumerate(("bin1", "bin2")):
                    dve.wait_ge(s_turn, i + 1)
                    dve.tensor_copy(S[n][:, :], banks[i][:, :])

            @block.tensor
            def _(pe):
                for i in range(2):
                    pe.wait_ge(s_bin, i + 1)
                    for c in range(FC):
                        last = nc.tensor.transpose(banks[i][:, c * 128:(c + 1) * 128], sgn[:, i, c, :],
                                                   S["ident"][:, :])
                    last.then_inc(s_turn, 1)


def second_half(nc, S, tag):
    x = S["x"]
    ident, rows, bias = S["ident"], S["rows"], S["chunk_bias"]
    rnnA, rnnB, rnnC, rnnD = S["rnnA"], S["rnnB"], S["rnnC"], S["rnnD"]
    minus_half = S["minus_half"]
    with ExitStack() as ctx:
        def sb(name, shape, dt=F32):
            return ctx.enter_context(nc.sbuf_tensor(f"{tag}_{name}", shape, dt))

        def bank(name):
            return ctx.enter_context(nc.psum_tensor(f"{tag}_{name}", [128, 512], F32))

        sems = []

        def sem(name):
            sems.append(ctx.enter_context(nc.semaphore(f"{tag}_{name}")))
            return sems[-1]

        NORMS = ("a", "p", "r", "z")
        FFNS = ("a", "r", "z")
        stats = {k: sb(f"stats_{k}", [128, NB, 6]) for k in NORMS}
        mv = {k: sb(f"mv_{k}", [128, NB, 2]) for k in NORMS}
        root = {k: sb(f"root_{k}", [128, 2, NB]) for k in NORMS}
        xn = {k: [sb(f"xn_{k}", [128, NB, D])] * 2 for k in ("a", "r", "z")}
        xn["p"] = [sb(f"xn_p{i}", [128, NB, D]) for i in range(2)]
        nT = {k: [sb(f"nT_{k}", [128, 512])] * 2 for k in ("a", "r", "z")}
        nT["p"] = [sb(f"nT_p{i}", [128, 512]) for i in range(2)]
        state = [sb(f"state{i}", [128, 512]) for i in range(2)]
        mixed = sb("mixed", [128, NB, D])
        resid = sb("resid", [128, NB, D])
        h_pre = [sb(f"h_pre{c}", [128, 512]) for c in range(FC)]
        h_post = [sb(f"h_post{c}", [128, 512]) for c in range(FC)]
        H = {"a": h_pre, "r": h_post, "z": h_post}
        scan = [bank(f"scan{i}") for i in range(2)]
        pre_misc, post_misc = bank("pre_misc"), bank("post_misc")
        up_pre, up_post = [bank(f"up_pre{i}") for i in range(2)], [bank(f"up_post{i}") for i in range(2)]
        MISC = {"a": pre_misc, "p": pre_misc, "r": post_misc, "z": post_misc}
        UP = {"a": up_pre, "r": up_post, "z": up_post + up_pre}
        W1 = {"a": S["bin1"], "r": S["mlp1"], "z": S["bin1"]}
        W2 = {"a": S["bin2"], "r": S["mlp2"], "z": S["bin2"]}
        BIAS = {"a": 0, "r": FC, "z": 0}

        s_stats = {k: sem(f"stats_{k}") for k in NORMS}
        s_root = {k: sem(f"root_{k}") for k in NORMS}
        s_xn = {k: sem(f"xn_{k}") for k in NORMS}
        s_turn = {k: sem(f"turned_{k}") for k in NORMS}
        s_nT = {k: sem(f"nT_{k}") for k in NORMS}
        s_up = {k: sem(f"up_{k}") for k in FFNS}
        s_h = {k: sem(f"h_{k}") for k in FFNS}
        s_down = {k: sem(f"down_{k}") for k in FFNS}
        s_x = {k: sem(f"x_{k}") for k in FFNS}
        s_step, s_tanh, s_out, s_zero = sem("step_product"), sem("tanh_done"), sem("mixed_product"), sem("zero_state")

        def grp(g):
            return x[:, bass.ds(g, 1), :, :].rearrange("p a s d -> p (a s) d")

        with nc.Block() as block:
            @block.sync
            def _(sp):
                for s in sems:
                    sp.sem_inc(s, ONE)

            @block.gpsimd
            def _(pool):
                def rsqrt(k, g):
                    pool.wait_ge(s_stats[k], ONE + g + 1)
                    pool.wait_ge(s_xn[k], ONE + g)
                    pool.tensor_tensor(root[k][:, 0, :], mv[k][:, :, 1], S["epsilon"][:, 0:NB], ALU.add)
                    pool.drain()
                    pool.tensor_tensor(root[k][:, 1, :], root[k][:, 0, :], minus_half[:, 0:NB],
                                       ALU.pow).then_inc(s_root[k], 1)

                def body(g, post, pre):
                    if pre:
                        rsqrt("a", g + 1)
                    if post:
                        rsqrt("r", g - 1)
                        rsqrt("z", g - 1)
                    if pre:
                        rsqrt("p", g + 1)

                body(-1, False, True)
                body(0, False, True)
                with pool.Fori(1, GROUPS - 1) as g:
                    body(g, True, True)
                body(GROUPS - 1, True, False)
                body(GROUPS, True, False)

            @block.vector
            def _(dve):
                def v_stats(k, src):
                    for s in range(NB):
                        dve.bn_stats(stats[k][:, s, :], src[:, s, :])
                    dve.drain()
                    for s in range(NB):
                        last = dve.bn_aggr(mv[k][:, s, :], stats[k][:, s, :])
                    last.then_inc(s_stats[k], 1)

                def v_norm(k, g, b, src):
                    dve.wait_ge(s_root[k], ONE + g + 1)
                    dve.wait_ge(s_turn[k], ONE + g)
                    for s in range(NB):
                        last = dve.tensor_scalar(xn[k][b][:, s, :], src[:, s, :], mv[k][:, s, 0:1],
                                                 root[k][:, 1, s:s + 1], ALU.subtract, ALU.mult)
                    last.then_inc(s_xn[k], 1)

                def v_nT(k, g, b):
                    dve.wait_ge(s_turn[k], ONE + g + 1)
                    if k == "p":
                        dve.tensor_copy(nT[k][b][:, :].rearrange("p (t s) -> p s t", s=NB),
                                        MISC[k][:, :].rearrange("p (s t) -> p s t", s=NB)).then_inc(s_nT[k], 1)
                        return
                    dve.wait_ge(s_up[k], ONE + FC * g)
                    if k == "r":
                        dve.tensor_scalar(nT[k][b][:, :], MISC[k][:, :], S["lnw_rnn"], S["lnb_rnn"],
                                          ALU.mult, ALU.add).then_inc(s_nT[k], 1)
                    else:
                        dve.tensor_copy(nT[k][b][:, :], MISC[k][:, :]).then_inc(s_nT[k], 1)

                def v_update_bin(k, g):
                    dve.wait_ge(s_down[k], ONE + g + 1)
                    dve.scalar_tensor_tensor(resid[:, :, :], MISC[k][:, :].rearrange("p (s d) -> p s d", d=D), 0.5,
                                             rows[:, 3, :].unsqueeze(1).broadcast_to([128, NB, D]), ALU.mult, ALU.add)
                    dve.drain()
                    dve.tensor_tensor(grp(g), grp(g), resid[:, :, :], ALU.add).then_inc(s_x[k], 1)
                    dve.drain()

                def v_mix(g, b):
                    dve.wait_ge(s_out, ONE + g + 1)
                    dve.tensor_tensor(mixed[:, :, :], post_misc[:, :].rearrange("p (s d) -> p s d", d=D),
                                      xn["p"][b][:, :, :], ALU.add)
                    dve.drain()
                    v_stats("r", mixed)

                def v_resid(g):
                    y = xn["r"][0]
                    dve.drain()
                    dve.tensor_tensor(resid[:, :, :], y[:, :, :],
                                      rows[:, 0, :].unsqueeze(1).broadcast_to([128, NB, D]), ALU.mult)
                    dve.drain()
                    dve.tensor_tensor(resid[:, :, :], resid[:, :, :],
                                      rows[:, 1, :].unsqueeze(1).broadcast_to([128, NB, D]), ALU.add)
                    dve.drain()
                    dve.tensor_tensor(grp(g), grp(g), resid[:, :, :], ALU.add)
                    dve.drain()

                def v_update_mlp(g):
                    dve.wait_ge(s_down["r"], ONE + g + 1)
                    dve.tensor_tensor(grp(g), post_misc[:, :].rearrange("p (s d) -> p s d", d=D), grp(g),
                                      ALU.add).then_inc(s_x["r"], 1)
                    dve.drain()

                def pre_first(g, b):
                    v_stats("a", grp(g))
                    v_norm("a", g, b, grp(g))

                def body(g, b, post, pre):
                    if pre:
                        pre_first(g + 1, 1 - b)
                        v_nT("a", g + 1, 1 - b)
                    if post:
                        v_mix(g - 1, 1 - b)
                        v_norm("r", g - 1, 1 - b, mixed)
                        v_nT("r", g - 1, 1 - b)
                        v_resid(g - 1)
                    if post:
                        v_update_mlp(g - 1)
                        v_stats("z", grp(g - 1))
                        v_norm("z", g - 1, 1 - b, grp(g - 1))
                        v_nT("z", g - 1, 1 - b)
                    if pre:
                        v_update_bin("a", g + 1)
                        v_stats("p", grp(g + 1))
                        v_norm("p", g + 1, 1 - b, grp(g + 1))
                        v_nT("p", g + 1, 1 - b)
                    if post:
                        v_update_bin("z", g - 1)

                for half in state:
                    last = dve.memset(half[:, :], 0.0)
                last.then_inc(s_zero, 1)
                body(-1, 1, False, True)
                body(0, 0, False, True)
                with dve.Fori(0, GROUPS // 2 - 1) as i:
                    body(2 * i + 1, 1, True, True)
                    body(2 * i + 2, 0, True, True)
                body(GROUPS - 1, 1, True, False)
                body(GROUPS, 0, True, False)

            def up_piece(pe, k, g, b, i, last_z=None, groups_a=None):
                c, s = divmod(i, NB)
                if s == 0:
                    pe.wait_ge(s_nT[k], ONE + g + 1)
                    if k == "a" and c < 2:
                        if last_z is not None:
                            pe.wait_ge(s_h["z"], ONE + FC * last_z)
                    elif k == "r" and c < 2:
                        pe.wait_ge(s_h["z"], ONE + FC * g)
                    elif k == "z" and c < 2:
                        pe.wait_ge(s_h["r"], ONE + FC * (g + 1))
                    elif k == "z":
                        pe.wait_ge(s_h["a"], ONE + FC * groups_a)
                    else:
                        pe.wait_ge(s_h[k], ONE + FC * g + c - 1)
                ins = nc.tensor.matmul(UP[k][c % len(UP[k])][:, s * 128:(s + 1) * 128], W1[k][:, c * 128:(c + 1) * 128],
                                       nT[k][b][:, s * 128:(s + 1) * 128], start=True, stop=True)
                if s == NB - 1:
                    ins.then_inc(s_up[k], 1)

            def down_piece(pe, k, g, i):
                s, c = divmod(i, FC)
                if i == 0:
                    pe.wait_ge(s_h[k], ONE + FC * (g + 1))
                ins = nc.tensor.matmul(MISC[k][:, s * 128:(s + 1) * 128], H[k][c][:, s * 128:(s + 1) * 128],
                                       W2[k][:, c * 128:(c + 1) * 128], start=(c == 0), stop=(c == FC - 1))
                if i == NB * FC - 1:
                    ins.then_inc(s_down[k], 1)

            def turn_piece(pe, k, g, b, s):
                if s == 0:
                    pe.wait_ge(s_xn[k], ONE + g + 1)
                    if k == "a":
                        pe.wait_ge(s_nT["p"], ONE + g)
                ins = nc.tensor.transpose(MISC[k][:, s * 128:(s + 1) * 128], xn[k][b][:, s, :], ident[:, :])
                if s == NB - 1:
                    ins.then_inc(s_turn[k], 1)

            def input_piece(pe, g, b, s):
                if s == 0:
                    pe.wait_ge(s_nT["p"], ONE + g + 1)
                part = slice(128 * s, 128 * (s + 1))
                nc.tensor.matmul(scan[b][0:STATE, part], rnnB[:, :], nT["p"][b][:, part], start=(s == 0), stop=False,
                                 skip_group_check=True)

            def mix_piece(pe, g, b, i):
                s, second = divmod(i, 2)
                if i == 0:
                    pe.wait_ge(s_tanh, ONE + 128 * (g + 1))
                    pe.wait_ge(s_x["z"], ONE + g)
                lhs = (nT["p"][b][:, :] if second else state[b][0:STATE, :]).rearrange("p (t s) -> p s t", s=NB)[:, s, :]
                ins = nc.tensor.matmul(post_misc[:, s * 128:(s + 1) * 128], lhs, (rnnD if second else rnnC)[:, :],
                                       start=not second, stop=bool(second))
                if i == 2 * NB - 1:
                    ins.then_inc(s_out, 1)

            UP_A = [6, 7, 8, 9, 18, 19, 22, 23]
            UP_R = [16, 17, 20, 21, 24, 25, 26, 27]
            DOWN_A = [38, 39, 40, 41, 42, 43, 44, 45]

            def plan_post(pe, g, b, groups_a):
                p = [(2 + i // 2, mix_piece, (pe, g, b, i)) for i in range(2 * NB)]
                p += [(12 + s // 2, turn_piece, (pe, "r", g, b, s)) for s in range(NB)]
                p += [(UP_R[i // 2], up_piece, (pe, "r", g, b, i)) for i in range(16)]
                p += [(30 + i // 2, down_piece, (pe, "r", g, i)) for i in range(16)]
                p += [(46 + s // 2, turn_piece, (pe, "z", g, b, s)) for s in range(NB)]
                p += [(50 + i // 2, up_piece, (pe, "z", g, b, i, None, groups_a)) for i in range(16)]
                p += [((60 if i < 4 else 62) + i // 2, down_piece, (pe, "z", g, i)) for i in range(16)]
                return p

            def plan_pre(pe, g, b, last_z):
                p = [(s // 2, turn_piece, (pe, "a", g, b, s)) for s in range(NB)]
                p += [(UP_A[i // 2], up_piece, (pe, "a", g, b, i, last_z)) for i in range(16)]
                p += [(DOWN_A[i // 2], down_piece, (pe, "a", g, i)) for i in range(16)]
                p += [(62 + s // 2, turn_piece, (pe, "p", g, b, s)) for s in range(NB)]
                p += [(70 + s // 2, input_piece, (pe, g, b, s)) for s in range(NB)]
                return p

            @block.tensor
            def _(pe):
                def run(plan, t):
                    for at, f, args in plan:
                        if at == t:
                            f(*args)

                def body(g, b, post, pre):
                    plan = plan_post(pe, g - 1, 1 - b, g + 2 if pre else GROUPS) if post else []
                    plan += plan_pre(pe, g + 1, 1 - b, g - 1 if post else None) if pre else []
                    for t in range(128):
                        last = state[b][:, NB * (t - 1):NB * t] if t else state[1 - b][:, 512 - NB:512]
                        pe.wait_ge(s_tanh, ONE + 128 * g + t)
                        nc.tensor.matmul(scan[b][0:STATE, NB * t:NB * (t + 1)], rnnA[:, :], last, start=False,
                                         stop=(t == 127), skip_group_check=True).then_inc(s_step, 1)
                        run(plan, t)

                pre = plan_pre(pe, 0, 0, None)
                for t in range(128):
                    run(pre, t)
                pe.wait_ge(s_zero, ONE + 1)
                body(0, 0, False, True)
                with pe.Fori(0, GROUPS // 2 - 1) as i:
                    body(2 * i + 1, 1, True, True)
                    body(2 * i + 2, 0, True, True)
                body(GROUPS - 1, 1, True, False)
                post = plan_post(pe, GROUPS - 1, 1, GROUPS)
                for t in range(128):
                    run(post, t)

            @block.scalar
            def _(act):
                def gelu_piece(k, g, c, s):
                    if s == 0:
                        act.wait_ge(s_up[k], ONE + FC * g + c + 1)
                        if k == "z":
                            act.wait_ge(s_down["r"], ONE + g + 1)
                        else:
                            act.wait_ge(s_down["z" if k == "r" else "a"], ONE + g)
                    ins = nc.scalar.activation(H[k][c][:, s * 128:(s + 1) * 128],
                                               UP[k][c % len(UP[k])][:, s * 128:(s + 1) * 128], ACT.Gelu,
                                               bias=bias[:, BIAS[k] + c:BIAS[k] + c + 1])
                    if s == NB - 1:
                        ins.then_inc(s_h[k], 1)

                GELU_A, GELU_R = [8, 10, 20, 24], [18, 22, 26, 28]

                def plan_gelus(g_post, g_pre):
                    p = []
                    for c in range(FC):
                        for s in range(NB):
                            if g_post is not None:
                                p.append((GELU_R[c] + s // 2, ("r", g_post, c, s)))
                                p.append((52 + 2 * c + s // 2, ("z", g_post, c, s)))
                            if g_pre is not None:
                                p.append((GELU_A[c] + s // 2, ("a", g_pre, c, s)))
                    return p

                def run(plan, t):
                    for at, args in plan:
                        if at == t:
                            gelu_piece(*args)

                def body(g, b, post, pre):
                    plan = plan_gelus(g - 1 if post else None, g + 1 if pre else None)
                    if post:
                        act.wait_ge(s_out, ONE + g - 1)
                    for t in range(128):
                        act.wait_ge(s_step, ONE + 128 * g + t + 1)
                        nc.scalar.activation(state[b][0:STATE, NB * t:NB * (t + 1)], scan[b][0:STATE, NB * t:NB * (t + 1)],
                                             ACT.Tanh).then_inc(s_tanh, 1)
                        run(plan, t)

                plan = plan_gelus(None, 0)
                for t in range(128):
                    run(plan, t)
                body(0, 0, False, True)
                with act.Fori(0, GROUPS // 2 - 1) as i:
                    body(2 * i + 1, 1, True, True)
                    body(2 * i + 2, 0, True, True)
                body(GROUPS - 1, 1, True, False)
                plan = plan_gelus(GROUPS - 1, None)
                for t in range(128):
                    run(plan, t)
HEADS, HD, BLK, LEVELS = 16, 64, 16, 5
HH = HEADS // 2
FINE = SEQ // BLK
NBLK = [FINE // 2 ** (l + 1) for l in range(1, LEVELS + 1)]
BASE = [FINE + sum(NBLK[:l]) for l in range(LEVELS)]
QBLK = 96
assert BASE[-1] + NBLK[-1] == QBLK - 1
COLS = [SEQ // 2 ** l for l in range(LEVELS + 1)]
COL0 = [sum(COLS[:l]) for l in range(LEVELS + 1)]
X_UP, M_UP, A_UP, N_UP, Y_UP, DEN_UP = 16.0, 16.0, 256.0, 256.0, 64.0, 64.0
ATT_EPS = 1e-8
MASK0 = -3e38
LEAST = 1e-20


def attention_layouts(f):
    import numpy as np
    w = f("L0_attn_w_qkv").reshape(3, HEADS, HD, D).transpose(0, 2, 1, 3).reshape(3, HD, HEADS * D)
    p = np.arange(128)
    head, i = p // BLK, p % BLK
    sel = np.zeros((128, 2, BLK, HEADS), np.float16)
    for half in range(2):
        sel[p, half, i, head + HH * half] = 1
    own = np.zeros((128, 2, HEADS), np.float32)
    for half in range(2):
        own[p, half, head + HH * half] = 1
    return {
        "att_wq": w[0], "att_wk": w[1], "att_wv": w[2],
        "att_wo": f("L0_attn_w_out").T.reshape(HEADS, HD, D).transpose(1, 0, 2).reshape(HD, HEADS * D),
        "att_bias": f("L0_attn_b_out").reshape(1, D),
        "att_sel": sel.reshape(128, -1), "att_selT": sel.transpose(3, 1, 2, 0).reshape(HEADS, -1),
        "att_own": own.reshape(128, -1),
        "att_mask": np.where(np.arange(BLK)[None, :] > i[:, None], MASK0, 0.0).astype(np.float32),
    }


def load_attention(nc, ctx, A, S, load):
    load("att_sel", [128, 2 * BLK * HEADS], A["att_sel"], F16)
    load("att_selT", [HEADS, 2 * BLK * 128], A["att_selT"], F16)
    load("att_own", [128, 2 * HEADS], A["att_own"])
    load("att_mask", [128, BLK], A["att_mask"])
    load("att_bias", [128, 1, D], A["att_bias"].partition_broadcast(128))


def combine_weights(nc, A, S, att):
    rmax = bass.bass_isa.ReduceOp.max
    with ExitStack() as ctx:
        sb = lambda n, shape: ctx.enter_context(nc.sbuf_tensor(n, shape, F32))
        w = {k: sb(f"w_{k}", [HD, HEADS * D]) for k in ("att_wq", "att_wk", "att_wv", "att_wo")}
        banks = [ctx.enter_context(nc.psum_tensor(f"cw{i}", [128, 512], F32)) for i in range(8)]
        scaled = [sb(f"scaled{i}", [128, HEADS * D]) for i in range(2)]
        peak, allpeak, up = sb("peak", [128, 32]), sb("allpeak", [128, 32]), sb("up", [128, 32])
        tmp = sb("own_peaks", [128, 2, HEADS])
        s_w, s_mm, s_peak, s_all, s_sc, s_hi = (ctx.enter_context(nc.semaphore(n)) for n in
                                               ("cw_load", "cw_mm", "cw_peak", "cw_all", "cw_scaled", "cw_hi"))
        with nc.Block() as block:
            @block.sync
            def _(sp):
                for k in w:
                    sp.dma_start(w[k][:, :], A[k]).then_inc(s_w, 16)

            @block.tensor
            def _(pe):
                pe.wait_ge(s_w, 64)
                for i, (a, b) in enumerate((("att_wq", "att_wk"), ("att_wv", "att_wo"))):
                    for h in range(HEADS):
                        ins = nc.tensor.matmul(banks[4 * i + h // 4][:, (h % 4) * D:(h % 4 + 1) * D],
                                               w[a][:, h * D:(h + 1) * D], w[b][:, h * D:(h + 1) * D],
                                               start=True, stop=True)
                    ins.then_inc(s_mm, 1)

            @block.gpsimd
            def _(pool):
                pool.wait_ge(s_peak, 1)
                pool.partition_all_reduce(allpeak[:, :], peak[:, :], 128, rmax).then_inc(s_all, 1)

            @block.vector
            def _(dve):
                dve.memset(peak[:, :], 0.0)
                dve.drain()
                dve.wait_ge(s_mm, 2)
                for j in range(4):
                    dve.tensor_reduce(peak[:, 4 * j:4 * j + 4], banks[j][:, :].rearrange("p (h d) -> p h d", d=D),
                                      AX.X, ALU.max, apply_absolute_value=True)
                    dve.tensor_reduce(peak[:, 16 + j:17 + j], banks[4 + j][:, :], AX.X, ALU.max,
                                      apply_absolute_value=True)
                dve.drain()
                dve.tensor_reduce(peak[:, 20:21], peak[:, 16:20], AX.X, ALU.max).then_inc(s_peak, 1)
                dve.wait_ge(s_all, 1)
                dve.tensor_scalar(allpeak[:, :], allpeak[:, :], LEAST, None, ALU.max)
                dve.drain()
                dve.reciprocal(up[:, :], allpeak[:, :])
                dve.drain()
                dve.tensor_scalar(up[:, 0:16], up[:, 0:16], M_UP, None, ALU.mult)
                dve.tensor_scalar(up[:, 20:21], up[:, 20:21], N_UP, None, ALU.mult)
                for half in range(2):
                    dve.tensor_tensor(tmp[:, half, :], S["att_own"][:, half * HEADS:(half + 1) * HEADS],
                                      allpeak[:, 0:HEADS], ALU.mult)
                dve.drain()
                dve.tensor_reduce(att["undo"][:, 0:2], tmp[:, :, :], AX.X, ALU.add)
                dve.tensor_scalar(att["undo"][:, 2:3], allpeak[:, 20:21], 1.0 / (N_UP * Y_UP), None, ALU.mult)
                dve.drain()
                dve.tensor_scalar(att["undo"][:, 0:2], att["undo"][:, 0:2], HD ** -0.5 / (X_UP * X_UP * M_UP), None,
                                  ALU.mult)
                for h in range(HEADS):
                    dve.tensor_scalar(scaled[0][:, h * D:(h + 1) * D], banks[h // 4][:, (h % 4) * D:(h % 4 + 1) * D],
                                      up[:, h:h + 1], None, ALU.mult)
                for j in range(4):
                    dve.tensor_scalar(scaled[1][:, 512 * j:512 * (j + 1)], banks[4 + j][:, :], up[:, 20:21], None,
                                      ALU.mult)
                dve.drain().then_inc(s_sc, 1)
                dve.wait_ge(s_hi, 2)
                for i, n in enumerate("MN"):
                    dve.tensor_tensor(att[n + "lo"][:, :], scaled[i][:, :], att[n + "hi"][:, :], ALU.subtract)

            @block.scalar
            def _(act):
                act.wait_ge(s_sc, 1)
                for i, n in enumerate("MN"):
                    nc.scalar.activation(att[n + "hi"][:, :], scaled[i][:, :], ACT.Copy).then_inc(s_hi, 1)


def hierarchical_attention(nc, A, S, tag):
    x, ident = S["x"], S["ident"]
    outer = ExitStack()
    with outer:
        att = {n: outer.enter_context(nc.sbuf_tensor("att_" + n, [128, HEADS * D], F16))
               for n in ("Mhi", "Mlo", "Nhi", "Nlo")}
        att["undo"] = outer.enter_context(nc.sbuf_tensor("att_undo", [128, 4], F32))
        combine_weights(nc, A, S, att)
        attention_core(nc, S, att, x, ident)


def attention_core(nc, S, att, x, ident):
    sel = S["att_sel"][:, :].rearrange("p (j h) -> p j h", h=HEADS)
    selT = S["att_selT"][:, :].rearrange("h (j p) -> h j p", p=128)
    with ExitStack() as ctx:
        sb = lambda n, shape, dt=F32: ctx.enter_context(nc.sbuf_tensor("at_" + n, shape, dt))
        bank = lambda n: ctx.enter_context(nc.psum_tensor("at_" + n, [128, 512], F32))
        sems = []

        def sem(n):
            sems.append(ctx.enter_context(nc.semaphore("at_" + n)))
            return sems[-1]

        stats, mv, root = sb("stats", [128, GROUPS, 6]), sb("mv", [128, GROUPS, 2]), sb("root", [128, 3, GROUPS])
        xn = sb("xn", [128, GROUPS, D])
        xT = sb("xT", [128, sum(COLS)])
        keys = sb("keys", [128, QBLK, 4, BLK], F16)
        coarse_q = sb("coarse_q", [128, 2, QBLK - FINE, BLK], F16)
        values = sb("values", [128, QBLK // 2, 2, D], F16)
        big = [sb(f"big{i}", [128, 2 * 32 * HEADS * BLK], F16) for i in range(2)]
        half_of = lambda t, i: t[:, i * 8192:(i + 1) * 8192].rearrange("p (q h i) -> p q h i", h=HEADS, i=BLK)
        XH, XL = ([half_of(t, i) for i in range(2)] for t in big)
        W4 = 2 * QBLK * 4 * BLK
        A4 = big[0][:, 0:W4].rearrange("p (a q e i) -> p a q e i", q=QBLK, e=4, i=BLK)
        A4T = big[1][:, 0:W4].rearrange("p (a q c) -> p a q c", a=2, c=128)
        tile_of = lambda t, i: t[:, W4 + i * HEADS * 128:W4 + (i + 1) * HEADS * 128].rearrange("p (h t) -> p h t", h=HEADS)
        YH, YL = ([tile_of(t, i) for i in range(2)] for t in big)
        den16 = big[0][0:HEADS, W4:W4 + 2 * BLK * QBLK].rearrange("h (e i q) -> h e i q", e=2, q=QBLK)
        logits = [sb(f"logits{i}", [128, 2, 16, BLK]) for i in range(2)]
        peaks = [sb(f"peaks{i}", [128, 2, 16]) for i in range(2)]
        E = sb("E", [128, 2, QBLK, BLK])
        sums, sums16 = sb("sums", [128, 2, QBLK]), sb("sums16", [128, 2, 2 * QBLK], F16)
        den = xn[0:HEADS, :, :].rearrange("h g d -> h (g d)")
        cden = sb("cden", [HEADS, BLK, QBLK - FINE])
        scale = sb("scale", [128, 2, QBLK])
        ident16 = sb("ident16", [128, 128], F16)

        RING = 4
        ring = [bank(f"ring{i}") for i in range(RING)]
        sbk = [bank(f"s{i}") for i in range(2)]
        TRN = 2
        tr = [bank(f"tr{i}") for i in range(TRN)]

        s_stats, s_root, s_xn = sem("stats"), sem("root"), sem("xn")
        s_tr, s_trout = sem("turned"), [sem(f"turn_out{i}") for i in range(TRN)]
        s_xT, s_pool, s_khi, s_klo, s_keys = sem("rows_out"), sem("pooled"), sem("keys_hi"), sem("keys_lo"), sem("keys")
        s_xm, s_xhi, s_xlo = sem("xm"), sem("xm_hi"), sem("xm_lo")
        s_s, s_sread, s_sub, s_e = sem("logits"), sem("logits_read"), sem("logits_shifted"), sem("exp")
        s_sums, s_den, s_denread, s_cden = sem("sums"), sem("den"), sem("den_read"), sem("coarse_den_read")
        s_dall, s_dhi, s_d16, s_scaled = sem("den_all_levels"), sem("den_hi"), sem("den16"), sem("scaled")
        s_ahi, s_a4, s_y, s_yhi, s_ylo, s_out, s_x = (sem("a_hi"), sem("a4"), sem("y"), sem("y_hi"), sem("y_lo"),
                                                      sem("out"), sem("x"))
        s_const = sem("const")

        U_X, U_V, U_R, U_A = 0, 2, 8, 9
        USES = U_A + 12
        BANK_USES = [len(range(b, USES, TRN)) for b in range(TRN)]
        A_ORDER = (2, 0, 1)
        VALUES_AT = (0, 2, 5, 8, 11, 14)

        def level(l, odd):
            v = xT[:, COL0[l]:COL0[l] + COLS[l]].rearrange("p (m o i) -> p m o i", o=2, i=BLK)
            return v[:, :, odd, :]

        def spots(t, l):
            step = 2 ** l
            v = t[:, :].rearrange("h (m o i r) -> h m o i r", o=2, i=BLK, r=step)
            return v[:, :, 1, :, step - 1]

        def den_parts():
            yield den[:, :].rearrange("h (q i) -> h q i", i=BLK), slice(0, FINE), DEN_UP
            for l in range(1, LEVELS + 1):
                yield spots(den, l), slice(BASE[l - 1], BASE[l - 1] + NBLK[l - 1]), DEN_UP * 2.0 ** -l

        def turned(s, u):
            return ONE + USES * s + u + 1

        def xs(s):
            return x[:, :, bass.ds(s, 1), :].rearrange("p g a d -> p g (a d)")

        def weight_use(u):
            c, r = divmod(u, 4)
            half, part = divmod(r, 2)
            return A_ORDER[c], half, 16 * A_ORDER[c] + 8 * part

        with nc.Block() as block:
            @block.sync
            def _(sp):
                for s in sems:
                    sp.sem_inc(s, ONE)

            @block.gpsimd
            def _(pool):
                def entry(s):
                    pool.wait_ge(s_stats, ONE + s + 1)
                    pool.wait_ge(s_xn, ONE + s)
                    pool.tensor_tensor(root[:, 0, :], mv[:, :, 1], S["epsilon"][:, 0:GROUPS], ALU.add)
                    pool.drain()
                    pool.tensor_tensor(root[:, 1, :], root[:, 0, :], S["minus_half"][:, 0:GROUPS], ALU.pow)
                    pool.drain()
                    pool.tensor_scalar(root[:, 2, :], root[:, 1, :], X_UP, None, ALU.mult).then_inc(s_root, 1)

                with pool.Fori(0, NB) as s:
                    entry(s)

            @block.scalar
            def _(act):
                def rows_out(s):
                    for u in range(2):
                        act.wait_ge(s_tr, turned(s, U_X + u))
                        nc.scalar.activation(xT[:, 512 * u:512 * (u + 1)], tr[(U_X + u) % TRN][:, :], ACT.Copy)
                        nc.scalar.drain().then_inc(s_trout[(U_X + u) % TRN], 1)
                    act.sem_inc(s_xT, 1)

                def hi_keys(s, l):
                    if l == 0:
                        act.wait_ge(s_pool, ONE + s + 1)
                        act.wait_ge(s_s, ONE + 6 * s)
                        nc.scalar.activation(keys[:, 0:FINE, 0:2, :],
                                             xT[:, 0:SEQ].rearrange("p (q i) -> p q i", i=BLK).unsqueeze(2)
                                             .broadcast_to([128, FINE, 2, BLK]), ACT.Copy).then_inc(s_khi, 1)
                        return
                    n, b = NBLK[l - 1], BASE[l - 1]
                    nc.scalar.activation(keys[:, b:b + n, 0:2, :],
                                         level(l, 0).unsqueeze(2).broadcast_to([128, n, 2, BLK]),
                                         ACT.Copy, scale=2.0 ** -l)
                    nc.scalar.activation(coarse_q[:, 0, b - FINE:b - FINE + n, :], level(l, 1),
                                         ACT.Copy, scale=2.0 ** -l).then_inc(s_khi, 1)

                def values_out(s, u):
                    act.wait_ge(s_tr, turned(s, U_V + u))
                    if u == 0:
                        act.wait_ge(s_y, ONE + 32 * s)
                    for o in range(2):
                        r = slice(64 * o, 64 * o + 64)
                        last = nc.scalar.activation(values[r, 8 * u:8 * u + 8, o, :],
                                                    tr[(U_V + u) % TRN][r, :].bitcast(F16)
                                                    .rearrange("p (q d) -> p q d", d=D), ACT.Copy)
                    last.then_inc(s_trout[(U_V + u) % TRN], 1)

                def hi_xm(s, c, h):
                    if h == 0:
                        act.wait_ge(s_s, ONE + 6 * s + 2 * max(c - 1, 0))
                        if c == 0:
                            act.wait_ge(s_out, ONE + 8 * s)
                    n = HEADS * c + h
                    act.wait_ge(s_xm, ONE + 48 * s + n + 1)
                    nc.scalar.activation(XH[c % 2][:, :, h, :], ring[n % RING][:, :].rearrange("p (q i) -> p q i", i=BLK),
                                         ACT.Copy).then_inc(s_xhi, 1)

                def exps(s, k):
                    act.wait_ge(s_sub, ONE + 6 * s + k + 1)
                    act.wait_ge(s_a4, ONE + 3 * s)
                    for half in range(2):
                        last = nc.scalar.activation(E[:, half, 16 * k:16 * k + 16, :], logits[k % 2][:, half, :, :],
                                                    ACT.Exp, scale=att["undo"][:, half:half + 1])
                    last.then_inc(s_e, 1)

                def coarse_den(s):
                    for u in range(4):
                        act.wait_ge(s_denread, ONE + 4 * s + u + 1)
                        b = ring[u][0:HEADS, :].rearrange("h (i q) -> h i q", q=128)
                        nc.scalar.activation(cden[:, 4 * u:4 * u + 4, :], b[:, :, FINE:QBLK],
                                             ACT.Copy).then_inc(s_cden, 1)

                def hi_den(s):
                    act.wait_ge(s_dall, ONE + s + 1)
                    for src, q, up in den_parts():
                        nc.scalar.activation(den16[:, 0, :, q].rearrange("h i q -> h q i"), src, ACT.Copy,
                                             scale=up).then_inc(s_dhi, 1)

                def hi_weights(s, c):
                    q = slice(32 * A_ORDER[c], 32 * A_ORDER[c] + 32)
                    act.wait_ge(s_scaled, ONE + 3 * s + c + 1)
                    for half in range(2):
                        last = nc.scalar.activation(A4[:, half, q, 0:4:2, :],
                                                    E[:, half, q, :].unsqueeze(2).broadcast_to([128, 32, 2, BLK]),
                                                    ACT.Copy)
                    last.then_inc(s_ahi, 1)

                def weights_out(s, u):
                    _, half, q = weight_use(u)
                    b = (U_A + u) % TRN
                    act.wait_ge(s_tr, turned(s, U_A + u))
                    nc.scalar.activation(A4T[:, half, q:q + 8, :].rearrange("p q d -> p (q d)"),
                                         tr[b][:, :].bitcast(F16), ACT.Copy).then_inc(s_trout[b], 1)

                def hi_y(s, ck, half):
                    n = 2 * ck + half
                    t = ck // 2
                    act.wait_ge(s_y, ONE + 32 * s + n + 1)
                    act.wait_ge(s_out, ONE + 8 * s + max(t - 1, 0))
                    nc.scalar.activation(YH[t % 2][:, HH * half:HH * (half + 1), 64 * (ck % 2):64 * (ck % 2) + 64],
                                         ring[n % RING][:, :].rearrange("p (h t) -> p h t", h=HH), ACT.Copy,
                                         scale=Y_UP / (X_UP * A_UP)).then_inc(s_yhi, 1)

                def keys_twice(s):
                    act.wait_ge(s_klo, ONE + s + 1)
                    nc.scalar.activation(keys[:, 0:QBLK - 1, 3, :], keys[:, 0:QBLK - 1, 2, :],
                                         ACT.Copy).then_inc(s_keys, 1)

                def entry(s, ahead):
                    for c in range(3):
                        for h in range(HEADS):
                            hi_xm(s, c, h)
                            if c == 0 and h in VALUES_AT and VALUES_AT.index(h) % 2 == 0:
                                values_out(s, VALUES_AT.index(h))
                            if c > 0 and h == 12:
                                exps(s, 2 * c - 2)
                            if c == 2 and h == 4:
                                exps(s, 1)
                    for k in (3, 4, 5):
                        exps(s, k)
                    coarse_den(s)
                    hi_den(s)
                    for c in range(3):
                        hi_weights(s, c)
                        for u in range(4 * c + 1, 4 * c + 4, 2):
                            weights_out(s, u)
                    for ck in range(16):
                        for half in range(2):
                            hi_y(s, ck, half)
                        if ahead:
                            if ck == 5:
                                rows_out(s + 1)
                            if 8 <= ck <= 8 + LEVELS:
                                hi_keys(s + 1, ck - 8)
                            if ck == 15:
                                keys_twice(s + 1)

                act.wait_ge(s_const, ONE + 1)
                rows_out(0)
                for l in range(LEVELS + 1):
                    hi_keys(0, l)
                keys_twice(0)
                with act.Fori(0, NB - 1) as s:
                    entry(s, True)
                entry(NB - 1, False)

            @block.tensor
            def _(pe):
                def use(s, u):
                    b = u % TRN
                    pe.wait_ge(s_trout[b], ONE + BANK_USES[b] * s + u // TRN)
                    return tr[b]

                def rows(s, u):
                    if u == 0:
                        pe.wait_ge(s_xn, ONE + s + 1)
                    b = use(s, U_X + u)
                    for j in range(4):
                        last = nc.tensor.transpose(b[:, 128 * j:128 * (j + 1)], xn[:, 4 * u + j, :], ident[:, :])
                    last.then_inc(s_tr, 1)

                def turn_values(s, u):
                    if u == 0:
                        pe.wait_ge(s_keys, ONE + s + 1)
                    b = use(s, U_V + u)[:, :].bitcast(F16)
                    for j in range(8):
                        src = keys[:, 16 * u + 2 * j:16 * u + 2 * j + 2, :, :].rearrange("p q e i -> p (q e i)")
                        last = nc.tensor.transpose(b[:, 128 * j:128 * (j + 1)], src, ident16[:, :])
                    last.then_inc(s_tr, 1)

                def xm(s, c, h):
                    src = lambda lo: keys[:, 32 * c:32 * c + 32, 2 * lo, :] if c < 2 else coarse_q[:, lo, :, :]
                    n = HEADS * c + h
                    if n == 0:
                        pe.wait_ge(s_klo, ONE + s + 1)
                    pe.wait_ge(s_xlo, ONE + 48 * s + max(n - RING + 1, 0))
                    if n < RING:
                        pe.wait_ge(s_ylo, ONE + 32 * s)
                    for i, (w, lo) in enumerate((("Mhi", 0), ("Mhi", 1), ("Mlo", 0))):
                        last = nc.tensor.matmul(ring[n % RING][:, :], att[w][:, h * D:(h + 1) * D], src(lo),
                                                start=(i == 0), stop=(i == 2))
                    last.then_inc(s_xm, 1)

                def logits_of(s, blk):
                    c, (k, q) = blk // 32, divmod(blk, 16)
                    j = k % 2
                    if blk % 32 == 0:
                        pe.wait_ge(s_xlo, ONE + 48 * s + HEADS * (c + 1))
                    if q == 0:
                        pe.wait_ge(s_sread, ONE + 6 * s + max(k - 1, 0))
                        if k < 2:
                            pe.wait_ge(s_x, ONE + 8 * s)
                    for half in range(2):
                        o = sbk[j][:, 256 * half + BLK * q:256 * half + BLK * (q + 1)]
                        hs_ = slice(HH * half, HH * (half + 1))
                        lh = XH[c % 2][:, blk % 32, hs_, :].rearrange("p h i -> p (h i)")
                        ll = XL[c % 2][:, blk % 32, hs_, :].rearrange("p h i -> p (h i)")
                        nc.tensor.matmul(o, lh, keys[:, blk, 0, :], start=True, stop=False)
                        nc.tensor.matmul(o, lh, keys[:, blk, 2, :], start=False, stop=False)
                        last = nc.tensor.matmul(o, ll, keys[:, blk, 0, :], start=False, stop=True)
                    if q == 15:
                        last.then_inc(s_s, 1)

                def denominators(s):
                    pe.wait_ge(s_sums, ONE + s + 1)
                    for u in range(4):
                        for ii in range(4):
                            i = 4 * u + ii
                            for n, (half, lo) in enumerate(((0, 0), (0, 1), (1, 0), (1, 1))):
                                last = nc.tensor.matmul(ring[u][0:HEADS, 128 * ii:128 * ii + QBLK],
                                                        sel[:, BLK * half + i, :],
                                                        sums16[:, lo, QBLK * half:QBLK * (half + 1)],
                                                        start=(n == 0), stop=(n == 3))
                        last.then_inc(s_den, 1)

                def spread(s):
                    pe.wait_ge(s_d16, ONE + s + 1)
                    b = use(s, U_R)
                    for half in range(2):
                        for i in range(BLK):
                            for lo in range(2):
                                last = nc.tensor.matmul(b[:, QBLK * half:QBLK * (half + 1)],
                                                        selT[:, BLK * half + i, :], den16[:, lo, i, :],
                                                        start=(i == 0 and lo == 0), stop=(i == BLK - 1 and lo == 1))
                    last.then_inc(s_tr, 1)

                def turn_weights(s, u):
                    c, half, q = weight_use(u)
                    if u % 4 == 0:
                        pe.wait_ge(s_a4, ONE + 3 * s + u // 4 + 1)
                    b = use(s, U_A + u)[:, :].bitcast(F16)
                    for j in range(8):
                        n = 2 * (q + j)
                        last = nc.tensor.transpose(b[:, 128 * j:128 * (j + 1)],
                                                   A4[:, half, n:n + 2, :, :].rearrange("p q e i -> p (q e i)"),
                                                   ident16[:, :])
                    last.then_inc(s_tr, 1)

                def apply_weights(s, ck, half):
                    n = 2 * ck + half
                    if n == 0:
                        for b in range(TRN):
                            pe.wait_ge(s_trout[b], ONE + BANK_USES[b] * (s + 1))
                        pe.wait_ge(s_denread, ONE + 4 * (s + 1))
                        pe.wait_ge(s_cden, ONE + 4 * (s + 1))
                    pe.wait_ge(s_ylo, ONE + 32 * s + max(n - RING + 1, 0))
                    y = ring[n % RING][:, :].rearrange("p (h t) -> p h t", h=HH)
                    jobs = [(4 * ck + j, 0, BLK, 16 * j, 1) for j in range(4)]
                    for l in range(1, LEVELS + 1):
                        step = 2 ** l
                        start = 64 * ck + step - 1 if step * BLK >= 64 else 64 * ck + 32 + step - 1
                        blk, i = divmod(start // step, BLK)
                        if blk % 2 == 1:
                            cnt = (64 * (ck + 1) - start + step - 1) // step
                            jobs.append((BASE[l - 1] + blk // 2, i, cnt, start - 64 * ck, step))
                    for a, (q, i, cnt, at, step) in enumerate(jobs):
                        rhs = A4T[:, half, q // 2, :].rearrange("p (h i) -> p h i", i=BLK)[:, :, i:i + cnt]
                        last = nc.tensor.matmul(y[:, :, at:at + (cnt - 1) * step + 1:step], values[:, q // 2, q % 2, :], rhs,
                                                start=(a == 0), stop=(a == len(jobs) - 1), skip_group_check=True)
                    last.then_inc(s_y, 1)

                def project(s, t):
                    pe.wait_ge(s_ylo, ONE + 32 * s + 4 * (t + 1))
                    pe.wait_ge(s_x, ONE + 8 * s + max(t - 1, 0))
                    for h in range(HEADS):
                        for n, (y, w) in enumerate(((YH, "Nhi"), (YH, "Nlo"), (YL, "Nhi"))):
                            last = nc.tensor.matmul(sbk[t % 2][:, 0:D], y[t % 2][:, h, :], att[w][:, h * D:(h + 1) * D],
                                                    start=(h == 0 and n == 0), stop=(h == HEADS - 1 and n == 2))
                    last.then_inc(s_out, 1)

                def entry(s, ahead):
                    for c in range(3):
                        for h in range(HEADS):
                            xm(s, c, h)
                            if c == 0 and h in VALUES_AT:
                                turn_values(s, VALUES_AT.index(h))
                            if c > 0:
                                for j in range(2):
                                    logits_of(s, 32 * (c - 1) + 2 * h + j)
                    for blk in range(64, 96):
                        logits_of(s, blk)
                    denominators(s)
                    spread(s)
                    for u in range(12):
                        turn_weights(s, u)
                    for ck in range(16):
                        for half in range(2):
                            apply_weights(s, ck, half)
                        if ck % 2 == 1 and ck >= 3:
                            project(s, ck // 2 - 1)
                        if ahead and ck in (4, 5):
                            rows(s + 1, ck - 4)
                    project(s, 7)

                pe.wait_ge(s_const, ONE + 1)
                rows(0, 0)
                rows(0, 1)
                with pe.Fori(0, NB - 1) as s:
                    entry(s, True)
                entry(NB - 1, False)

            @block.vector
            def _(dve):
                def statistics(s):
                    for g in range(GROUPS):
                        dve.bn_stats(stats[:, g, :], xs(s)[:, g, :])
                    dve.drain()
                    for g in range(GROUPS):
                        last = dve.bn_aggr(mv[:, g, :], stats[:, g, :])
                    last.then_inc(s_stats, 1)

                def norm(s):
                    dve.wait_ge(s_root, ONE + s + 1)
                    dve.wait_ge(s_tr, ONE + USES * s)
                    for g in range(GROUPS):
                        last = dve.tensor_scalar(xn[:, g, :], xs(s)[:, g, :], mv[:, g, 0:1], root[:, 2, g:g + 1],
                                                 ALU.subtract, ALU.mult)
                    last.then_inc(s_xn, 1)
                    dve.wait_ge(s_xn, ONE + s + 1)
                    dve.tensor_tensor(xs(s), xs(s), S["att_bias"][:, :, :].broadcast_to([128, GROUPS, D]), ALU.add)

                def pool_levels(s):
                    dve.wait_ge(s_xT, ONE + s + 1)
                    for l in range(1, LEVELS + 1):
                        v = xT[:, COL0[l - 1]:COL0[l - 1] + COLS[l - 1]].rearrange("p (t o) -> p t o", o=2)
                        last = dve.tensor_tensor(xT[:, COL0[l]:COL0[l] + COLS[l]], v[:, :, 0], v[:, :, 1], ALU.add)
                        if l < LEVELS:
                            dve.drain()
                    last.then_inc(s_pool, 1)

                def lo_keys(s, l):
                    dve.wait_ge(s_khi, ONE + (LEVELS + 1) * s + l + 1)
                    if l == 0:
                        dve.wait_ge(s_pool, ONE + s + 1)
                        fine = xT[:, 0:SEQ].rearrange("p (q i) -> p q i", i=BLK)
                        dve.tensor_tensor(keys[:, 0:FINE, 2, :], fine, keys[:, 0:FINE, 0, :], ALU.subtract)
                        return
                    n, b = NBLK[l - 1], BASE[l - 1]
                    dve.scalar_tensor_tensor(keys[:, b:b + n, 2, :], level(l, 0), 2.0 ** -l,
                                             keys[:, b:b + n, 0, :], ALU.mult, ALU.subtract)
                    c = slice(b - FINE, b - FINE + n)
                    last = dve.scalar_tensor_tensor(coarse_q[:, 1, c, :], level(l, 1), 2.0 ** -l,
                                                    coarse_q[:, 0, c, :], ALU.mult, ALU.subtract)
                    if l == LEVELS:
                        last.then_inc(s_klo, 1)

                def lo_xm(s, c, h):
                    if h == 0:
                        dve.wait_ge(s_s, ONE + 6 * s + 2 * max(c - 1, 0))
                        if c == 0:
                            dve.wait_ge(s_out, ONE + 8 * s)
                    n = HEADS * c + h
                    dve.wait_ge(s_xhi, ONE + 48 * s + n + 1)
                    dve.tensor_tensor(XL[c % 2][:, :, h, :], ring[n % RING][:, :].rearrange("p (q i) -> p q i", i=BLK),
                                      XH[c % 2][:, :, h, :], ALU.subtract).then_inc(s_xlo, 1)

                def shift(s, k):
                    j = k % 2
                    dve.wait_ge(s_s, ONE + 6 * s + k + 1)
                    dve.wait_ge(s_e, ONE + 6 * s + max(k - 1, 0))
                    t = logits[j][:, :, :, :].rearrange("p a q i -> p (a q) i")
                    src = sbk[j][:, :].rearrange("p (q i) -> p q i", i=BLK)
                    if k < 4:
                        dve.tensor_tensor(t, src, S["att_mask"][:, :].unsqueeze(1).broadcast_to([128, 32, BLK]),
                                          ALU.add).then_inc(s_sread, 1)
                    else:
                        dve.tensor_copy(t, src).then_inc(s_sread, 1)
                    dve.drain()
                    pk = peaks[j][:, :, :].rearrange("p a q -> p (a q)")
                    dve.tensor_reduce(pk, t, AX.X, ALU.max)
                    dve.drain()
                    dve.tensor_tensor(t, t, pk.unsqueeze(2).broadcast_to([128, 32, BLK]),
                                      ALU.subtract).then_inc(s_sub, 1)

                def add_up(s, k):
                    dve.wait_ge(s_e, ONE + 6 * s + k + 1)
                    dve.tensor_reduce(sums[:, :, 16 * k:16 * k + 16], E[:, :, 16 * k:16 * k + 16, :], AX.X, ALU.add)

                def split_sums(s):
                    dve.drain()
                    flat = sums[:, :, :].rearrange("p a q -> p (a q)")
                    dve.tensor_copy(sums16[:, 0, :], flat)
                    dve.drain()
                    dve.tensor_tensor(sums16[:, 1, :], flat, sums16[:, 0, :], ALU.subtract).then_inc(s_sums, 1)

                def all_levels(s):
                    dv = den[:, :].rearrange("h (q i) -> h i q", i=BLK)
                    for u in range(4):
                        dve.wait_ge(s_den, ONE + 4 * s + u + 1)
                        b = ring[u][0:HEADS, :].rearrange("h (i q) -> h i q", q=128)
                        dve.tensor_scalar(dv[:, 4 * u:4 * u + 4, :], b[:, :, 0:FINE], ATT_EPS, None,
                                          ALU.add).then_inc(s_denread, 1)
                    dve.drain()
                    dve.wait_ge(s_cden, ONE + 4 * (s + 1))
                    for l in range(1, LEVELS + 1):
                        n, b = NBLK[l - 1], BASE[l - 1] - FINE
                        at = spots(den, l)
                        last = dve.tensor_tensor(at, at, cden[:, :, b:b + n].rearrange("h i m -> h m i"), ALU.add)
                        if l < LEVELS:
                            dve.drain()
                    last.then_inc(s_dall, 1)
                    for n, (src, q, up) in enumerate(den_parts()):
                        dve.wait_ge(s_dhi, ONE + (LEVELS + 1) * s + n + 1)
                        if n == 0:
                            dve.wait_ge(s_dall, ONE + s + 1)
                        last = dve.scalar_tensor_tensor(den16[:, 1, :, q].rearrange("h i q -> h q i"), src, up,
                                                        den16[:, 0, :, q].rearrange("h i q -> h q i"),
                                                        ALU.mult, ALU.subtract)
                    last.then_inc(s_d16, 1)

                def reciprocals(s):
                    dve.wait_ge(s_tr, turned(s, U_R))
                    dve.reciprocal(scale[:, :, :].rearrange("p a q -> p (a q)"),
                                   tr[U_R % TRN][:, 0:2 * QBLK]).then_inc(s_trout[U_R % TRN], 1)
                    dve.drain()
                    dve.memset(scale[:, :, QBLK - 1:QBLK], 0.0)
                    dve.drain()

                def scale_weights(s, c):
                    q = slice(32 * A_ORDER[c], 32 * A_ORDER[c] + 32)
                    for half in range(2):
                        e = E[:, half, q, :]
                        last = dve.scalar_tensor_tensor(e, e, A_UP * DEN_UP,
                                                        scale[:, half, q].unsqueeze(2).broadcast_to([128, 32, BLK]),
                                                        ALU.mult, ALU.mult)
                    last.then_inc(s_scaled, 1)

                def lo_weights(s, c):
                    q = slice(32 * A_ORDER[c], 32 * A_ORDER[c] + 32)
                    dve.wait_ge(s_ahi, ONE + 3 * s + c + 1)
                    dve.wait_ge(s_scaled, ONE + 3 * s + c + 1)
                    dve.tensor_tensor(A4[:, :, q, 1, :], E[:, :, q, :], A4[:, :, q, 0, :], ALU.subtract)
                    dve.drain()
                    dve.tensor_copy(A4[:, :, q, 3, :], A4[:, :, q, 1, :]).then_inc(s_a4, 1)

                def weights_out(s, u):
                    _, half, q = weight_use(u)
                    b = (U_A + u) % TRN
                    dve.wait_ge(s_tr, turned(s, U_A + u))
                    dve.tensor_copy(A4T[:, half, q:q + 8, :].rearrange("p q d -> p (q d)"),
                                    tr[b][:, :].bitcast(F16)).then_inc(s_trout[b], 1)

                def lo_y(s, ck, half):
                    n = 2 * ck + half
                    t = ck // 2
                    dve.wait_ge(s_yhi, ONE + 32 * s + n + 1)
                    dve.wait_ge(s_out, ONE + 8 * s + max(t - 1, 0))
                    where = (slice(None), slice(HH * half, HH * (half + 1)), slice(64 * (ck % 2), 64 * (ck % 2) + 64))
                    dve.scalar_tensor_tensor(YL[t % 2][where], ring[n % RING][:, :].rearrange("p (h t) -> p h t", h=HH),
                                             Y_UP / (X_UP * A_UP), YH[t % 2][where], ALU.mult,
                                             ALU.subtract).then_inc(s_ylo, 1)

                def values_out(s, u):
                    dve.wait_ge(s_tr, turned(s, U_V + u))
                    if u == 1:
                        dve.wait_ge(s_y, ONE + 32 * s)
                    for o in range(2):
                        r = slice(64 * o, 64 * o + 64)
                        last = dve.tensor_copy(values[r, 8 * u:8 * u + 8, o, :],
                                               tr[(U_V + u) % TRN][r, :].bitcast(F16)
                                               .rearrange("p (q d) -> p q d", d=D))
                    last.then_inc(s_trout[(U_V + u) % TRN], 1)

                def update(s, t):
                    dve.wait_ge(s_out, ONE + 8 * s + t + 1)
                    xt = xs(s)[:, t, :]
                    dve.scalar_tensor_tensor(xt, sbk[t % 2][:, 0:D], att["undo"][:, 2:3], xt, ALU.mult,
                                             ALU.add).then_inc(s_x, 1)

                def entry(s, ahead):
                    for c in range(3):
                        for h in range(HEADS):
                            lo_xm(s, c, h)
                            if c == 0 and h in VALUES_AT and VALUES_AT.index(h) % 2 == 1:
                                values_out(s, VALUES_AT.index(h))
                            if c > 0 and h == 9:
                                shift(s, 2 * c - 2)
                            if c == 2 and h == 1:
                                shift(s, 1)
                            if c == 2 and h == 6:
                                add_up(s, 0)
                            if c == 2 and h == 12:
                                add_up(s, 1)
                    shift(s, 3)
                    add_up(s, 2)
                    shift(s, 4)
                    add_up(s, 3)
                    shift(s, 5)
                    add_up(s, 4)
                    add_up(s, 5)
                    split_sums(s)
                    all_levels(s)
                    reciprocals(s)
                    scale_weights(s, 0)
                    scale_weights(s, 1)
                    for c in range(3):
                        lo_weights(s, c)
                        if c == 0:
                            scale_weights(s, 2)
                        for u in range(4 * c, 4 * c + 4, 2):
                            weights_out(s, u)
                    for ck in range(16):
                        for half in range(2):
                            lo_y(s, ck, half)
                        if ck % 2 == 1 and ck >= 3:
                            update(s, ck // 2 - 1)
                        if ahead:
                            if ck == 0:
                                statistics(s + 1)
                            if ck == 2:
                                norm(s + 1)
                            if ck == 7:
                                pool_levels(s + 1)
                            if 9 <= ck <= 9 + LEVELS:
                                lo_keys(s + 1, ck - 9)
                    update(s, 7)
                    dve.drain()

                dve.memset(values[:, :, :, :], 0.0)
                dve.memset(keys[:, QBLK - 1:QBLK, :, :], 0.0)
                dve.memset(coarse_q[:, :, QBLK - FINE - 1:QBLK - FINE, :], 0.0)
                dve.tensor_copy(ident16[:, :], ident[:, :])
                dve.drain().then_inc(s_const, 1)
                statistics(0)
                norm(0)
                pool_levels(0)
                for l in range(LEVELS + 1):
                    lo_keys(0, l)
                with dve.Fori(0, NB - 1) as s:
                    entry(s, True)
                entry(NB - 1, False)
def macaron_kernel(nc, A, out, phases):
    with ExitStack() as ctx:
        def sb(name, shape, dt=F32):
            return ctx.enter_context(nc.sbuf_tensor(name, shape, dt))

        S = {"x": sb("x_all", [128, GROUPS, NB, D])}
        first, experts, others = [], [], []

        def load(name, shape, src, dt=F32, into=others):
            S[name] = sb(name, shape, dt)
            into.append((S[name], src))

        load("columns", [128, 6], A["columns"], into=first)
        load("ident", [128, 128], A["ident"], into=first)
        load("wqkv", [128, QKV], A["wqkvT"], into=first)
        load("wproj", [128, D], A["wprojT"], into=experts)
        load("wrouter", [128, EXPERTS], A["wrouterT"], into=experts)
        load("expert_ids", [128, EXPERTS], A["expert_ids"], into=experts)
        load("moe1", [128, EXPERTS * EXP_F], A["moe1"], into=experts)
        load("moe2", [128, CHUNKS * D], A["moe2"], into=experts)
        for i, n in enumerate(("lnw1", "lnb1", "lnw2", "lnb2")):
            S[n] = S["columns"][:, i:i + 1]
        S["minus_half"], S["epsilon"] = sb("minus_half", [128, GROUPS]), sb("epsilon", [128, GROUPS])
        s_first, s_experts, s_others = (ctx.enter_context(nc.semaphore(n)) for n in
                                        ("loaded_first", "loaded_experts", "loaded_others"))
        s_store = ctx.enter_context(nc.semaphore("stored"))
        s_const = ctx.enter_context(nc.semaphore("constants"))
        load_second_half(nc, ctx, A, S, load)
        load_attention(nc, ctx, A, S, load)
        S["lnw_rnn"], S["lnb_rnn"] = S["columns"][:, 4:5], S["columns"][:, 5:6]
        with nc.Block() as block:
            @block.sync
            def _(sp):
                for s in range(NB):
                    sp.dma_start(S["x"][:, :, s, :], A["x"][s].rearrange("(g p) d -> p g d", p=128)).then_inc(s_first, 16)
                for loads, signal in ((first, s_first), (experts, s_experts), (others, s_others)):
                    for dst, src in loads:
                        sp.dma_start(dst[tuple(slice(None) for _ in dst.shape)], src).then_inc(signal, 16)
                sp.wait_ge(s_first, 16 * (NB + len(first)))

            @block.vector
            def _(dve):
                dve.memset(S["minus_half"][:, :], -0.5)
                dve.memset(S["epsilon"][:, :], EPS).then_inc(s_const, 1)

        for i, ph in enumerate(phases):
            if ph != "ffn" or i > 0:
                with nc.Block() as block:
                    @block.sync
                    def _(sp):
                        sp.wait_ge(s_experts, 16 * len(experts))
                        sp.wait_ge(s_others, 16 * len(others))
            if ph == "ffn":
                causal_moe_ffn(nc, S, f"f{i}", s_experts, 16 * len(experts))
            if ph == "attn":
                hierarchical_attention(nc, A, S, f"h{i}")
            if ph == "second":
                binarize(nc, S)
                second_half(nc, S, "r")
        with nc.Block() as block:
            @block.sync
            def _(sp):
                for s in range(NB):
                    sp.dma_start(out[s].rearrange("(g p) d -> p g d", p=128), S["x"][:, :, s, :]).then_inc(s_store, 16)
                sp.wait_ge(s_store, 16 * NB)


PHASES = ("ffn", "attn", "ffn", "second")


def layouts(inputs):
    import numpy as np
    f = lambda n: np.asarray(inputs[n])
    kv = slice(0, 0)
    q = f("L0_ffn_qkv_weight")
    nq, nk = HEADS0 * HD0, KV_HEADS0 * HD0
    rep = HEADS0 // KV_HEADS0
    per_head = lambda w: np.repeat(w.reshape(KV_HEADS0, 1, HD0, D), rep, axis=1).reshape(HEADS0 * HD0, D)
    wq = np.concatenate([q[:nq], per_head(q[nq:nq + nk]), per_head(q[nq + nk:])], 0)
    cols = np.zeros((128, 6), np.float32)
    for i, n in enumerate(("L0_ffn_ln1_weight", "L0_ffn_ln1_bias", "L0_ffn_ln2_weight", "L0_ffn_ln2_bias",
                           "L1_attn_ln_w", "L1_attn_ln_b")):
        cols[:, i] = f(n)
    a = {
        "x": f("L0_attn_x"),
        "wqkvT": wq.T, "wprojT": f("L0_ffn_proj_weight").T, "wrouterT": f("L0_ffn_router_weight").T,
        "moe1": f("L0_ffn_moe_w1").transpose(1, 0, 2).reshape(D, EXPERTS * EXP_F),
        "moe2": f("L0_ffn_moe_w2").reshape(CHUNKS, 128, D).transpose(1, 0, 2).reshape(128, CHUNKS * D),
        "columns": cols,
        "ident": np.eye(128, dtype=np.float32),
        "expert_ids": np.tile(np.arange(EXPERTS, dtype=np.float32), (128, 1)),
    }
    a.update(layouts_second_half(f))
    a.update(attention_layouts(f))
    return {k: np.ascontiguousarray(v) for k, v in a.items()}


def kernel(phases=PHASES, **inputs):
    import concourse.bacc as bacc
    from concourse.bass_utils import run_bass_kernel_spmd

    arrays = layouts(inputs)
    nc = bacc.Bacc("TRN2", target_bir_lowering=False, num_devices=1)
    aps = {k: nc.dram_tensor(f"in_{k}", v.shape, mybir.dt.from_np(v.dtype), kind="ExternalInput").ap()
           for k, v in arrays.items()}
    out = nc.dram_tensor("out", (NB, SEQ, D), F32, kind="ExternalOutput").ap()
    macaron_kernel(nc, aps, out, phases)
    r = run_bass_kernel_spmd(nc, [{f"in_{k}": v for k, v in arrays.items()}], core_ids=[0])
    return r.results[0]["out"]
```

```python
import concourse.bass as bass
from concourse import mybir
from contextlib import ExitStack

F32 = mybir.dt.float32
F16 = mybir.dt.float16
U32 = mybir.dt.uint32
ALU = mybir.AluOpType
ACT = mybir.ActivationFunctionType
AX = mybir.AxisListType

NB, SEQ, D = 4, 1024, 128
GROUPS = SEQ // 128
EPS = 1e-5
MASKED = -1e30
ONE = 1
HEADS0, KV_HEADS0 = 16, 4
HD0 = D // HEADS0
QKV = 3 * D
PAIRS = NB * (NB + 1) // 2
EXPERTS, EXP_F, TOP_K = 8, 256, 2
CHUNKS = EXPERTS * EXP_F // 128
H_RING, UP_RING = 4, 3
FC = 4
STATE = 32


def causal_moe_ffn(nc, S, tag, s_weights, weights_loaded):
    x = S["x"]
    ident, lnw1, lnb1, lnw2, lnb2 = S["ident"], S["lnw1"], S["lnb1"], S["lnw2"], S["lnb2"]
    wqkv, wproj, wrouter, w1, w2 = S["wqkv"], S["wproj"], S["wrouter"], S["moe1"], S["moe2"]
    minus_half, epsilon, expert_ids = S["minus_half"], S["epsilon"], S["expert_ids"]
    with ExitStack() as ctx:
        def sb(name, shape, dt=F32):
            return ctx.enter_context(nc.sbuf_tensor(f"{tag}_{name}", shape, dt))

        def bank(name):
            return ctx.enter_context(nc.psum_tensor(f"{tag}_{name}", [128, 512], F32))

        sems = []

        def sem(name):
            sems.append(ctx.enter_context(nc.semaphore(f"{tag}_{name}")))
            return sems[-1]

        stats, mv = sb("stats", [128, NB, 6]), sb("mv", [128, NB, 2])
        stats2, mv2 = sb("stats2", [128, NB, 6]), sb("mv2", [128, NB, 2])
        roots, roots2 = sb("roots", [128, 5, NB]), sb("roots2", [128, 2, NB])
        hs = [sb(f"hs{i}", [128, NB, D]) for i in range(2)]
        xn1, xn2 = sb("xn1", [128, NB, D]), sb("xn2", [128, NB, D])
        ln1T, headsT = sb("ln1T", [128, NB * 128]), sb("headsT", [128, NB * 128])
        qkv = sb("qkv", [128, NB, QKV])
        pairs = sb("pairs", [128, PAIRS, D])
        pvs = sb("pvs", [128, PAIRS, D])
        scores = sb("scores", [128, NB, HEADS0, NB])
        shifted = sb("shifted", [128, NB, HEADS0, NB])
        probs = sb("probs", [128, NB, HEADS0, NB])
        small = sb("small", [128, 3, NB, HEADS0])
        after = sb("after", [128, NB, D])
        x2T = [sb(f"x2T{i}", [128, NB * 128]) for i in range(2)]
        shifted_g, gate = sb("shifted_g", [128, NB, EXPERTS]), sb("gate", [128, NB, EXPERTS])
        gsmall = sb("gsmall", [128, 3, NB])
        top, topf = sb("top", [128, NB, 8]), sb("topf", [128, NB, 8])
        topi = sb("topi", [128, NB, 8], U32)
        pick = sb("pick", [128, NB, TOP_K, EXPERTS])
        weight = [sb(f"weight{i}", [128, NB, EXPERTS]) for i in range(2)]
        hT = [sb(f"hT{i}", [128, NB * 128]) for i in range(H_RING)]

        up = [bank(f"up{i}") for i in range(UP_RING)]
        down = [bank(f"down{i}") for i in range(2)]
        qb = [bank(f"qkvb{i}") for i in range(2)]
        turn = bank("turn")

        s_stats, s_root = sem("stats_done"), sem("root_done")
        s_stats2, s_root2 = sem("stats2_done"), sem("root2_done")
        s_xn1, s_turn1, s_ln1T = sem("xn1_done"), sem("turned1"), sem("ln1T_done")
        s_q, s_qkv = sem("qkv_product"), sem("qkv_in_sbuf")
        s_pairs, s_shift, s_exp, s_heads = sem("pairs"), sem("scores_shifted"), sem("scores_exp"), sem("heads_done")
        s_turn2, s_headsT, s_proj = sem("turned2"), sem("headsT_done"), sem("proj_done")
        s_xn2, s_turn3, s_x2T = sem("xn2_done"), sem("turned3"), sem("x2T_done")
        s_logit, s_gshift, s_gexp = sem("logits_done"), sem("logits_shifted"), sem("logits_exp")
        s_up, s_h, s_down, s_add = sem("up_done"), sem("h_done"), sem("down_done"), sem("add_done")

        first = [sum(NB - u for u in range(t)) for t in range(NB)]

        def grp(t, g):
            return t[:, bass.ds(g, 1), :, :].rearrange("p a s d -> p (a s) d")

        with nc.Block() as block:
            @block.sync
            def _(sp):
                for s in sems:
                    sp.sem_inc(s, ONE)

            @block.gpsimd
            def _(pool):
                def power(out, in_):
                    pool.tensor_tensor(out, in_, minus_half[:, 0:NB], ALU.pow)
                    pool.drain()

                def a1(g):
                    pool.wait_ge(s_stats, ONE + g + 1)
                    pool.wait_ge(s_xn1, ONE + g)
                    var = mv[:, :, 1]
                    pool.tensor_tensor(roots[:, 0, :], var, epsilon[:, 0:NB], ALU.add)
                    pool.drain()
                    power(roots[:, 1, :], roots[:, 0, :])
                    pool.tensor_tensor(roots[:, 2, :], roots[:, 1, :], roots[:, 1, :], ALU.mult)
                    pool.drain()
                    pool.tensor_tensor(roots[:, 0, :], roots[:, 2, :], var, ALU.mult)
                    pool.drain()
                    pool.tensor_scalar(roots[:, 2, :], roots[:, 0, :], EPS, None, ALU.add)
                    pool.drain()
                    power(roots[:, 3, :], roots[:, 2, :])
                    pool.tensor_tensor(roots[:, 4, :], roots[:, 3, :], roots[:, 1, :], ALU.mult).then_inc(s_root, 1)

                def a2(g):
                    pool.wait_ge(s_stats2, ONE + g + 1)
                    pool.wait_ge(s_xn2, ONE + g)
                    pool.tensor_tensor(roots2[:, 0, :], mv2[:, :, 1], epsilon[:, 0:NB], ALU.add)
                    pool.drain()
                    pool.tensor_tensor(roots2[:, 1, :], roots2[:, 0, :], minus_half[:, 0:NB],
                                       ALU.pow).then_inc(s_root2, 1)

                def query_key(g):
                    pool.wait_ge(s_qkv, ONE + NB * (g + 1))
                    pool.wait_ge(s_shift, ONE + g)
                    for t in range(NB):
                        n = NB - t
                        last = pool.tensor_tensor(pairs[:, first[t]:first[t] + n, :], qkv[:, t:NB, 0:D],
                                                  qkv[:, t, D:2 * D].unsqueeze(1).broadcast_to([128, n, D]), ALU.mult)
                    last.then_inc(s_pairs, 1)

                a1(0)
                query_key(0)
                with pool.Fori(0, GROUPS - 1) as g:
                    a1(g + 1)
                    a2(g)
                    query_key(g + 1)
                a2(GROUPS - 1)

            @block.scalar
            def _(act):
                def a_ln1T(g):
                    act.wait_ge(s_turn1, ONE + g + 1)
                    act.wait_ge(s_q, ONE + NB * g)
                    nc.scalar.activation(ln1T[:, :], qb[1][:, :], ACT.Identity, bias=lnb1[:, :],
                                         scale=lnw1[:, :]).then_inc(s_ln1T, 1)

                def a_qkv(g):
                    act.wait_ge(s_heads, ONE + g)
                    for s in range(NB):
                        act.wait_ge(s_q, ONE + NB * g + s + 1)
                        nc.scalar.activation(qkv[:, s, :], qb[s % 2][:, 0:QKV], ACT.Copy).then_inc(s_qkv, 1)

                def a_exp(g):
                    act.wait_ge(s_shift, ONE + g + 1)
                    nc.scalar.activation(probs[:, :, :, :], shifted[:, :, :, :], ACT.Exp,
                                         scale=HD0 ** -0.5).then_inc(s_exp, 1)

                def a_headsT(g):
                    act.wait_ge(s_turn2, ONE + g + 1)
                    act.wait_ge(s_proj, ONE + g)
                    nc.scalar.activation(headsT[:, :], turn[:, :], ACT.Copy).then_inc(s_headsT, 1)

                def a_x2T(g, b):
                    act.wait_ge(s_turn3, ONE + g + 1)
                    nc.scalar.activation(x2T[b][:, :], turn[:, :], ACT.Identity, bias=lnb2[:, :],
                                         scale=lnw2[:, :]).then_inc(s_x2T, 1)

                def a_gexp(g):
                    act.wait_ge(s_gshift, ONE + g + 1)
                    nc.scalar.activation(gate[:, :, :], shifted_g[:, :, :], ACT.Exp).then_inc(s_gexp, 1)

                def gelu(g, c):
                    act.wait_ge(s_up, ONE + CHUNKS * g + c + 1)
                    act.wait_ge(s_down, ONE + EXPERTS * g + (max(c - H_RING, -2)) // 2 + 1)
                    nc.scalar.activation(hT[c % H_RING][:, :], up[c % UP_RING][:, :],
                                         ACT.Gelu_apprx_tanh).then_inc(s_h, 1)

                def between(g, b, c, front, back):
                    if c == 7 and back:
                        a_headsT(g + 1)
                    if c == 9 and front:
                        a_ln1T(g + 2)
                    if c == 11 and front:
                        a_qkv(g + 2)
                    if c == 13 and back:
                        a_x2T(g + 1, 1 - b)
                    if c == 15 and front:
                        a_exp(g + 2)
                    if c == 15 and back:
                        a_gexp(g + 1)

                def group(g, b, front, back):
                    for c in range(CHUNKS):
                        gelu(g, c)
                        between(g, b, c, front, back)

                a_ln1T(0)
                a_qkv(0)
                a_exp(0)
                for c in range(CHUNKS):
                    between(-1, 1, c, True, True)
                with act.Fori(0, GROUPS // 2 - 1) as i:
                    group(2 * i, 0, True, True)
                    group(2 * i + 1, 1, True, True)
                group(GROUPS - 2, 0, False, True)
                group(GROUPS - 1, 1, False, False)

            @block.tensor
            def _(pe):
                def turn_tiles(src, signal, bank=turn):
                    for s in range(NB):
                        last = nc.tensor.transpose(bank[:, s * 128:(s + 1) * 128], src[:, s, :], ident[:, :])
                    last.then_inc(signal, 1)

                def p_turn1(g):
                    pe.wait_ge(s_xn1, ONE + g + 1)
                    pe.wait_ge(s_qkv, ONE + NB * g)
                    turn_tiles(xn1, s_turn1, qb[1])

                def p_qkv(g):
                    pe.wait_ge(s_ln1T, ONE + g + 1)
                    for s in range(NB):
                        pe.wait_ge(s_qkv, ONE + NB * g + max(s - 1, 0))
                        nc.tensor.matmul(qb[s % 2][:, 0:QKV], ln1T[:, s * 128:(s + 1) * 128], wqkv[:, :],
                                         start=True, stop=True).then_inc(s_q, 1)

                def p_turn2(g):
                    pe.wait_ge(s_heads, ONE + g + 1)
                    pe.wait_ge(s_gshift, ONE + g)
                    turn_tiles(pvs[:, 0:NB, :], s_turn2)

                def p_proj(g):
                    pe.wait_ge(s_headsT, ONE + g + 1)
                    for s in range(NB):
                        last = nc.tensor.matmul(turn[:, s * 128:(s + 1) * 128], headsT[:, s * 128:(s + 1) * 128],
                                                wproj[:, :], start=True, stop=True)
                    last.then_inc(s_proj, 1)

                def p_turn3(g):
                    pe.wait_ge(s_xn2, ONE + g + 1)
                    turn_tiles(xn2, s_turn3)

                def p_router(g, b):
                    pe.wait_ge(s_x2T, ONE + g + 1)
                    for s in range(NB):
                        last = nc.tensor.matmul(turn[:, s * EXPERTS:(s + 1) * EXPERTS],
                                                x2T[b][:, s * 128:(s + 1) * 128], wrouter[:, :],
                                                start=True, stop=True)
                    last.then_inc(s_logit, 1)

                def up_products(g, b, e):
                    for c in (2 * e, 2 * e + 1):
                        pe.wait_ge(s_h, ONE + CHUNKS * g + max(c - UP_RING + 1, 0))
                        nc.tensor.matmul(up[c % UP_RING][:, :], w1[:, c * 128:(c + 1) * 128], x2T[b][:, :],
                                         start=True, stop=True).then_inc(s_up, 1)

                def down_products(g, e):
                    pe.wait_ge(s_h, ONE + CHUNKS * g + 2 * e + 2)
                    pe.wait_ge(s_add, ONE + EXPERTS * g + max(e - 1, 0))
                    for s in range(NB):
                        for c in (2 * e, 2 * e + 1):
                            last = nc.tensor.matmul(down[e % 2][:, s * 128:(s + 1) * 128],
                                                    hT[c % H_RING][:, s * 128:(s + 1) * 128],
                                                    w2[:, c * 128:(c + 1) * 128],
                                                    start=(c % 2 == 0), stop=(c % 2 == 1))
                    last.then_inc(s_down, 1)

                def between(g, b, e, front, back):
                    if e == 2 and back:
                        p_turn2(g + 1)
                    if e == 3 and back:
                        p_proj(g + 1)
                    if e == 3 and front:
                        p_turn1(g + 2)
                    if e == 4 and front:
                        p_qkv(g + 2)
                    if e == 5 and back:
                        p_turn3(g + 1)
                    if e == 6 and back:
                        p_router(g + 1, 1 - b)

                def group(g, b, front, back):
                    up_products(g, b, 0)
                    for e in range(EXPERTS):
                        if e + 1 < EXPERTS:
                            up_products(g, b, e + 1)
                        down_products(g, e)
                        between(g, b, e, front, back)

                p_turn1(0)
                p_qkv(0)
                pe.wait_ge(s_weights, weights_loaded)
                for e in range(EXPERTS):
                    between(-1, 1, e, True, True)
                with pe.Fori(0, GROUPS // 2 - 1) as i:
                    group(2 * i, 0, True, True)
                    group(2 * i + 1, 1, True, True)
                group(GROUPS - 2, 0, False, True)
                group(GROUPS - 1, 1, False, False)

            @block.vector
            def _(dve):
                def v_stats(g):
                    xg = grp(x, g)
                    for s in range(NB):
                        dve.bn_stats(stats[:, s, :], xg[:, s, :])
                    dve.drain()
                    for s in range(NB):
                        last = dve.bn_aggr(mv[:, s, :], stats[:, s, :])
                    last.then_inc(s_stats, 1)

                def v_norm1(g, b):
                    dve.wait_ge(s_root, ONE + g + 1)
                    dve.wait_ge(s_turn1, ONE + g)
                    xg = grp(x, g)
                    for s in range(NB):
                        dve.tensor_scalar(hs[b][:, s, :], xg[:, s, :], mv[:, s, 0:1], roots[:, 1, s:s + 1],
                                          ALU.subtract, ALU.mult)
                    for s in range(NB):
                        last = dve.tensor_scalar(xn1[:, s, :], xg[:, s, :], mv[:, s, 0:1], roots[:, 4, s:s + 1],
                                                 ALU.subtract, ALU.mult)
                    last.then_inc(s_xn1, 1)

                def v_scores(g):
                    dve.drain()
                    dve.wait_ge(s_pairs, ONE + g + 1)
                    for t in range(NB):
                        n = NB - t
                        dve.tensor_reduce(scores[:, t:NB, :, t],
                                          pairs[:, first[t]:first[t] + n, :].rearrange("p s (h d) -> p s h d", d=HD0),
                                          AX.X, ALU.add)

                def v_shift(g):
                    dve.drain()
                    dve.tensor_reduce(small[:, 0, :, :], scores[:, :, :, :], AX.X, ALU.max)
                    dve.drain()
                    dve.tensor_tensor(shifted[:, :, :, :], scores[:, :, :, :],
                                      small[:, 0, :, :].unsqueeze(3).broadcast_to([128, NB, HEADS0, NB]),
                                      ALU.subtract).then_inc(s_shift, 1)

                def v_values(g):
                    dve.wait_ge(s_exp, ONE + g + 1)
                    dve.wait_ge(s_turn2, ONE + g)
                    dve.tensor_reduce(small[:, 1, :, :], probs[:, :, :, :], AX.X, ALU.add)
                    dve.drain()
                    dve.reciprocal(small[:, 2, :, :], small[:, 1, :, :])
                    v_products(g, 0)

                def v_products(g, t):
                    for s in range(t, NB):
                        dve.tensor_tensor(
                            pvs[:, first[t] + s - t, :].rearrange("p (h d) -> p h d", d=HD0),
                            probs[:, s, :, t].unsqueeze(2).broadcast_to([128, HEADS0, HD0]),
                            qkv[:, t, 2 * D:3 * D].rearrange("p (h d) -> p h d", d=HD0), ALU.mult)

                def v_heads(g):
                    for t in range(1, NB):
                        v_products(g, t)
                    dve.drain()
                    for t in range(1, NB):
                        n = NB - t
                        dve.tensor_tensor(pvs[:, t:NB, :], pvs[:, t:NB, :], pvs[:, first[t]:first[t] + n, :], ALU.add)
                        dve.drain()
                    out = pvs[:, 0:NB, :].rearrange("p s (h d) -> p (s h) d", d=HD0)
                    dve.tensor_tensor(out, out,
                                      small[:, 2, :, :].rearrange("p s h -> p (s h)").unsqueeze(2)
                                      .broadcast_to([128, NB * HEADS0, HD0]), ALU.mult).then_inc(s_heads, 1)

                def v_after(g, b):
                    dve.wait_ge(s_proj, ONE + g + 1)
                    dve.tensor_tensor(after[:, :, :], turn[:, :].rearrange("p (s d) -> p s d", d=D),
                                      hs[b][:, :, :], ALU.add)
                    dve.drain()
                    for s in range(NB):
                        dve.bn_stats(stats2[:, s, :], after[:, s, :])
                    dve.drain()
                    for s in range(NB):
                        last = dve.bn_aggr(mv2[:, s, :], stats2[:, s, :])
                    last.then_inc(s_stats2, 1)

                def v_norm2(g):
                    dve.wait_ge(s_root2, ONE + g + 1)
                    dve.wait_ge(s_turn3, ONE + g)
                    for s in range(NB):
                        last = dve.tensor_scalar(xn2[:, s, :], after[:, s, :], mv2[:, s, 0:1],
                                                 roots2[:, 1, s:s + 1], ALU.subtract, ALU.mult)
                    last.then_inc(s_xn2, 1)

                def v_logits(g):
                    dve.wait_ge(s_logit, ONE + g + 1)
                    logits = turn[:, 0:NB * EXPERTS].rearrange("p (s e) -> p s e", e=EXPERTS)
                    dve.tensor_reduce(gsmall[:, 0, :], logits, AX.X, ALU.max)
                    dve.drain()
                    dve.tensor_tensor(shifted_g[:, :, :], logits,
                                      gsmall[:, 0, :].unsqueeze(2).broadcast_to([128, NB, EXPERTS]),
                                      ALU.subtract).then_inc(s_gshift, 1)

                def v_weights(g, b):
                    dve.wait_ge(s_gexp, ONE + g + 1)
                    dve.tensor_reduce(gsmall[:, 1, :], gate[:, :, :], AX.X, ALU.add)
                    dve.drain()
                    dve.reciprocal(gsmall[:, 2, :], gsmall[:, 1, :])
                    dve.drain()
                    dve.scalar_tensor_tensor(gate[:, :, :], gate[:, :, :], 0.5,
                                             gsmall[:, 2, :].unsqueeze(2).broadcast_to([128, NB, EXPERTS]),
                                             ALU.mult, ALU.mult)
                    dve.drain()
                    for s in range(NB):
                        dve.max(top[:, s, :], gate[:, s, :])
                    dve.drain()
                    for s in range(NB):
                        dve.max_index(topi[:, s, :], top[:, s, :], gate[:, s, :])
                    dve.drain()
                    dve.tensor_copy(topf[:, :, :], topi[:, :, :])
                    dve.drain()
                    ids = expert_ids[:, :].unsqueeze(1).unsqueeze(1).broadcast_to([128, NB, TOP_K, EXPERTS])
                    best = lambda t: t[:, :, 0:TOP_K].unsqueeze(3).broadcast_to([128, NB, TOP_K, EXPERTS])
                    dve.tensor_tensor(pick[:, :, :, :], ids, best(topf), ALU.is_equal)
                    dve.drain()
                    dve.tensor_tensor(pick[:, :, :, :], pick[:, :, :, :], best(top), ALU.mult)
                    dve.drain()
                    dve.tensor_tensor(weight[b][:, :, :], pick[:, :, 0, :], pick[:, :, 1, :], ALU.add)
                    dve.drain()

                def add_expert(g, b, e):
                    dve.wait_ge(s_down, ONE + EXPERTS * g + e + 1)
                    dve.wait_ge(s_add, ONE + EXPERTS * g + e)
                    xg = grp(x, g)
                    for s in range(NB):
                        last = dve.scalar_tensor_tensor(xg[:, s, :], down[e % 2][:, s * 128:(s + 1) * 128],
                                                        weight[b][:, s, e:e + 1], xg[:, s, :],
                                                        ALU.mult, ALU.add)
                    last.then_inc(s_add, 1)

                def residual(g):
                    xg = grp(x, g)
                    dve.scalar_tensor_tensor(xg, after[:, :, :], 0.5, xg, ALU.mult, ALU.add)
                    dve.drain()

                def between(g, b, e, front, back):
                    if e == 0 and back:
                        v_values(g + 1)
                    if e == 1 and back:
                        v_heads(g + 1)
                    if e == 2 and front:
                        v_norm1(g + 2, b)
                    if e == 3 and back:
                        v_after(g + 1, 1 - b)
                    if e == 4 and back:
                        v_norm2(g + 1)
                        residual(g + 1)
                    if e == 5 and front:
                        v_scores(g + 2)
                    if e == 6 and front:
                        v_shift(g + 2)
                    if e == 6 and back:
                        v_logits(g + 1)
                    if e == 7 and back:
                        v_weights(g + 1, 1 - b)

                def group(g, b, front, back):
                    if front:
                        v_stats(g + 2)
                    for e in range(EXPERTS):
                        add_expert(g, b, e)
                        between(g, b, e, front, back)

                dve.memset(scores[:, :, :, :], MASKED)
                dve.drain()
                v_stats(0)
                v_norm1(0, 0)
                v_scores(0)
                v_shift(0)
                dve.wait_ge(s_weights, weights_loaded)
                v_stats(1)
                for e in range(EXPERTS):
                    between(-1, 1, e, True, True)
                with dve.Fori(0, GROUPS // 2 - 1) as i:
                    group(2 * i, 0, True, True)
                    group(2 * i + 1, 1, True, True)
                group(GROUPS - 2, 0, False, True)
                group(GROUPS - 1, 1, False, False)
def load_second_half(nc, ctx, A, S, load):
    load("bin1", [128, FC * D], A["bin1"])
    load("bin2", [128, FC * 128], A["bin2"])
    load("rnnA", [128, STATE], A["rnnA"])
    load("rnnB", [D, STATE], A["rnnB"])
    load("rnnC", [STATE, D], A["rnnC"])
    load("rnnD", [128, D], A["rnnD"])
    load("mlp1", [128, FC * 128], A["mlp1"])
    load("mlp2", [128, FC * D], A["mlp2"])
    load("chunk_bias", [128, 2 * FC], A["chunk_bias"])
    load("rows", [128, 4, D], A["rows"].partition_broadcast(128))


def layouts_second_half(f):
    import numpy as np
    chunks_first = lambda w: w.reshape(FC, 128, -1).transpose(1, 0, 2).reshape(128, -1)
    return {
        "bin1": chunks_first(f("L1_ffn_w1")), "bin2": f("L1_ffn_w2"),
        "rnnA": np.pad(f("L1_attn_A").T, ((0, 128 - STATE), (0, 0))), "rnnB": f("L1_attn_Bm").T, "rnnC": f("L1_attn_C").T,
        "rnnD": f("L1_attn_D").T,
        "mlp1": f("L1_attn_W1").T, "mlp2": chunks_first(f("L1_attn_W2").T),
        "chunk_bias": np.concatenate([f("L1_ffn_b1").reshape(FC, 128).T, f("L1_attn_b1").reshape(FC, 128).T], 1),
        "rows": np.stack([f("L1_attn_ln_w"), f("L1_attn_ln_b"), f("L1_attn_b2"), f("L1_ffn_b2")]),
    }


def binarize(nc, S):
    with ExitStack() as ctx:
        sgn = ctx.enter_context(nc.sbuf_tensor("sgn", [128, 2, FC, 128], F32))
        alpha = ctx.enter_context(nc.sbuf_tensor("alpha", [128, FC + 1], F32))
        banks = [ctx.enter_context(nc.psum_tensor(f"bin_turn{i}", [128, 512], F32)) for i in range(2)]
        s_sign, s_bin, s_turn = (ctx.enter_context(nc.semaphore(n)) for n in ("signs", "binarised", "bin_turned"))
        w1 = S["bin1"][:, :].rearrange("p (c d) -> p c d", d=D)
        w2 = S["bin2"][:, :].rearrange("p (c h) -> p c h", h=128)
        with nc.Block() as block:
            @block.scalar
            def _(act):
                for i, w in enumerate((w1, w2)):
                    nc.scalar.activation(sgn[:, i, :, :], w, ACT.Sign).then_inc(s_sign, 1)

            @block.vector
            def _(dve):
                dve.tensor_reduce(alpha[:, 0:FC], w1, AX.X, ALU.add, apply_absolute_value=True)
                dve.tensor_reduce(alpha[:, FC:FC + 1], w2, AX.XY, ALU.add, apply_absolute_value=True)
                dve.drain()
                dve.tensor_scalar(alpha[:, 0:FC], alpha[:, 0:FC], 1.0 / D, None, ALU.mult)
                dve.tensor_scalar(alpha[:, FC:FC + 1], alpha[:, FC:FC + 1], 1.0 / (FC * 128), None, ALU.mult)
                dve.drain()
                dve.wait_ge(s_sign, 2)
                for i, w in enumerate((w1, w2)):
                    for c in range(FC):
                        a = alpha[:, c:c + 1] if i == 0 else alpha[:, FC:FC + 1]
                        dve.scalar_tensor_tensor(sgn[:, i, c, :], sgn[:, i, c, :], a, w[:, c, :],
                                                 ALU.mult, ALU.subtract)
                dve.drain()
                for i, w in enumerate((w1, w2)):
                    dve.tensor_tensor(sgn[:, i, :, :], sgn[:, i, :, :], w, ALU.add).then_inc(s_bin, 1)
                rows = S["rows"]
                dve.tensor_tensor(rows[:, 1, :], rows[:, 1, :], rows[:, 2, :], ALU.add)
                dve.tensor_scalar(rows[:, 3, :], rows[:, 3, :], 0.5, None, ALU.mult)
                for i, n in enumerate(("bin1", "bin2")):
                    dve.wait_ge(s_turn, i + 1)
                    dve.tensor_copy(S[n][:, :], banks[i][:, :])

            @block.tensor
            def _(pe):
                for i in range(2):
                    pe.wait_ge(s_bin, i + 1)
                    for c in range(FC):
                        last = nc.tensor.transpose(banks[i][:, c * 128:(c + 1) * 128], sgn[:, i, c, :],
                                                   S["ident"][:, :])
                    last.then_inc(s_turn, 1)


def second_half(nc, S, out, s_store, tag):
    x = S["x"]
    ident, rows, bias = S["ident"], S["rows"], S["chunk_bias"]
    rnnA, rnnB, rnnC, rnnD = S["rnnA"], S["rnnB"], S["rnnC"], S["rnnD"]
    minus_half = S["minus_half"]
    with ExitStack() as ctx:
        def sb(name, shape, dt=F32):
            return ctx.enter_context(nc.sbuf_tensor(f"{tag}_{name}", shape, dt))

        def bank(name):
            return ctx.enter_context(nc.psum_tensor(f"{tag}_{name}", [128, 512], F32))

        sems = []

        def sem(name):
            sems.append(ctx.enter_context(nc.semaphore(f"{tag}_{name}")))
            return sems[-1]

        NORMS = ("a", "p", "r", "z")
        FFNS = ("a", "r", "z")
        stats = {k: sb(f"stats_{k}", [128, NB, 6]) for k in NORMS}
        mv = {k: sb(f"mv_{k}", [128, NB, 2]) for k in NORMS}
        root = {k: sb(f"root_{k}", [128, 2, NB]) for k in NORMS}
        xn = {k: [sb(f"xn_{k}", [128, NB, D])] * 2 for k in ("a", "r", "z")}
        xn["p"] = [sb(f"xn_p{i}", [128, NB, D]) for i in range(2)]
        nT = {k: [sb(f"nT_{k}", [128, 512])] * 2 for k in ("a", "r", "z")}
        nT["p"] = [sb(f"nT_p{i}", [128, 512]) for i in range(2)]
        state = [sb(f"state{i}", [128, 512]) for i in range(2)]
        mixed = sb("mixed", [128, NB, D])
        resid = sb("resid", [128, NB, D])
        h_pre = [sb(f"h_pre{c}", [128, 512]) for c in range(FC)]
        h_post = [sb(f"h_post{c}", [128, 512]) for c in range(FC)]
        H = {"a": h_pre, "r": h_post, "z": h_post}
        scan = [bank(f"scan{i}") for i in range(2)]
        pre_misc, post_misc = bank("pre_misc"), bank("post_misc")
        up_pre, up_post = [bank(f"up_pre{i}") for i in range(2)], [bank(f"up_post{i}") for i in range(2)]
        MISC = {"a": pre_misc, "p": pre_misc, "r": post_misc, "z": post_misc}
        UP = {"a": up_pre, "r": up_post, "z": up_post + up_pre}
        W1 = {"a": S["bin1"], "r": S["mlp1"], "z": S["bin1"]}
        W2 = {"a": S["bin2"], "r": S["mlp2"], "z": S["bin2"]}
        BIAS = {"a": 0, "r": FC, "z": 0}

        s_stats = {k: sem(f"stats_{k}") for k in NORMS}
        s_root = {k: sem(f"root_{k}") for k in NORMS}
        s_xn = {k: sem(f"xn_{k}") for k in NORMS}
        s_turn = {k: sem(f"turned_{k}") for k in NORMS}
        s_nT = {k: sem(f"nT_{k}") for k in NORMS}
        s_up = {k: sem(f"up_{k}") for k in FFNS}
        s_h = {k: sem(f"h_{k}") for k in FFNS}
        s_down = {k: sem(f"down_{k}") for k in FFNS}
        s_x = {k: sem(f"x_{k}") for k in FFNS}
        s_step, s_tanh, s_out, s_zero = sem("step_product"), sem("tanh_done"), sem("mixed_product"), sem("zero_state")

        def grp(g):
            return x[:, bass.ds(g, 1), :, :].rearrange("p a s d -> p (a s) d")

        with nc.Block() as block:
            @block.sync
            def _(sp):
                for s in sems:
                    sp.sem_inc(s, ONE)
                for g in range(GROUPS):
                    sp.wait_ge(s_x["z"], ONE + g + 1)
                    sp.dma_start(out[:, 128 * g:128 * (g + 1), :].rearrange("s p d -> p s d"),
                                 x[:, g, :, :]).then_inc(s_store, 16)
                sp.wait_ge(s_store, 16 * GROUPS)

            @block.gpsimd
            def _(pool):
                def rsqrt(k, g):
                    pool.wait_ge(s_stats[k], ONE + g + 1)
                    pool.wait_ge(s_xn[k], ONE + g)
                    pool.tensor_tensor(root[k][:, 0, :], mv[k][:, :, 1], S["epsilon"][:, 0:NB], ALU.add)
                    pool.drain()
                    pool.tensor_tensor(root[k][:, 1, :], root[k][:, 0, :], minus_half[:, 0:NB],
                                       ALU.pow).then_inc(s_root[k], 1)

                def body(g, post, pre):
                    if pre:
                        rsqrt("a", g + 1)
                    if post:
                        rsqrt("r", g - 1)
                        rsqrt("z", g - 1)
                    if pre:
                        rsqrt("p", g + 1)

                body(-1, False, True)
                body(0, False, True)
                with pool.Fori(1, GROUPS - 1) as g:
                    body(g, True, True)
                body(GROUPS - 1, True, False)
                body(GROUPS, True, False)

            @block.vector
            def _(dve):
                def v_stats(k, src):
                    for s in range(NB):
                        dve.bn_stats(stats[k][:, s, :], src[:, s, :])
                    dve.drain()
                    for s in range(NB):
                        last = dve.bn_aggr(mv[k][:, s, :], stats[k][:, s, :])
                    last.then_inc(s_stats[k], 1)

                def v_norm(k, g, b, src):
                    dve.wait_ge(s_root[k], ONE + g + 1)
                    dve.wait_ge(s_turn[k], ONE + g)
                    for s in range(NB):
                        last = dve.tensor_scalar(xn[k][b][:, s, :], src[:, s, :], mv[k][:, s, 0:1],
                                                 root[k][:, 1, s:s + 1], ALU.subtract, ALU.mult)
                    last.then_inc(s_xn[k], 1)

                def v_nT(k, g, b):
                    dve.wait_ge(s_turn[k], ONE + g + 1)
                    if k == "p":
                        dve.tensor_copy(nT[k][b][:, :].rearrange("p (t s) -> p s t", s=NB),
                                        MISC[k][:, :].rearrange("p (s t) -> p s t", s=NB)).then_inc(s_nT[k], 1)
                        return
                    dve.wait_ge(s_up[k], ONE + FC * g)
                    if k == "r":
                        dve.tensor_scalar(nT[k][b][:, :], MISC[k][:, :], S["lnw_rnn"], S["lnb_rnn"],
                                          ALU.mult, ALU.add).then_inc(s_nT[k], 1)
                    else:
                        dve.tensor_copy(nT[k][b][:, :], MISC[k][:, :]).then_inc(s_nT[k], 1)

                def v_update_bin(k, g):
                    dve.wait_ge(s_down[k], ONE + g + 1)
                    dve.scalar_tensor_tensor(resid[:, :, :], MISC[k][:, :].rearrange("p (s d) -> p s d", d=D), 0.5,
                                             rows[:, 3, :].unsqueeze(1).broadcast_to([128, NB, D]), ALU.mult, ALU.add)
                    dve.drain()
                    dve.tensor_tensor(grp(g), grp(g), resid[:, :, :], ALU.add).then_inc(s_x[k], 1)
                    dve.drain()

                def v_mix(g, b):
                    dve.wait_ge(s_out, ONE + g + 1)
                    dve.tensor_tensor(mixed[:, :, :], post_misc[:, :].rearrange("p (s d) -> p s d", d=D),
                                      xn["p"][b][:, :, :], ALU.add)
                    dve.drain()
                    v_stats("r", mixed)

                def v_resid(g):
                    y = xn["r"][0]
                    dve.drain()
                    dve.tensor_tensor(resid[:, :, :], y[:, :, :],
                                      rows[:, 0, :].unsqueeze(1).broadcast_to([128, NB, D]), ALU.mult)
                    dve.drain()
                    dve.tensor_tensor(resid[:, :, :], resid[:, :, :],
                                      rows[:, 1, :].unsqueeze(1).broadcast_to([128, NB, D]), ALU.add)
                    dve.drain()
                    dve.tensor_tensor(grp(g), grp(g), resid[:, :, :], ALU.add)
                    dve.drain()

                def v_update_mlp(g):
                    dve.wait_ge(s_down["r"], ONE + g + 1)
                    dve.tensor_tensor(grp(g), post_misc[:, :].rearrange("p (s d) -> p s d", d=D), grp(g),
                                      ALU.add).then_inc(s_x["r"], 1)
                    dve.drain()

                def pre_first(g, b):
                    v_stats("a", grp(g))
                    v_norm("a", g, b, grp(g))

                def body(g, b, post, pre):
                    if pre:
                        pre_first(g + 1, 1 - b)
                        v_nT("a", g + 1, 1 - b)
                    if post:
                        v_mix(g - 1, 1 - b)
                        v_norm("r", g - 1, 1 - b, mixed)
                        v_nT("r", g - 1, 1 - b)
                        v_resid(g - 1)
                    if post:
                        v_update_mlp(g - 1)
                        v_stats("z", grp(g - 1))
                        v_norm("z", g - 1, 1 - b, grp(g - 1))
                        v_nT("z", g - 1, 1 - b)
                    if pre:
                        v_update_bin("a", g + 1)
                        v_stats("p", grp(g + 1))
                        v_norm("p", g + 1, 1 - b, grp(g + 1))
                        v_nT("p", g + 1, 1 - b)
                    if post:
                        v_update_bin("z", g - 1)

                for half in state:
                    last = dve.memset(half[:, :], 0.0)
                last.then_inc(s_zero, 1)
                body(-1, 1, False, True)
                body(0, 0, False, True)
                with dve.Fori(0, GROUPS // 2 - 1) as i:
                    body(2 * i + 1, 1, True, True)
                    body(2 * i + 2, 0, True, True)
                body(GROUPS - 1, 1, True, False)
                body(GROUPS, 0, True, False)

            def up_piece(pe, k, g, b, i, last_z=None, groups_a=None):
                c, s = divmod(i, NB)
                if s == 0:
                    pe.wait_ge(s_nT[k], ONE + g + 1)
                    if k == "a" and c < 2:
                        if last_z is not None:
                            pe.wait_ge(s_h["z"], ONE + FC * last_z)
                    elif k == "r" and c < 2:
                        pe.wait_ge(s_h["z"], ONE + FC * g)
                    elif k == "z" and c < 2:
                        pe.wait_ge(s_h["r"], ONE + FC * (g + 1))
                    elif k == "z":
                        pe.wait_ge(s_h["a"], ONE + FC * groups_a)
                    else:
                        pe.wait_ge(s_h[k], ONE + FC * g + c - 1)
                ins = nc.tensor.matmul(UP[k][c % len(UP[k])][:, s * 128:(s + 1) * 128], W1[k][:, c * 128:(c + 1) * 128],
                                       nT[k][b][:, s * 128:(s + 1) * 128], start=True, stop=True)
                if s == NB - 1:
                    ins.then_inc(s_up[k], 1)

            def down_piece(pe, k, g, i):
                s, c = divmod(i, FC)
                if i == 0:
                    pe.wait_ge(s_h[k], ONE + FC * (g + 1))
                ins = nc.tensor.matmul(MISC[k][:, s * 128:(s + 1) * 128], H[k][c][:, s * 128:(s + 1) * 128],
                                       W2[k][:, c * 128:(c + 1) * 128], start=(c == 0), stop=(c == FC - 1))
                if i == NB * FC - 1:
                    ins.then_inc(s_down[k], 1)

            def turn_piece(pe, k, g, b, s):
                if s == 0:
                    pe.wait_ge(s_xn[k], ONE + g + 1)
                    if k == "a":
                        pe.wait_ge(s_nT["p"], ONE + g)
                ins = nc.tensor.transpose(MISC[k][:, s * 128:(s + 1) * 128], xn[k][b][:, s, :], ident[:, :])
                if s == NB - 1:
                    ins.then_inc(s_turn[k], 1)

            def input_piece(pe, g, b, s):
                if s == 0:
                    pe.wait_ge(s_nT["p"], ONE + g + 1)
                part = slice(128 * s, 128 * (s + 1))
                nc.tensor.matmul(scan[b][0:STATE, part], rnnB[:, :], nT["p"][b][:, part], start=(s == 0), stop=False,
                                 skip_group_check=True)

            def mix_piece(pe, g, b, i):
                s, second = divmod(i, 2)
                if i == 0:
                    pe.wait_ge(s_tanh, ONE + 128 * (g + 1))
                    pe.wait_ge(s_x["z"], ONE + g)
                lhs = (nT["p"][b][:, :] if second else state[b][0:STATE, :]).rearrange("p (t s) -> p s t", s=NB)[:, s, :]
                ins = nc.tensor.matmul(post_misc[:, s * 128:(s + 1) * 128], lhs, (rnnD if second else rnnC)[:, :],
                                       start=not second, stop=bool(second))
                if i == 2 * NB - 1:
                    ins.then_inc(s_out, 1)

            UP_A = [6, 7, 8, 9, 18, 19, 22, 23]
            UP_R = [16, 17, 20, 21, 24, 25, 26, 27]
            DOWN_A = [38, 39, 40, 41, 42, 43, 44, 45]

            def plan_post(pe, g, b, groups_a):
                p = [(2 + i // 2, mix_piece, (pe, g, b, i)) for i in range(2 * NB)]
                p += [(12 + s // 2, turn_piece, (pe, "r", g, b, s)) for s in range(NB)]
                p += [(UP_R[i // 2], up_piece, (pe, "r", g, b, i)) for i in range(16)]
                p += [(30 + i // 2, down_piece, (pe, "r", g, i)) for i in range(16)]
                p += [(46 + s // 2, turn_piece, (pe, "z", g, b, s)) for s in range(NB)]
                p += [(50 + i // 2, up_piece, (pe, "z", g, b, i, None, groups_a)) for i in range(16)]
                p += [((60 if i < 4 else 62) + i // 2, down_piece, (pe, "z", g, i)) for i in range(16)]
                return p

            def plan_pre(pe, g, b, last_z):
                p = [(s // 2, turn_piece, (pe, "a", g, b, s)) for s in range(NB)]
                p += [(UP_A[i // 2], up_piece, (pe, "a", g, b, i, last_z)) for i in range(16)]
                p += [(DOWN_A[i // 2], down_piece, (pe, "a", g, i)) for i in range(16)]
                p += [(62 + s // 2, turn_piece, (pe, "p", g, b, s)) for s in range(NB)]
                p += [(70 + s // 2, input_piece, (pe, g, b, s)) for s in range(NB)]
                return p

            @block.tensor
            def _(pe):
                def run(plan, t):
                    for at, f, args in plan:
                        if at == t:
                            f(*args)

                def body(g, b, post, pre):
                    plan = plan_post(pe, g - 1, 1 - b, g + 2 if pre else GROUPS) if post else []
                    plan += plan_pre(pe, g + 1, 1 - b, g - 1 if post else None) if pre else []
                    for t in range(128):
                        last = state[b][:, NB * (t - 1):NB * t] if t else state[1 - b][:, 512 - NB:512]
                        pe.wait_ge(s_tanh, ONE + 128 * g + t)
                        nc.tensor.matmul(scan[b][0:STATE, NB * t:NB * (t + 1)], rnnA[:, :], last, start=False,
                                         stop=(t == 127), skip_group_check=True).then_inc(s_step, 1)
                        run(plan, t)

                pre = plan_pre(pe, 0, 0, None)
                for t in range(128):
                    run(pre, t)
                pe.wait_ge(s_zero, ONE + 1)
                body(0, 0, False, True)
                with pe.Fori(0, GROUPS // 2 - 1) as i:
                    body(2 * i + 1, 1, True, True)
                    body(2 * i + 2, 0, True, True)
                body(GROUPS - 1, 1, True, False)
                post = plan_post(pe, GROUPS - 1, 1, GROUPS)
                for t in range(128):
                    run(post, t)

            @block.scalar
            def _(act):
                def gelu_piece(k, g, c, s):
                    if s == 0:
                        act.wait_ge(s_up[k], ONE + FC * g + c + 1)
                        if k == "z":
                            act.wait_ge(s_down["r"], ONE + g + 1)
                        else:
                            act.wait_ge(s_down["z" if k == "r" else "a"], ONE + g)
                    ins = nc.scalar.activation(H[k][c][:, s * 128:(s + 1) * 128],
                                               UP[k][c % len(UP[k])][:, s * 128:(s + 1) * 128], ACT.Gelu,
                                               bias=bias[:, BIAS[k] + c:BIAS[k] + c + 1])
                    if s == NB - 1:
                        ins.then_inc(s_h[k], 1)

                GELU_A, GELU_R = [8, 10, 20, 24], [18, 22, 26, 28]

                def plan_gelus(g_post, g_pre):
                    p = []
                    for c in range(FC):
                        for s in range(NB):
                            if g_post is not None:
                                p.append((GELU_R[c] + s // 2, ("r", g_post, c, s)))
                                p.append((52 + 2 * c + s // 2, ("z", g_post, c, s)))
                            if g_pre is not None:
                                p.append((GELU_A[c] + s // 2, ("a", g_pre, c, s)))
                    return p

                def run(plan, t):
                    for at, args in plan:
                        if at == t:
                            gelu_piece(*args)

                def body(g, b, post, pre):
                    plan = plan_gelus(g - 1 if post else None, g + 1 if pre else None)
                    if post:
                        act.wait_ge(s_out, ONE + g - 1)
                    for t in range(128):
                        act.wait_ge(s_step, ONE + 128 * g + t + 1)
                        nc.scalar.activation(state[b][0:STATE, NB * t:NB * (t + 1)], scan[b][0:STATE, NB * t:NB * (t + 1)],
                                             ACT.Tanh).then_inc(s_tanh, 1)
                        run(plan, t)

                plan = plan_gelus(None, 0)
                for t in range(128):
                    run(plan, t)
                body(0, 0, False, True)
                with act.Fori(0, GROUPS // 2 - 1) as i:
                    body(2 * i + 1, 1, True, True)
                    body(2 * i + 2, 0, True, True)
                body(GROUPS - 1, 1, True, False)
                plan = plan_gelus(GROUPS - 1, None)
                for t in range(128):
                    run(plan, t)
HEADS, HD, BLK, LEVELS = 16, 64, 16, 5
HH = HEADS // 2
FINE = SEQ // BLK
NBLK = [FINE // 2 ** (l + 1) for l in range(1, LEVELS + 1)]
BASE = [FINE + sum(NBLK[:l]) for l in range(LEVELS)]
QBLK = 96
assert BASE[-1] + NBLK[-1] == QBLK - 1
COLS = [SEQ // 2 ** l for l in range(LEVELS + 1)]
COL0 = [sum(COLS[:l]) for l in range(LEVELS + 1)]
X_UP, M_UP, A_UP, N_UP, Y_UP, DEN_UP = 16.0, 16.0, 256.0, 256.0, 64.0, 64.0
ATT_EPS = 1e-8
MASK0 = -3e38
LEAST = 1e-20
LOW = 32


def attention_layouts(f):
    import numpy as np
    w = f("L0_attn_w_qkv").reshape(3, HEADS, HD, D).transpose(0, 2, 1, 3).reshape(3, HD, HEADS * D)
    p = np.arange(128)
    head, i = p // BLK, p % BLK
    sel = np.zeros((128, 2, BLK, HEADS), np.float16)
    for half in range(2):
        sel[p, half, i, head + HH * half] = 1
    selT = sel.transpose(3, 1, 2, 0).reshape(HEADS, -1)
    own = np.zeros((128, 2, HEADS), np.float32)
    for half in range(2):
        own[p, half, head + HH * half] = 1
    return {
        "att_wq": w[0], "att_wk": w[1], "att_wv": w[2],
        "att_wo": f("L0_attn_w_out").T.reshape(HEADS, HD, D).transpose(1, 0, 2).reshape(HD, HEADS * D),
        "att_bias": f("L0_attn_b_out").reshape(1, D),
        "att_sel": sel.reshape(128, -1), "att_selT": np.concatenate([selT, np.zeros((LOW - HEADS, selT.shape[1]), np.float16), selT]),
        "att_own": own.reshape(128, -1),
        "att_mask": np.where(np.arange(BLK)[None, :] > i[:, None], MASK0, 0.0).astype(np.float32),
    }


def load_attention(nc, ctx, A, S, load):
    load("att_sel", [128, 2 * BLK * HEADS], A["att_sel"], F16)
    load("att_selT", [LOW + HEADS, 2 * BLK * 128], A["att_selT"], F16)
    load("att_own", [128, 2 * HEADS], A["att_own"])
    load("att_mask", [128, BLK], A["att_mask"])
    load("att_bias", [128, 1, D], A["att_bias"].partition_broadcast(128))


ATT_W = ("att_wq", "att_wk", "att_wv", "att_wo")


def attention_memory(nc, ctx, A, load):
    att = {n: ctx.enter_context(nc.sbuf_tensor("att_" + n, [128, HEADS * D], F16))
           for n in ("Mhi", "Mlo", "Nhi", "Nlo")}
    att["undo"] = ctx.enter_context(nc.sbuf_tensor("att_undo", [128, 4], F32))
    att["big"] = [ctx.enter_context(nc.sbuf_tensor(f"att_big{i}", [128, 2 * 32 * HEADS * BLK], F16)) for i in range(2)]
    att["values"] = ctx.enter_context(nc.sbuf_tensor("att_values", [128, QBLK // 2, 2, D], F16))
    for i, n in enumerate(ATT_W):
        att[n] = att["big"][0][0:HD, 4096 * i:4096 * (i + 1)].bitcast(F32)
        load(att[n], A[n])
    return att


def hierarchical_attention(nc, S, att):
    x, ident = S["x"], S["ident"]
    sel = S["att_sel"][:, :].rearrange("p (j h) -> p j h", h=HEADS)
    selT = S["att_selT"][:, :].rearrange("h (j p) -> h j p", p=128)
    with ExitStack() as ctx:
        sb = lambda n, shape, dt=F32: ctx.enter_context(nc.sbuf_tensor("at_" + n, shape, dt))
        bank = lambda n: ctx.enter_context(nc.psum_tensor("at_" + n, [128, 512], F32))
        sems = []

        def sem(n):
            sems.append(ctx.enter_context(nc.semaphore("at_" + n)))
            return sems[-1]

        stats, mv, root = sb("stats", [128, GROUPS, 6]), sb("mv", [128, GROUPS, 2]), sb("root", [128, 3, GROUPS])
        xn = sb("xn", [128, GROUPS, D])
        xT = sb("xT", [128, sum(COLS)])
        keys = sb("keys", [128, QBLK, 4, BLK], F16)
        coarse_q = sb("coarse_q", [128, 2, QBLK - FINE, BLK], F16)
        values = att["values"]
        big = att["big"]
        half_of = lambda t, i: t[:, i * 8192:(i + 1) * 8192].rearrange("p (q h i) -> p q h i", h=HEADS, i=BLK)
        XH, XL = ([half_of(t, i) for i in range(2)] for t in big)
        W4 = 2 * QBLK * 4 * BLK
        A4 = big[0][:, 0:W4].rearrange("p (a q e i) -> p a q e i", q=QBLK, e=4, i=BLK)
        A4T = big[1][:, 0:W4].rearrange("p (a q c) -> p a q c", a=2, c=128)
        tile_of = lambda t, i: t[:, W4 + i * HEADS * 128:W4 + (i + 1) * HEADS * 128].rearrange("p (h t) -> p h t", h=HEADS)
        YH, YL = ([tile_of(t, i) for i in range(2)] for t in big)
        den16 = big[0][0:LOW + HEADS, W4:W4 + BLK * QBLK].rearrange("h (i q) -> h i q", q=QBLK)
        den_hi, den_lo = den16[0:HEADS], den16[LOW:LOW + HEADS]
        logits = [sb(f"logits{i}", [128, 2, 16, BLK]) for i in range(2)]
        peaks = [sb(f"peaks{i}", [128, 2, 16]) for i in range(2)]
        E = sb("E", [128, 2, QBLK, BLK])
        sums, sums16 = sb("sums", [128, 2, QBLK]), sb("sums16", [128, 2, 2 * QBLK], F16)
        den = xn[0:HEADS, :, :].rearrange("h g d -> h (g d)")
        cden = sb("cden", [HEADS, BLK, QBLK - FINE])
        scale = sb("scale", [128, 2, QBLK])
        ident16 = sb("ident16", [128, 128], F16)
        N_AT = HEADS
        peak, allpeak, up = (sb(n, [128, 32]) for n in ("peak", "allpeak", "up"))
        own_peaks = sb("own_peaks", [128, 2, HEADS])

        RING = 4
        ring = [bank(f"ring{i}") for i in range(RING)]
        sbk = [bank(f"s{i}") for i in range(2)]
        tr = [bank(f"tr{i}") for i in range(2)] + ring[2:4]

        s_stats, s_root, s_xn = sem("stats"), sem("root"), sem("xn")
        s_tr, s_trout = sem("turned"), [sem(f"turn_out{i}") for i in range(len(tr))]
        s_xT, s_pool, s_khi, s_klo, s_keys = sem("rows_out"), sem("pooled"), sem("keys_hi"), sem("keys_lo"), sem("keys")
        s_xm, s_xhi, s_xlo = sem("xm"), sem("xm_hi"), sem("xm_lo")
        s_s, s_sread, s_sub, s_e = sem("logits"), sem("logits_read"), sem("logits_shifted"), sem("exp")
        s_sums, s_den, s_denread, s_cden = sem("sums"), sem("den"), sem("den_read"), sem("coarse_den_read")
        s_dall, s_dhi, s_d16, s_scaled = sem("den_all_levels"), sem("den_hi"), sem("den16"), sem("scaled")
        s_ahi, s_a4, s_y, s_yhi, s_ylo, s_out, s_x = (sem("a_hi"), sem("a4"), sem("y"), sem("y_hi"), sem("y_lo"),
                                                      sem("out"), sem("x"))
        s_const, s_bias = sem("const"), sem("bias")

        mn_banks = {"M": ring, "N": sbk + tr[0:2]}
        s_mm, s_peak, s_allpeak, s_up, s_hi, s_lo = (ctx.enter_context(nc.semaphore("at_" + n)) for n in
                                                     ("mn_products", "mn_peaks", "mn_all_peaks", "mn_factors",
                                                      "mn_hi", "mn_lo"))

        def mn_parts(k):
            if k == "M":
                return [(ring[h // 4], slice((h % 4) * D, (h % 4 + 1) * D), slice(h * D, (h + 1) * D), up[:, h:h + 1])
                        for h in range(HEADS)]
            return [(b, slice(0, 512), slice(512 * j, 512 * (j + 1)), up[:, N_AT + 4:N_AT + 5])
                    for j, b in enumerate(mn_banks[k])]

        U_X, U_V, U_R, U_A = 0, 2, 8, 9
        USES = U_A + 12
        BANK_OF = [u % 2 for u in range(U_A)] + [(u + 1) % 4 for u in range(USES - U_A)]
        BANK_USES = [BANK_OF.count(b) for b in range(len(tr))]
        A_ORDER = (2, 0, 1)
        VALUES_AT = (0, 2, 5, 8, 11, 14)

        def level(l, odd):
            v = xT[:, COL0[l]:COL0[l] + COLS[l]].rearrange("p (m o i) -> p m o i", o=2, i=BLK)
            return v[:, :, odd, :]

        def spots(t, l):
            step = 2 ** l
            v = t[:, :].rearrange("h (m o i r) -> h m o i r", o=2, i=BLK, r=step)
            return v[:, :, 1, :, step - 1]

        def den_parts():
            yield den[:, :].rearrange("h (q i) -> h q i", i=BLK), slice(0, FINE), DEN_UP
            for l in range(1, LEVELS + 1):
                yield spots(den, l), slice(BASE[l - 1], BASE[l - 1] + NBLK[l - 1]), DEN_UP * 2.0 ** -l

        def turned(s, u):
            return ONE + USES * s + u + 1

        def xs(s):
            return x[:, :, bass.ds(s, 1), :].rearrange("p g a d -> p g (a d)")

        def weight_use(u):
            c, r = divmod(u, 4)
            half, part = divmod(r, 2)
            return A_ORDER[c], half, 16 * A_ORDER[c] + 8 * part

        with nc.Block() as block:
            @block.sync
            def _(sp):
                for s in sems:
                    sp.sem_inc(s, ONE)

            @block.gpsimd
            def _(pool):
                def scales(s):
                    pool.wait_ge(s_stats, ONE + s + 1)
                    pool.wait_ge(s_xn, ONE + s)
                    pool.tensor_tensor(root[:, 0, :], mv[:, :, 1], S["epsilon"][:, 0:GROUPS], ALU.add)
                    pool.drain()
                    pool.tensor_tensor(root[:, 1, :], root[:, 0, :], S["minus_half"][:, 0:GROUPS], ALU.pow)
                    pool.drain()
                    pool.tensor_scalar(root[:, 2, :], root[:, 1, :], X_UP, None, ALU.mult).then_inc(s_root, 1)

                def pool_levels(s):
                    pool.wait_ge(s_xT, ONE + s + 1)
                    for l in range(1, LEVELS + 1):
                        v = xT[:, COL0[l - 1]:COL0[l - 1] + COLS[l - 1]].rearrange("p (t o) -> p t o", o=2)
                        last = pool.tensor_tensor(xT[:, COL0[l]:COL0[l] + COLS[l]], v[:, :, 0], v[:, :, 1], ALU.add)
                        if l < LEVELS:
                            pool.drain()
                    last.then_inc(s_pool, 1)
                    pool.tensor_tensor(xs(s), xs(s), S["att_bias"][:, :, :].broadcast_to([128, GROUPS, D]),
                                       ALU.add).then_inc(s_bias, 1)

                def all_peaks(i):
                    pool.wait_ge(s_peak, i + 1)
                    pool.partition_all_reduce(allpeak[:, 16 * i:16 * i + 16], peak[:, 16 * i:16 * i + 16], 128,
                                              bass.bass_isa.ReduceOp.max).then_inc(s_allpeak, 1)

                scales(0)
                all_peaks(0)
                pool_levels(0)
                all_peaks(1)
                with pool.Fori(0, NB - 1) as s:
                    scales(s + 1)
                    pool_levels(s + 1)

            @block.scalar
            def _(act):
                def rows_out(s):
                    for u in range(2):
                        act.wait_ge(s_tr, turned(s, U_X + u))
                        nc.scalar.activation(xT[:, 512 * u:512 * (u + 1)], tr[BANK_OF[U_X + u]][:, :], ACT.Copy)
                        nc.scalar.drain().then_inc(s_trout[BANK_OF[U_X + u]], 1)
                    act.sem_inc(s_xT, 1)

                def hi_keys(s, l):
                    if l == 0:
                        act.wait_ge(s_pool, ONE + s + 1)
                        act.wait_ge(s_s, ONE + 6 * s)
                        nc.scalar.activation(keys[:, 0:FINE, 0:2, :],
                                             xT[:, 0:SEQ].rearrange("p (q i) -> p q i", i=BLK).unsqueeze(2)
                                             .broadcast_to([128, FINE, 2, BLK]), ACT.Copy).then_inc(s_khi, 1)
                        return
                    n, b = NBLK[l - 1], BASE[l - 1]
                    nc.scalar.activation(keys[:, b:b + n, 0:2, :],
                                         level(l, 0).unsqueeze(2).broadcast_to([128, n, 2, BLK]),
                                         ACT.Copy, scale=2.0 ** -l)
                    nc.scalar.activation(coarse_q[:, 0, b - FINE:b - FINE + n, :], level(l, 1),
                                         ACT.Copy, scale=2.0 ** -l).then_inc(s_khi, 1)

                def values_out(s, u):
                    act.wait_ge(s_tr, turned(s, U_V + u))
                    if u == 0:
                        act.wait_ge(s_y, ONE + 32 * s)
                    for o in range(2):
                        r = slice(64 * o, 64 * o + 64)
                        last = nc.scalar.activation(values[r, 8 * u:8 * u + 8, o, :],
                                                    tr[BANK_OF[U_V + u]][r, :].bitcast(F16)
                                                    .rearrange("p (q d) -> p q d", d=D), ACT.Copy)
                    last.then_inc(s_trout[BANK_OF[U_V + u]], 1)

                def hi_xm(s, c, h):
                    if h == 0:
                        act.wait_ge(s_s, ONE + 6 * s + 2 * max(c - 1, 0))
                        if c == 0:
                            act.wait_ge(s_out, ONE + 8 * s)
                    n = HEADS * c + h
                    act.wait_ge(s_xm, ONE + 48 * s + n + 1)
                    nc.scalar.activation(XH[c % 2][:, :, h, :], ring[n % RING][:, :].rearrange("p (q i) -> p q i", i=BLK),
                                         ACT.Copy).then_inc(s_xhi, 1)

                def exps(s, k):
                    act.wait_ge(s_sub, ONE + 6 * s + k + 1)
                    act.wait_ge(s_a4, ONE + 3 * s)
                    for half in range(2):
                        last = nc.scalar.activation(E[:, half, 16 * k:16 * k + 16, :], logits[k % 2][:, half, :, :],
                                                    ACT.Exp, scale=att["undo"][:, half:half + 1])
                    last.then_inc(s_e, 1)

                def coarse_den(s):
                    act.wait_ge(s_den, ONE + 3 * (s + 1))
                    nc.scalar.activation(cden[:, :, :], ring[2][0:HEADS, :].rearrange("h (i q) -> h i q", i=BLK),
                                         ACT.Copy).then_inc(s_cden, 1)

                def hi_den(s):
                    act.wait_ge(s_dall, ONE + s + 1)
                    for src, q, up in den_parts():
                        nc.scalar.activation(den_hi[:, :, q].rearrange("h i q -> h q i"), src, ACT.Copy,
                                             scale=up).then_inc(s_dhi, 1)

                def hi_weights(s, c):
                    q = slice(32 * A_ORDER[c], 32 * A_ORDER[c] + 32)
                    act.wait_ge(s_scaled, ONE + 3 * s + c + 1)
                    nc.scalar.activation(A4[:, :, q, 0, :], E[:, :, q, :], ACT.Copy).then_inc(s_ahi, 1)

                def weights_out(s, u):
                    _, half, q = weight_use(u)
                    b = BANK_OF[U_A + u]
                    act.wait_ge(s_tr, turned(s, U_A + u))
                    nc.scalar.activation(A4T[:, half, q:q + 8, :].rearrange("p q d -> p (q d)"),
                                         tr[b][:, :].bitcast(F16), ACT.Copy).then_inc(s_trout[b], 1)

                def hi_y(s, ck, half):
                    n = 2 * ck + half
                    t = ck // 2
                    act.wait_ge(s_y, ONE + 32 * s + n + 1)
                    act.wait_ge(s_out, ONE + 8 * s + max(t - 1, 0))
                    nc.scalar.activation(YH[t % 2][:, HH * half:HH * (half + 1), 64 * (ck % 2):64 * (ck % 2) + 64],
                                         ring[n % RING][:, :].rearrange("p (h t) -> p h t", h=HH), ACT.Copy,
                                         scale=Y_UP / (X_UP * A_UP)).then_inc(s_yhi, 1)

                def keys_twice(s):
                    act.wait_ge(s_klo, ONE + s + 1)
                    nc.scalar.activation(keys[:, 0:QBLK - 1, 3, :], keys[:, 0:QBLK - 1, 2, :],
                                         ACT.Copy).then_inc(s_keys, 1)

                def entry(s, ahead):
                    for c in range(3):
                        for h in range(HEADS):
                            hi_xm(s, c, h)
                            if c == 0 and h in VALUES_AT and VALUES_AT.index(h) % 2 == 0:
                                values_out(s, VALUES_AT.index(h))
                            if c > 0 and h == 12:
                                exps(s, 2 * c - 2)
                            if c == 2 and h == 4:
                                exps(s, 1)
                    for k in (3, 4, 5):
                        exps(s, k)
                    coarse_den(s)
                    hi_den(s)
                    for c in range(3):
                        hi_weights(s, c)
                    for c in range(3):
                        for u in range(4 * c + 1, 4 * c + 4, 2):
                            weights_out(s, u)
                    for ck in range(16):
                        for half in range(2):
                            hi_y(s, ck, half)
                        if ahead:
                            if ck == 5:
                                rows_out(s + 1)
                            if 8 <= ck <= 8 + LEVELS:
                                hi_keys(s + 1, ck - 8)
                            if ck == 15:
                                keys_twice(s + 1)

                def hi_mn(i, k):
                    act.wait_ge(s_up, i + 1)
                    for b, cols, place, factor in mn_parts(k):
                        nc.scalar.activation(att[k + "hi"][:, place], b[:, cols], ACT.Copy,
                                             scale=factor).then_inc(s_hi, 1)

                act.wait_ge(s_const, ONE + 1)
                rows_out(0)
                hi_mn(0, "M")
                hi_mn(1, "N")
                for l in range(LEVELS + 1):
                    hi_keys(0, l)
                keys_twice(0)
                with act.Fori(0, NB - 1) as s:
                    entry(s, True)
                entry(NB - 1, False)

            @block.tensor
            def _(pe):
                def use(s, u):
                    b = BANK_OF[u]
                    pe.wait_ge(s_trout[b], ONE + BANK_USES[b] * s + BANK_OF[:u].count(b))
                    return tr[b]

                def rows(s, u):
                    if u == 0:
                        pe.wait_ge(s_xn, ONE + s + 1)
                    b = use(s, U_X + u)
                    for j in range(4):
                        last = nc.tensor.transpose(b[:, 128 * j:128 * (j + 1)], xn[:, 4 * u + j, :], ident[:, :])
                    last.then_inc(s_tr, 1)

                def turn_values(s, u):
                    if u == 0:
                        pe.wait_ge(s_keys, ONE + s + 1)
                    b = use(s, U_V + u)[:, :].bitcast(F16)
                    for j in range(8):
                        src = keys[:, 16 * u + 2 * j:16 * u + 2 * j + 2, :, :].rearrange("p q e i -> p (q e i)")
                        last = nc.tensor.transpose(b[:, 128 * j:128 * (j + 1)], src, ident16[:, :])
                    last.then_inc(s_tr, 1)

                def xm(s, c, h):
                    src = lambda lo: keys[:, 32 * c:32 * c + 32, 2 * lo, :] if c < 2 else coarse_q[:, lo, :, :]
                    n = HEADS * c + h
                    if n == 0:
                        pe.wait_ge(s_klo, ONE + s + 1)
                    pe.wait_ge(s_xlo, ONE + 48 * s + max(n - RING + 1, 0))
                    if n < RING:
                        pe.wait_ge(s_ylo, ONE + 32 * s)
                    for i, (w, lo) in enumerate((("Mhi", 0), ("Mhi", 1), ("Mlo", 0))):
                        last = nc.tensor.matmul(ring[n % RING][:, :], att[w][:, h * D:(h + 1) * D], src(lo),
                                                start=(i == 0), stop=(i == 2))
                    last.then_inc(s_xm, 1)

                def logits_of(s, blk):
                    c, (k, q) = blk // 32, divmod(blk, 16)
                    j = k % 2
                    if blk % 32 == 0:
                        pe.wait_ge(s_xlo, ONE + 48 * s + HEADS * (c + 1))
                    if q == 0:
                        pe.wait_ge(s_sread, ONE + 6 * s + max(k - 1, 0))
                        if k < 2:
                            pe.wait_ge(s_x, ONE + 8 * s)
                    for half in range(2):
                        o = sbk[j][:, 256 * half + BLK * q:256 * half + BLK * (q + 1)]
                        hs_ = slice(HH * half, HH * (half + 1))
                        lh = XH[c % 2][:, blk % 32, hs_, :].rearrange("p h i -> p (h i)")
                        ll = XL[c % 2][:, blk % 32, hs_, :].rearrange("p h i -> p (h i)")
                        nc.tensor.matmul(o, lh, keys[:, blk, 0, :], start=True, stop=False)
                        nc.tensor.matmul(o, lh, keys[:, blk, 2, :], start=False, stop=False)
                        last = nc.tensor.matmul(o, ll, keys[:, blk, 0, :], start=False, stop=True)
                    if q == 15:
                        last.then_inc(s_s, 1)

                def denominators(s, coarse):
                    pe.wait_ge(s_sums, ONE + 2 * s + coarse + 1)
                    q, n = (FINE, QBLK - FINE) if coarse else (0, FINE)
                    for i in range(BLK):
                        b, at = divmod(n * i, 512)
                        for m, (half, lo) in enumerate(((0, 0), (0, 1), (1, 0), (1, 1))):
                            last = nc.tensor.matmul(ring[2 * coarse + b][0:HEADS, at:at + n], sel[:, BLK * half + i, :],
                                                    sums16[:, lo, QBLK * half + q:QBLK * half + q + n],
                                                    start=(m == 0), stop=(m == 3))
                        if i % (512 // n) == 512 // n - 1:
                            last.then_inc(s_den, 1)

                def spread(s):
                    pe.wait_ge(s_d16, ONE + s + 1)
                    b = use(s, U_R)
                    for half in range(2):
                        for i in range(BLK):
                            last = nc.tensor.matmul(b[:, QBLK * half:QBLK * (half + 1)], selT[:, BLK * half + i, :],
                                                    den16[:, i, :], start=(i == 0), stop=(i == BLK - 1))
                    last.then_inc(s_tr, 1)

                def turn_weights(s, u):
                    c, half, q = weight_use(u)
                    if u % 4 == 0:
                        pe.wait_ge(s_a4, ONE + 3 * s + u // 4 + 1)
                    b = use(s, U_A + u)[:, :].bitcast(F16)
                    for j in range(8):
                        n = 2 * (q + j)
                        last = nc.tensor.transpose(b[:, 128 * j:128 * (j + 1)],
                                                   A4[:, half, n:n + 2, :, :].rearrange("p q e i -> p (q e i)"),
                                                   ident16[:, :])
                    last.then_inc(s_tr, 1)

                def apply_weights(s, ck, half):
                    n = 2 * ck + half
                    if n == 0:
                        for b in range(len(tr)):
                            pe.wait_ge(s_trout[b], ONE + BANK_USES[b] * (s + 1))
                        pe.wait_ge(s_denread, ONE + 2 * (s + 1))
                        pe.wait_ge(s_cden, ONE + s + 1)
                    pe.wait_ge(s_ylo, ONE + 32 * s + max(n - RING + 1, 0))
                    y = ring[n % RING][:, :].rearrange("p (h t) -> p h t", h=HH)
                    jobs = [(4 * ck + j, 0, BLK, 16 * j, 1) for j in range(4)]
                    for l in range(1, LEVELS + 1):
                        step = 2 ** l
                        start = 64 * ck + step - 1 if step * BLK >= 64 else 64 * ck + 32 + step - 1
                        blk, i = divmod(start // step, BLK)
                        if blk % 2 == 1:
                            cnt = (64 * (ck + 1) - start + step - 1) // step
                            jobs.append((BASE[l - 1] + blk // 2, i, cnt, start - 64 * ck, step))
                    for a, (q, i, cnt, at, step) in enumerate(jobs):
                        rhs = A4T[:, half, q // 2, :].rearrange("p (h i) -> p h i", i=BLK)[:, :, i:i + cnt]
                        last = nc.tensor.matmul(y[:, :, at:at + (cnt - 1) * step + 1:step], values[:, q // 2, q % 2, :], rhs,
                                                start=(a == 0), stop=(a == len(jobs) - 1), skip_group_check=True)
                    last.then_inc(s_y, 1)

                def project(s, t):
                    pe.wait_ge(s_ylo, ONE + 32 * s + 4 * (t + 1))
                    pe.wait_ge(s_x, ONE + 8 * s + max(t - 1, 0))
                    for h in range(HEADS):
                        for n, (y, w) in enumerate(((YH, "Nhi"), (YH, "Nlo"), (YL, "Nhi"))):
                            last = nc.tensor.matmul(sbk[t % 2][:, 0:D], y[t % 2][:, h, :], att[w][:, h * D:(h + 1) * D],
                                                    start=(h == 0 and n == 0), stop=(h == HEADS - 1 and n == 2))
                    last.then_inc(s_out, 1)

                def entry(s, ahead):
                    for c in range(3):
                        for h in range(HEADS):
                            xm(s, c, h)
                            if c == 0 and h in VALUES_AT:
                                turn_values(s, VALUES_AT.index(h))
                            if c > 0:
                                for j in range(2):
                                    logits_of(s, 32 * (c - 1) + 2 * h + j)
                    for blk in range(64, 96):
                        logits_of(s, blk)
                    denominators(s, 0)
                    denominators(s, 1)
                    spread(s)
                    for u in range(12):
                        turn_weights(s, u)
                    for ck in range(16):
                        for half in range(2):
                            apply_weights(s, ck, half)
                        if ck % 2 == 1 and ck >= 3:
                            project(s, ck // 2 - 1)
                        if ahead and ck in (4, 5):
                            rows(s + 1, ck - 4)
                    project(s, 7)

                def products(a, b, banks):
                    for h in range(HEADS):
                        last = nc.tensor.matmul(banks[h // 4][:, (h % 4) * D:(h % 4 + 1) * D],
                                                att[a][:, h * D:(h + 1) * D], att[b][:, h * D:(h + 1) * D],
                                                start=True, stop=True)
                        if h % 4 == 3:
                            last.then_inc(s_mm, 1)

                pe.wait_ge(s_const, ONE + 1)
                products("att_wq", "att_wk", mn_banks["M"])
                rows(0, 0)
                rows(0, 1)
                for b in range(2):
                    pe.wait_ge(s_trout[b], ONE + 1)
                products("att_wv", "att_wo", mn_banks["N"])
                pe.wait_ge(s_lo, 2)
                with pe.Fori(0, NB - 1) as s:
                    entry(s, True)
                entry(NB - 1, False)

            @block.vector
            def _(dve):
                def statistics(s):
                    for g in range(GROUPS):
                        dve.bn_stats(stats[:, g, :], xs(s)[:, g, :])
                    dve.drain()
                    for g in range(GROUPS):
                        last = dve.bn_aggr(mv[:, g, :], stats[:, g, :])
                    last.then_inc(s_stats, 1)

                def norm(s):
                    dve.wait_ge(s_root, ONE + s + 1)
                    dve.wait_ge(s_tr, ONE + USES * s)
                    for g in range(GROUPS):
                        last = dve.tensor_scalar(xn[:, g, :], xs(s)[:, g, :], mv[:, g, 0:1], root[:, 2, g:g + 1],
                                                 ALU.subtract, ALU.mult)
                    last.then_inc(s_xn, 1)

                def lo_keys(s, l):
                    dve.wait_ge(s_khi, ONE + (LEVELS + 1) * s + l + 1)
                    if l == 0:
                        dve.wait_ge(s_pool, ONE + s + 1)
                        fine = xT[:, 0:SEQ].rearrange("p (q i) -> p q i", i=BLK)
                        dve.tensor_tensor(keys[:, 0:FINE, 2, :], fine, keys[:, 0:FINE, 0, :], ALU.subtract)
                        return
                    n, b = NBLK[l - 1], BASE[l - 1]
                    dve.scalar_tensor_tensor(keys[:, b:b + n, 2, :], level(l, 0), 2.0 ** -l,
                                             keys[:, b:b + n, 0, :], ALU.mult, ALU.subtract)
                    c = slice(b - FINE, b - FINE + n)
                    last = dve.scalar_tensor_tensor(coarse_q[:, 1, c, :], level(l, 1), 2.0 ** -l,
                                                    coarse_q[:, 0, c, :], ALU.mult, ALU.subtract)
                    if l == LEVELS:
                        last.then_inc(s_klo, 1)

                def lo_xm(s, c, h):
                    if h == 0:
                        dve.wait_ge(s_s, ONE + 6 * s + 2 * max(c - 1, 0))
                        if c == 0:
                            dve.wait_ge(s_out, ONE + 8 * s)
                    n = HEADS * c + h
                    dve.wait_ge(s_xhi, ONE + 48 * s + n + 1)
                    dve.tensor_tensor(XL[c % 2][:, :, h, :], ring[n % RING][:, :].rearrange("p (q i) -> p q i", i=BLK),
                                      XH[c % 2][:, :, h, :], ALU.subtract).then_inc(s_xlo, 1)

                def shift(s, k):
                    j = k % 2
                    dve.wait_ge(s_s, ONE + 6 * s + k + 1)
                    dve.wait_ge(s_e, ONE + 6 * s + max(k - 1, 0))
                    t = logits[j][:, :, :, :].rearrange("p a q i -> p (a q) i")
                    src = sbk[j][:, :].rearrange("p (q i) -> p q i", i=BLK)
                    if k < 4:
                        dve.tensor_tensor(t, src, S["att_mask"][:, :].unsqueeze(1).broadcast_to([128, 32, BLK]),
                                          ALU.add).then_inc(s_sread, 1)
                        dve.drain()
                        src = t
                    pk = peaks[j][:, :, :].rearrange("p a q -> p (a q)")
                    dve.tensor_reduce(pk, src, AX.X, ALU.max)
                    dve.drain()
                    dve.tensor_tensor(t, src, pk.unsqueeze(2).broadcast_to([128, 32, BLK]),
                                      ALU.subtract).then_inc(s_sub, 1)
                    if k >= 4:
                        dve.drain().then_inc(s_sread, 1)

                def add_up(s, k):
                    dve.wait_ge(s_e, ONE + 6 * s + k + 1)
                    dve.tensor_reduce(sums[:, :, 16 * k:16 * k + 16], E[:, :, 16 * k:16 * k + 16, :], AX.X, ALU.add)

                def split_sums(s, coarse):
                    dve.drain()
                    q = slice(FINE, QBLK) if coarse else slice(0, FINE)
                    hi, lo = (sums16[:, e, :].rearrange("p (a q) -> p a q", a=2)[:, :, q] for e in range(2))
                    dve.tensor_copy(hi, sums[:, :, q])
                    dve.drain()
                    dve.tensor_tensor(lo, sums[:, :, q], hi, ALU.subtract).then_inc(s_sums, 1)

                def clear_den16(s):
                    dve.wait_ge(s_out, ONE + 8 * s)
                    dve.memset(den16[:, :, :], 0.0)

                def all_levels(s):
                    dv = den[:, :].rearrange("h (q i) -> h i q", i=BLK)
                    for k in range(2):
                        dve.wait_ge(s_den, ONE + 3 * s + k + 1)
                        b = ring[k][0:HEADS, :].rearrange("h (i q) -> h i q", q=FINE)
                        dve.tensor_scalar(dv[:, 8 * k:8 * k + 8, :], b, ATT_EPS, None, ALU.add).then_inc(s_denread, 1)
                    dve.drain()
                    dve.wait_ge(s_cden, ONE + s + 1)
                    for l in range(1, LEVELS + 1):
                        n, b = NBLK[l - 1], BASE[l - 1] - FINE
                        at = spots(den, l)
                        last = dve.tensor_tensor(at, at, cden[:, :, b:b + n].rearrange("h i m -> h m i"), ALU.add)
                        if l < LEVELS:
                            dve.drain()
                    last.then_inc(s_dall, 1)
                    for n, (src, q, up) in enumerate(den_parts()):
                        dve.wait_ge(s_dhi, ONE + (LEVELS + 1) * s + n + 1)
                        if n == 0:
                            dve.wait_ge(s_dall, ONE + s + 1)
                        last = dve.scalar_tensor_tensor(den_lo[:, :, q].rearrange("h i q -> h q i"), src, up,
                                                        den_hi[:, :, q].rearrange("h i q -> h q i"),
                                                        ALU.mult, ALU.subtract)
                    last.then_inc(s_d16, 1)

                def reciprocals(s):
                    dve.wait_ge(s_tr, turned(s, U_R))
                    dve.reciprocal(scale[:, :, :].rearrange("p a q -> p (a q)"),
                                   tr[BANK_OF[U_R]][:, 0:2 * QBLK]).then_inc(s_trout[BANK_OF[U_R]], 1)
                    dve.drain()
                    dve.memset(scale[:, :, QBLK - 1:QBLK], 0.0)
                    dve.drain()

                def scale_weights(s, c):
                    q = slice(32 * A_ORDER[c], 32 * A_ORDER[c] + 32)
                    for half in range(2):
                        e = E[:, half, q, :]
                        last = dve.scalar_tensor_tensor(e, e, A_UP * DEN_UP,
                                                        scale[:, half, q].unsqueeze(2).broadcast_to([128, 32, BLK]),
                                                        ALU.mult, ALU.mult)
                    last.then_inc(s_scaled, 1)

                def lo_weights(s, c):
                    q = slice(32 * A_ORDER[c], 32 * A_ORDER[c] + 32)
                    dve.wait_ge(s_ahi, ONE + 3 * s + c + 1)
                    dve.wait_ge(s_scaled, ONE + 3 * s + c + 1)
                    dve.tensor_tensor(A4[:, :, q, 1, :], E[:, :, q, :], A4[:, :, q, 0, :], ALU.subtract)
                    dve.drain()
                    for half in range(2):
                        last = dve.tensor_copy(A4[:, half, q, 2:4, :], A4[:, half, q, 0:2, :])
                    last.then_inc(s_a4, 1)

                def weights_out(s, u):
                    _, half, q = weight_use(u)
                    b = BANK_OF[U_A + u]
                    dve.wait_ge(s_tr, turned(s, U_A + u))
                    dve.tensor_copy(A4T[:, half, q:q + 8, :].rearrange("p q d -> p (q d)"),
                                    tr[b][:, :].bitcast(F16)).then_inc(s_trout[b], 1)

                def lo_y(s, ck, half):
                    n = 2 * ck + half
                    t = ck // 2
                    dve.wait_ge(s_yhi, ONE + 32 * s + n + 1)
                    dve.wait_ge(s_out, ONE + 8 * s + max(t - 1, 0))
                    where = (slice(None), slice(HH * half, HH * (half + 1)), slice(64 * (ck % 2), 64 * (ck % 2) + 64))
                    dve.scalar_tensor_tensor(YL[t % 2][where], ring[n % RING][:, :].rearrange("p (h t) -> p h t", h=HH),
                                             Y_UP / (X_UP * A_UP), YH[t % 2][where], ALU.mult,
                                             ALU.subtract).then_inc(s_ylo, 1)

                def values_out(s, u):
                    dve.wait_ge(s_tr, turned(s, U_V + u))
                    if u == 1:
                        dve.wait_ge(s_y, ONE + 32 * s)
                    for o in range(2):
                        r = slice(64 * o, 64 * o + 64)
                        last = dve.tensor_copy(values[r, 8 * u:8 * u + 8, o, :],
                                               tr[BANK_OF[U_V + u]][r, :].bitcast(F16)
                                               .rearrange("p (q d) -> p q d", d=D))
                    last.then_inc(s_trout[BANK_OF[U_V + u]], 1)

                def update(s, t):
                    dve.wait_ge(s_out, ONE + 8 * s + t + 1)
                    xt = xs(s)[:, t, :]
                    dve.scalar_tensor_tensor(xt, sbk[t % 2][:, 0:D], att["undo"][:, 2:3], xt, ALU.mult,
                                             ALU.add).then_inc(s_x, 1)

                def entry(s, ahead):
                    for c in range(3):
                        for h in range(HEADS):
                            lo_xm(s, c, h)
                            if c == 0 and h in VALUES_AT and VALUES_AT.index(h) % 2 == 1:
                                values_out(s, VALUES_AT.index(h))
                            if c > 0 and h == 9:
                                shift(s, 2 * c - 2)
                            if c == 2 and h == 1:
                                shift(s, 1)
                            if c == 2 and h == 6:
                                add_up(s, 0)
                            if c == 2 and h == 12:
                                add_up(s, 1)
                    shift(s, 3)
                    add_up(s, 2)
                    shift(s, 4)
                    add_up(s, 3)
                    split_sums(s, 0)
                    shift(s, 5)
                    add_up(s, 4)
                    clear_den16(s)
                    add_up(s, 5)
                    split_sums(s, 1)
                    all_levels(s)
                    reciprocals(s)
                    scale_weights(s, 0)
                    scale_weights(s, 1)
                    lo_weights(s, 0)
                    scale_weights(s, 2)
                    for c in range(3):
                        if c < 2:
                            lo_weights(s, c + 1)
                        for u in range(4 * c, 4 * c + 4, 2):
                            weights_out(s, u)
                    dve.wait_ge(s_bias, ONE + s + 1)
                    for ck in range(16):
                        for half in range(2):
                            lo_y(s, ck, half)
                        if ck % 2 == 1 and ck >= 3:
                            update(s, ck // 2 - 1)
                        if ahead:
                            if ck == 0:
                                statistics(s + 1)
                            if ck == 2:
                                norm(s + 1)
                            if 9 <= ck <= 9 + LEVELS:
                                lo_keys(s + 1, ck - 9)
                    update(s, 7)
                    dve.drain()

                def mn_peaks(i, k):
                    for j, b in enumerate(mn_banks[k]):
                        dve.wait_ge(s_mm, 4 * i + j + 1)
                        if k == "M":
                            last = dve.tensor_reduce(peak[:, 4 * j:4 * j + 4],
                                                     b[:, :].rearrange("p (h d) -> p h d", d=D),
                                                     AX.X, ALU.max, apply_absolute_value=True)
                        else:
                            last = dve.tensor_reduce(peak[:, N_AT + j:N_AT + j + 1], b[:, :], AX.X, ALU.max,
                                                     apply_absolute_value=True)
                    if k == "N":
                        dve.drain()
                        last = dve.tensor_reduce(peak[:, N_AT + 4:N_AT + 5], peak[:, N_AT:N_AT + 4], AX.X, ALU.max)
                    last.then_inc(s_peak, 1)

                def factors(i, k):
                    part = slice(16 * i, 16 * i + 16)
                    dve.wait_ge(s_allpeak, i + 1)
                    dve.tensor_scalar(allpeak[:, part], allpeak[:, part], LEAST, None, ALU.max)
                    dve.drain()
                    dve.reciprocal(up[:, part], allpeak[:, part])
                    dve.drain()
                    dve.tensor_scalar(up[:, part], up[:, part], M_UP if k == "M" else N_UP, None,
                                      ALU.mult).then_inc(s_up, 1)
                    if k == "N":
                        dve.tensor_scalar(att["undo"][:, 2:3], allpeak[:, N_AT + 4:N_AT + 5], 1.0 / (N_UP * Y_UP), None,
                                          ALU.mult)
                        return
                    for half in range(2):
                        dve.tensor_tensor(own_peaks[:, half, :], S["att_own"][:, half * HEADS:(half + 1) * HEADS],
                                          allpeak[:, 0:HEADS], ALU.mult)
                    dve.drain()
                    dve.tensor_reduce(att["undo"][:, 0:2], own_peaks[:, :, :], AX.X, ALU.add)
                    dve.drain()
                    dve.tensor_scalar(att["undo"][:, 0:2], att["undo"][:, 0:2], HD ** -0.5 / (X_UP * X_UP * M_UP), None,
                                      ALU.mult)

                def lo_mn(i, k):
                    for n, (b, cols, place, factor) in enumerate(mn_parts(k)):
                        if k == "N" or n % 4 == 0:
                            dve.wait_ge(s_hi, n + 4 if k == "M" else HEADS + n + 1)
                        last = dve.scalar_tensor_tensor(att[k + "lo"][:, place], b[:, cols], factor,
                                                        att[k + "hi"][:, place], ALU.mult, ALU.subtract)
                    last.then_inc(s_lo, 1)

                dve.memset(keys[:, QBLK - 1:QBLK, :, :], 0.0)
                dve.memset(coarse_q[:, :, QBLK - FINE - 1:QBLK - FINE, :], 0.0)
                dve.memset(peak[:, :], 0.0)
                dve.tensor_copy(ident16[:, :], ident[:, :])
                dve.drain().then_inc(s_const, 1)
                statistics(0)
                norm(0)
                for i, k in enumerate("MN"):
                    mn_peaks(i, k)
                    factors(i, k)
                    lo_mn(i, k)
                for l in range(LEVELS + 1):
                    lo_keys(0, l)
                with dve.Fori(0, NB - 1) as s:
                    entry(s, True)
                entry(NB - 1, False)
def macaron_kernel(nc, A, out, phases):
    with ExitStack() as ctx:
        def sb(name, shape, dt=F32):
            return ctx.enter_context(nc.sbuf_tensor(name, shape, dt))

        S = {"x": sb("x_all", [128, GROUPS, NB, D])}
        first, experts, others = [], [], []

        def load(name, shape, src, dt=F32, into=others):
            S[name] = sb(name, shape, dt)
            into.append((S[name], src))

        load("columns", [128, 6], A["columns"], into=first)
        load("ident", [128, 128], A["ident"], into=first)
        load("wqkv", [128, QKV], A["wqkvT"], into=first)
        load("wproj", [128, D], A["wprojT"], into=experts)
        load("wrouter", [128, EXPERTS], A["wrouterT"], into=experts)
        load("expert_ids", [128, EXPERTS], A["expert_ids"], into=experts)
        load("moe1", [128, EXPERTS * EXP_F], A["moe1"], into=experts)
        load("moe2", [128, CHUNKS * D], A["moe2"], into=experts)
        for i, n in enumerate(("lnw1", "lnb1", "lnw2", "lnb2")):
            S[n] = S["columns"][:, i:i + 1]
        S["minus_half"], S["epsilon"] = sb("minus_half", [128, GROUPS]), sb("epsilon", [128, GROUPS])
        s_first, s_experts, s_others = (ctx.enter_context(nc.semaphore(n)) for n in
                                        ("loaded_first", "loaded_experts", "loaded_others"))
        s_store = ctx.enter_context(nc.semaphore("stored"))
        s_const = ctx.enter_context(nc.semaphore("constants"))
        load_second_half(nc, ctx, A, S, load)
        load_attention(nc, ctx, A, S, load)
        S["lnw_rnn"], S["lnb_rnn"] = S["columns"][:, 4:5], S["columns"][:, 5:6]
        att_ctx = ctx.enter_context(ExitStack())
        att = attention_memory(nc, att_ctx, A, lambda dst, src: others.append((dst, src))) if "attn" in phases else None
        with nc.Block() as block:
            @block.sync
            def _(sp):
                for s in range(NB):
                    sp.dma_start(S["x"][:, :, s, :], A["x"][s].rearrange("(g p) d -> p g d", p=128)).then_inc(s_first, 16)
                for loads, signal in ((first, s_first), (experts, s_experts), (others, s_others)):
                    for dst, src in loads:
                        sp.dma_start(dst[tuple(slice(None) for _ in dst.shape)], src).then_inc(signal, 16)
                sp.wait_ge(s_first, 16 * (NB + len(first)))

            @block.vector
            def _(dve):
                if att:
                    dve.memset(att["values"][:, :, :, :], 0.0)
                dve.memset(S["minus_half"][:, :], -0.5)
                dve.memset(S["epsilon"][:, :], EPS).then_inc(s_const, 1)

        for i, ph in enumerate(phases):
            if ph != "ffn" or i > 0:
                with nc.Block() as block:
                    @block.sync
                    def _(sp):
                        sp.wait_ge(s_experts, 16 * len(experts))
                        sp.wait_ge(s_others, 16 * len(others))
            if ph == "ffn":
                causal_moe_ffn(nc, S, f"f{i}", s_experts, 16 * len(experts))
            if ph == "attn":
                hierarchical_attention(nc, S, att)
                att_ctx.close()
            if ph == "second":
                binarize(nc, S)
                second_half(nc, S, out, s_store, "r")
                return
        with nc.Block() as block:
            @block.sync
            def _(sp):
                for s in range(NB):
                    sp.dma_start(out[s].rearrange("(g p) d -> p g d", p=128), S["x"][:, :, s, :]).then_inc(s_store, 16)
                sp.wait_ge(s_store, 16 * NB)


PHASES = ("ffn", "attn", "ffn", "second")


def layouts(inputs):
    import numpy as np
    f = lambda n: np.asarray(inputs[n])
    kv = slice(0, 0)
    q = f("L0_ffn_qkv_weight")
    nq, nk = HEADS0 * HD0, KV_HEADS0 * HD0
    rep = HEADS0 // KV_HEADS0
    per_head = lambda w: np.repeat(w.reshape(KV_HEADS0, 1, HD0, D), rep, axis=1).reshape(HEADS0 * HD0, D)
    wq = np.concatenate([q[:nq], per_head(q[nq:nq + nk]), per_head(q[nq + nk:])], 0)
    cols = np.zeros((128, 6), np.float32)
    for i, n in enumerate(("L0_ffn_ln1_weight", "L0_ffn_ln1_bias", "L0_ffn_ln2_weight", "L0_ffn_ln2_bias",
                           "L1_attn_ln_w", "L1_attn_ln_b")):
        cols[:, i] = f(n)
    a = {
        "x": f("L0_attn_x"),
        "wqkvT": wq.T, "wprojT": f("L0_ffn_proj_weight").T, "wrouterT": f("L0_ffn_router_weight").T,
        "moe1": f("L0_ffn_moe_w1").transpose(1, 0, 2).reshape(D, EXPERTS * EXP_F),
        "moe2": f("L0_ffn_moe_w2").reshape(CHUNKS, 128, D).transpose(1, 0, 2).reshape(128, CHUNKS * D),
        "columns": cols,
        "ident": np.eye(128, dtype=np.float32),
        "expert_ids": np.tile(np.arange(EXPERTS, dtype=np.float32), (128, 1)),
    }
    a.update(layouts_second_half(f))
    a.update(attention_layouts(f))
    return {k: np.ascontiguousarray(v) for k, v in a.items()}


def kernel(phases=PHASES, **inputs):
    import concourse.bacc as bacc
    from concourse.bass_utils import run_bass_kernel_spmd

    arrays = layouts(inputs)
    nc = bacc.Bacc("TRN2", target_bir_lowering=False, num_devices=1)
    aps = {k: nc.dram_tensor(f"in_{k}", v.shape, mybir.dt.from_np(v.dtype), kind="ExternalInput").ap()
           for k, v in arrays.items()}
    out = nc.dram_tensor("out", (NB, SEQ, D), F32, kind="ExternalOutput").ap()
    macaron_kernel(nc, aps, out, phases)
    r = run_bass_kernel_spmd(nc, [{f"in_{k}": v for k, v in arrays.items()}], core_ids=[0])
    return r.results[0]["out"]
```
